# Optimizing a Trainium2 kernel written in Bass

```python
import numpy as np
import jax
import jax.numpy as jnp

def _softmax(x, axis=-1):
    return jax.nn.softmax(x, axis=axis)
def _gelu(x):
    return jax.nn.gelu(x, approximate=True)
def _silu(x):
    return jax.nn.silu(x)
def _sigmoid(x):
    return jax.nn.sigmoid(x)
def _layernorm(x, axis=-1, eps=1e-5):
    m = jnp.mean(x, axis=axis, keepdims=True)
    v = jnp.var(x, axis=axis, keepdims=True)
    return (x - m) / jnp.sqrt(v + eps)
def _scatter_add(tgt, idx, src, axis=0):
    return tgt.at[idx].add(src)
def _segment_sum(src, seg, n):
    return jax.ops.segment_sum(src, seg, n)

kernel_name = 'mk_metaformer_d2_conv_nhwc256_12b9ea'

def setup_inputs(seed: int = 0):
    np.random.seed(seed)
    _w = jnp.asarray
    def _rec_inputs():
        import jax
        import jax.numpy as jnp
        _gk = jax.random.key(seed)
        x = -0.0005207 + 1.001 * jax.random.normal(jax.random.fold_in(_gk, 1), (8, 32, 32, 256), jnp.float32)
        return x
    x = _rec_inputs()
    def _L0_conv_setup():
        import jax, jax.numpy as jnp
        import numpy as np
        D_MODEL = 256
        NB = 2
        D_STATE = 64
        D_CONV = 4
        D_INNER = 2 * D_MODEL
        HEADDIM = 64
        NHEADS = D_INNER // HEADDIM
        CONV_DIM = D_INNER + 2 * D_STATE
        D_IN_PROJ = 2 * D_INNER + 2 * D_STATE + NHEADS
        EPS = 1e-05

        def _mamba2_block(h, wi, cw, cb, dtb, a_log, d_skip, nw, wo):
            B, L, _ = h.shape
            zxbcdt = jnp.einsum('blc,pc->blp', h, wi)
            z = zxbcdt[..., :D_INNER]
            xBC = zxbcdt[..., D_INNER:D_INNER + CONV_DIM]
            dt = jax.nn.softplus(zxbcdt[..., -NHEADS:] + dtb)
            xBC = jax.lax.conv_general_dilated(xBC.swapaxes(1, 2), cw, window_strides=(1,), padding=[(D_CONV - 1, 0)], dimension_numbers=('NCH', 'OIH', 'NCH'), feature_group_count=CONV_DIM)
            xBC = jax.nn.silu((xBC + cb[None, :, None]).swapaxes(1, 2))
            xs = xBC[..., :D_INNER].reshape(B, L, NHEADS, HEADDIM)
            Bm = xBC[..., D_INNER:D_INNER + D_STATE]
            Cm = xBC[..., D_INNER + D_STATE:]
            A = -jnp.exp(a_log)
            dA = jnp.exp(dt * A)

            def step(s, inp):
                dA_t, dt_t, x_t, B_t, C_t = inp
                s = s * dA_t[:, :, None, None] + (dt_t[:, :, None] * x_t)[..., None] * B_t[:, None, None, :]
                y = jnp.einsum('bhps,bs->bhp', s, C_t)
                return (s, y)
            s0 = jnp.zeros((B, NHEADS, HEADDIM, D_STATE), dtype=h.dtype)
            _, ys = jax.lax.scan(step, s0, (dA.swapaxes(0, 1), dt.swapaxes(0, 1), xs.swapaxes(0, 1), Bm.swapaxes(0, 1), Cm.swapaxes(0, 1)))
            y = ys.swapaxes(0, 1) + d_skip[:, None] * xs
            y = y.reshape(B, L, D_INNER) * jax.nn.silu(z)
            y = y * jax.lax.rsqrt(jnp.mean(y * y, axis=-1, keepdims=True) + EPS) * nw
            return jnp.einsum('bld,cd->blc', y, wo)
        key = jax.random.key(seed)
        ks = jax.random.split(key, 10)
        x = jax.random.normal(ks[0], (8, 32, 32, D_MODEL), dtype=jnp.float32)
        in_proj_w = jax.random.normal(ks[1], (NB, D_IN_PROJ, D_MODEL), dtype=jnp.float32) * 0.02
        conv_w = jax.random.normal(ks[2], (NB, CONV_DIM, 1, D_CONV), dtype=jnp.float32) * 0.2
        conv_b = jax.random.normal(ks[3], (NB, CONV_DIM), dtype=jnp.float32) * 0.02
        dt_bias = jax.random.normal(ks[4], (NB, NHEADS), dtype=jnp.float32) * 0.5
        A_log = jnp.log(jax.random.uniform(ks[5], (NB, NHEADS), minval=1.0, maxval=16.0, dtype=jnp.float32))
        D = jax.random.normal(ks[6], (NB, NHEADS), dtype=jnp.float32) * 0.1 + 1.0
        norm_w = jnp.ones((NB, D_INNER), dtype=jnp.float32)
        out_proj_w = jax.random.normal(ks[7], (NB, D_MODEL, D_INNER), dtype=jnp.float32) * 0.02
        return {'x': x, 'in_proj_w': in_proj_w, 'conv_w': conv_w, 'conv_b': conv_b, 'dt_bias': dt_bias, 'A_log': A_log, 'D': D, 'norm_w': norm_w, 'out_proj_w': out_proj_w}
    _L0_conv_all = _L0_conv_setup()
    _L0_conv_in = {k: v for k, v in _L0_conv_all.items() if k in ('in_proj_w', 'conv_w', 'conv_b', 'dt_bias', 'A_log', 'D', 'norm_w', 'out_proj_w', )}
    del _L0_conv_all

    def _L0_ffn_setup():
        import math
        import jax, jax.numpy as jnp
        import numpy as np
        CAPACITY_FACTOR = 1.25
        TOP_K = 2
        LN_EPS = 1e-05

        def _layer_norm(x, gamma, beta):
            mu = jnp.mean(x, axis=-1, keepdims=True)
            var = jnp.var(x, axis=-1, keepdims=True)
            return (x - mu) * jax.lax.rsqrt(var + LN_EPS) * gamma + beta
        key = jax.random.key(seed)
        ks = jax.random.split(key, 4)
        B, S, D, F, E = (8, 4096, 256, 512, 8)
        x = jax.random.normal(ks[0], (B, S, D), dtype=jnp.float32)
        Wr = jax.random.normal(ks[1], (D, E), dtype=jnp.float32) / np.sqrt(D)
        br = jnp.zeros((E,), jnp.float32)
        W1 = jax.random.normal(ks[2], (E, D, F), dtype=jnp.float32) / np.sqrt(D)
        b1 = jnp.zeros((E, F), jnp.float32)
        W2 = jax.random.normal(ks[3], (E, F, D), dtype=jnp.float32) / np.sqrt(F)
        b2 = jnp.zeros((E, D), jnp.float32)
        gamma = jnp.ones((D,), jnp.float32)
        beta = jnp.zeros((D,), jnp.float32)
        return {'x': x, 'Wr': Wr, 'br': br, 'W1': W1, 'b1': b1, 'W2': W2, 'b2': b2, 'gamma': gamma, 'beta': beta}
    _L0_ffn_all = _L0_ffn_setup()
    _L0_ffn_in = {k: v for k, v in _L0_ffn_all.items() if k in ('Wr', 'br', 'W1', 'b1', 'W2', 'b2', 'gamma', 'beta', )}
    del _L0_ffn_all

    def _L1_conv_setup():
        import jax, jax.numpy as jnp
        import numpy as np
        B, R, C, E, H = (2, 190, 512, 256, 8)
        D = E // H
        key = jax.random.key(seed)
        ks = jax.random.split(key, 6)
        s = 0.02
        return {'x': jax.random.normal(ks[0], (B, R, C, E), dtype=jnp.float32), 'Wq': jax.random.normal(ks[1], (H, E), dtype=jnp.float32) * s, 'bq': jnp.zeros((H,), dtype=jnp.float32), 'Wk': jax.random.normal(ks[2], (H, E), dtype=jnp.float32) * s, 'bk': jnp.zeros((H,), dtype=jnp.float32), 'Wv': jax.random.normal(ks[3], (E, E), dtype=jnp.float32) * s, 'bv': jnp.zeros((E,), dtype=jnp.float32), 'Wo': jax.random.normal(ks[4], (E, E), dtype=jnp.float32) * s, 'bo': jnp.zeros((E,), dtype=jnp.float32)}
    _L1_conv_all = _L1_conv_setup()
    _L1_conv_in = {k: v for k, v in _L1_conv_all.items() if k in ('Wq', 'bq', 'Wk', 'bk', 'Wv', 'bv', 'Wo', 'bo', )}
    del _L1_conv_all

    def _L1_ffn_setup():
        import jax, jax.numpy as jnp
        import numpy as np
        B, N, D = (16, 4096, 256)
        NUM_EXPERTS, TOP_K, HEADS = (4, 2, 4)
        N_EDGES = 1048576
        LN_EPS = 1e-05

        def _layernorm(x, g, b):
            mu = x.mean(-1, keepdims=True)
            var = ((x - mu) ** 2).mean(-1, keepdims=True)
            return (x - mu) * jax.lax.rsqrt(var + LN_EPS) * g + b

        def _forward(x, edge_index, W_gat, att_src, att_dst, b_gat, ln_gamma, ln_beta, W1, b1, W2, b2):
            Bc, Nc, Dc = x.shape
            M = Bc * Nc
            x_flat = x.reshape(M, Dc)
            h = (x_flat @ W_gat).reshape(M, HEADS, NUM_EXPERTS)
            loops = jnp.arange(M, dtype=edge_index.dtype)
            src = jnp.concatenate([edge_index[0], loops])
            dst = jnp.concatenate([edge_index[1], loops])
            a_src = (h * att_src).sum(-1)
            a_dst = (h * att_dst).sum(-1)
            e = jax.nn.leaky_relu(a_src[src] + a_dst[dst], negative_slope=0.2)
            e_max = jax.ops.segment_max(e, dst, num_segments=M)
            ee = jnp.exp(e - e_max[dst])
            denom = jax.ops.segment_sum(ee, dst, num_segments=M)
            alpha = ee / (denom[dst] + 1e-16)
            msg = h[src] * alpha[:, :, None]
            agg = jax.ops.segment_sum(msg, dst, num_segments=M).reshape(M, HEADS * NUM_EXPERTS) + b_gat
            scores = _layernorm(agg, ln_gamma, ln_beta).reshape(M, HEADS, NUM_EXPERTS).mean(1)
            scores = scores.reshape(Bc, Nc, NUM_EXPERTS)
            topk_s, topk_i = jax.lax.top_k(scores, TOP_K)
            w = jax.nn.softmax(topk_s, axis=-1)
            out = jnp.zeros_like(x)
            for ei in range(NUM_EXPERTS):
                g = jnp.where(topk_i == ei, w, 0.0).sum(-1)
                hh = jax.nn.gelu(x @ W1[ei] + b1[ei], approximate=False)
                out = out + g[..., None] * (hh @ W2[ei] + b2[ei])
            return out
        key = jax.random.key(seed)
        ks = jax.random.split(key, 8)
        s = 0.05
        return {'x': jax.random.normal(ks[0], (B, N, D), jnp.float32), 'W_gat': jax.random.normal(ks[1], (D, HEADS * NUM_EXPERTS), jnp.float32) * s, 'att_src': jax.random.normal(ks[2], (HEADS, NUM_EXPERTS), jnp.float32) * s, 'att_dst': jax.random.normal(ks[3], (HEADS, NUM_EXPERTS), jnp.float32) * s, 'b_gat': jnp.zeros((HEADS * NUM_EXPERTS,), jnp.float32), 'ln_gamma': jnp.ones((HEADS * NUM_EXPERTS,), jnp.float32), 'ln_beta': jnp.zeros((HEADS * NUM_EXPERTS,), jnp.float32), 'W1': jax.random.normal(ks[4], (NUM_EXPERTS, D, 2 * D), jnp.float32) * s, 'b1': jnp.zeros((NUM_EXPERTS, 2 * D), jnp.float32), 'W2': jax.random.normal(ks[5], (NUM_EXPERTS, 2 * D, D), jnp.float32) * s, 'b2': jnp.zeros((NUM_EXPERTS, D), jnp.float32), 'edge_index': jax.random.randint(ks[6], (2, N_EDGES), 0, B * N, jnp.int32)}
    _L1_ffn_all = _L1_ffn_setup()
    _L1_ffn_in = {k: v for k, v in _L1_ffn_all.items() if k in ('W_gat', 'att_src', 'att_dst', 'b_gat', 'ln_gamma', 'ln_beta', 'W1', 'b1', 'W2', 'b2', 'edge_index', )}
    del _L1_ffn_all

    return {
        "x": x,
        "L0_conv_in_proj_w": _L0_conv_in["in_proj_w"],
        "L0_conv_conv_w": _L0_conv_in["conv_w"],
        "L0_conv_conv_b": _L0_conv_in["conv_b"],
        "L0_conv_dt_bias": _L0_conv_in["dt_bias"],
        "L0_conv_A_log": _L0_conv_in["A_log"],
        "L0_conv_D": _L0_conv_in["D"],
        "L0_conv_norm_w": _L0_conv_in["norm_w"],
        "L0_conv_out_proj_w": _L0_conv_in["out_proj_w"],
        "L0_ffn_Wr": _L0_ffn_in["Wr"],
        "L0_ffn_br": _L0_ffn_in["br"],
        "L0_ffn_W1": _L0_ffn_in["W1"],
        "L0_ffn_b1": _L0_ffn_in["b1"],
        "L0_ffn_W2": _L0_ffn_in["W2"],
        "L0_ffn_b2": _L0_ffn_in["b2"],
        "L0_ffn_gamma": _L0_ffn_in["gamma"],
        "L0_ffn_beta": _L0_ffn_in["beta"],
        "L1_conv_Wq": _L1_conv_in["Wq"],
        "L1_conv_bq": _L1_conv_in["bq"],
        "L1_conv_Wk": _L1_conv_in["Wk"],
        "L1_conv_bk": _L1_conv_in["bk"],
        "L1_conv_Wv": _L1_conv_in["Wv"],
        "L1_conv_bv": _L1_conv_in["bv"],
        "L1_conv_Wo": _L1_conv_in["Wo"],
        "L1_conv_bo": _L1_conv_in["bo"],
        "L1_ffn_W_gat": _L1_ffn_in["W_gat"],
        "L1_ffn_att_src": _L1_ffn_in["att_src"],
        "L1_ffn_att_dst": _L1_ffn_in["att_dst"],
        "L1_ffn_b_gat": _L1_ffn_in["b_gat"],
        "L1_ffn_ln_gamma": _L1_ffn_in["ln_gamma"],
        "L1_ffn_ln_beta": _L1_ffn_in["ln_beta"],
        "L1_ffn_W1": _L1_ffn_in["W1"],
        "L1_ffn_b1": _L1_ffn_in["b1"],
        "L1_ffn_W2": _L1_ffn_in["W2"],
        "L1_ffn_b2": _L1_ffn_in["b2"],
        "L1_ffn_edge_index": _L1_ffn_in["edge_index"],
    }

def reference(x, L0_conv_in_proj_w, L0_conv_conv_w, L0_conv_conv_b, L0_conv_dt_bias, L0_conv_A_log, L0_conv_D, L0_conv_norm_w, L0_conv_out_proj_w, L0_ffn_Wr, L0_ffn_br, L0_ffn_W1, L0_ffn_b1, L0_ffn_W2, L0_ffn_b2, L0_ffn_gamma, L0_ffn_beta, L1_conv_Wq, L1_conv_bq, L1_conv_Wk, L1_conv_bk, L1_conv_Wv, L1_conv_bv, L1_conv_Wo, L1_conv_bo, L1_ffn_W_gat, L1_ffn_att_src, L1_ffn_att_dst, L1_ffn_b_gat, L1_ffn_ln_gamma, L1_ffn_ln_beta, L1_ffn_W1, L1_ffn_b1, L1_ffn_W2, L1_ffn_b2, L1_ffn_edge_index):
    import jax
    import jax.numpy as jnp
    def _L0_conv_ref(x, in_proj_w, conv_w, conv_b, dt_bias, A_log, D, norm_w, out_proj_w):
        import jax, jax.numpy as jnp
        import numpy as np
        D_MODEL = 256
        NB = 2
        D_STATE = 64
        D_CONV = 4
        D_INNER = 2 * D_MODEL
        HEADDIM = 64
        NHEADS = D_INNER // HEADDIM
        CONV_DIM = D_INNER + 2 * D_STATE
        D_IN_PROJ = 2 * D_INNER + 2 * D_STATE + NHEADS
        EPS = 1e-05

        def _mamba2_block(h, wi, cw, cb, dtb, a_log, d_skip, nw, wo):
            B, L, _ = h.shape
            zxbcdt = jnp.einsum('blc,pc->blp', h, wi)
            z = zxbcdt[..., :D_INNER]
            xBC = zxbcdt[..., D_INNER:D_INNER + CONV_DIM]
            dt = jax.nn.softplus(zxbcdt[..., -NHEADS:] + dtb)
            xBC = jax.lax.conv_general_dilated(xBC.swapaxes(1, 2), cw, window_strides=(1,), padding=[(D_CONV - 1, 0)], dimension_numbers=('NCH', 'OIH', 'NCH'), feature_group_count=CONV_DIM)
            xBC = jax.nn.silu((xBC + cb[None, :, None]).swapaxes(1, 2))
            xs = xBC[..., :D_INNER].reshape(B, L, NHEADS, HEADDIM)
            Bm = xBC[..., D_INNER:D_INNER + D_STATE]
            Cm = xBC[..., D_INNER + D_STATE:]
            A = -jnp.exp(a_log)
            dA = jnp.exp(dt * A)

            def step(s, inp):
                dA_t, dt_t, x_t, B_t, C_t = inp
                s = s * dA_t[:, :, None, None] + (dt_t[:, :, None] * x_t)[..., None] * B_t[:, None, None, :]
                y = jnp.einsum('bhps,bs->bhp', s, C_t)
                return (s, y)
            s0 = jnp.zeros((B, NHEADS, HEADDIM, D_STATE), dtype=h.dtype)
            _, ys = jax.lax.scan(step, s0, (dA.swapaxes(0, 1), dt.swapaxes(0, 1), xs.swapaxes(0, 1), Bm.swapaxes(0, 1), Cm.swapaxes(0, 1)))
            y = ys.swapaxes(0, 1) + d_skip[:, None] * xs
            y = y.reshape(B, L, D_INNER) * jax.nn.silu(z)
            y = y * jax.lax.rsqrt(jnp.mean(y * y, axis=-1, keepdims=True) + EPS) * nw
            return jnp.einsum('bld,cd->blc', y, wo)
        B, H, W, C = x.shape
        h = x.reshape(B, H * W, C)
        for i in range(NB):
            h = _mamba2_block(h, in_proj_w[i], conv_w[i], conv_b[i], dt_bias[i], A_log[i], D[i], norm_w[i], out_proj_w[i])
        return h.reshape(B, H, W, C)

    def _L0_ffn_ref(x, Wr, br, W1, b1, W2, b2, gamma, beta):
        import math
        import jax, jax.numpy as jnp
        import numpy as np
        CAPACITY_FACTOR = 1.25
        TOP_K = 2
        LN_EPS = 1e-05

        def _layer_norm(x, gamma, beta):
            mu = jnp.mean(x, axis=-1, keepdims=True)
            var = jnp.var(x, axis=-1, keepdims=True)
            return (x - mu) * jax.lax.rsqrt(var + LN_EPS) * gamma + beta
        B, S, D = x.shape
        E = Wr.shape[1]
        N = B * S
        K = TOP_K
        logits = jnp.mean(x, axis=1) @ Wr + br
        routing_weights = jax.nn.softmax(logits, axis=-1)
        capacity = float(math.ceil(N * CAPACITY_FACTOR / E))
        expected_loads = routing_weights.sum(axis=0) * (N / B)
        scale = jnp.where(expected_loads > capacity, capacity / expected_loads, 1.0)
        routing_weights = jax.nn.softmax(routing_weights * scale, axis=-1)
        rw_tok = jnp.broadcast_to(routing_weights[:, None, :], (B, S, E)).reshape(N, E)
        top_w, top_i = jax.lax.top_k(rw_tok, K)
        top_w = jax.nn.softmax(top_w, axis=-1)
        xf = x.reshape(N, D)
        h = jax.nn.gelu(jnp.einsum('nd,edf->enf', xf, W1) + b1[:, None, :], approximate=False)
        y = jnp.einsum('enf,efd->end', h, W2) + b2[:, None, :]
        w_dense = jnp.zeros((N, E), x.dtype).at[jnp.arange(N)[:, None], top_i].add(top_w)
        out = jnp.einsum('ne,end->nd', w_dense, y).reshape(B, S, D)
        out = _layer_norm(out + x, gamma, beta)
        return out

    def _L1_conv_ref(x, Wq, bq, Wk, bk, Wv, bv, Wo, bo):
        import jax, jax.numpy as jnp
        import numpy as np
        B, R, C, E, H = (2, 190, 512, 256, 8)
        D = E // H
        b, r, c, e = x.shape
        h = Wq.shape[0]
        d = e // h
        q = jnp.einsum('brce,he->brhc', x, Wq) + bq[:, None]
        k = jnp.einsum('brce,he->brhc', x, Wk) + bk[:, None]
        v = (jnp.einsum('brce,fe->brcf', x, Wv) + bv).reshape(b, r, c, h, d)
        v = jnp.transpose(v, (0, 1, 3, 2, 4))
        q = jax.nn.elu(q) + 1.0
        k = jax.nn.elu(k) + 1.0
        q = q / jnp.mean(q, axis=-1, keepdims=True)
        k = k / jnp.sum(k, axis=-1, keepdims=True)
        ktv = jnp.einsum('brhc,brhcd->brhd', k, v)
        V = jnp.einsum('brhc,brhd->brchd', q, ktv).reshape(b, r, c, e)
        out = jnp.einsum('brce,fe->brcf', V, Wo) + bo
        return out

    def _L1_ffn_ref(x, W_gat, att_src, att_dst, b_gat, ln_gamma, ln_beta, W1, b1, W2, b2, edge_index):
        import jax, jax.numpy as jnp
        import numpy as np
        B, N, D = (16, 4096, 256)
        NUM_EXPERTS, TOP_K, HEADS = (4, 2, 4)
        N_EDGES = 1048576
        LN_EPS = 1e-05

        def _layernorm(x, g, b):
            mu = x.mean(-1, keepdims=True)
            var = ((x - mu) ** 2).mean(-1, keepdims=True)
            return (x - mu) * jax.lax.rsqrt(var + LN_EPS) * g + b

        def _forward(x, edge_index, W_gat, att_src, att_dst, b_gat, ln_gamma, ln_beta, W1, b1, W2, b2):
            Bc, Nc, Dc = x.shape
            M = Bc * Nc
            x_flat = x.reshape(M, Dc)
            h = (x_flat @ W_gat).reshape(M, HEADS, NUM_EXPERTS)
            loops = jnp.arange(M, dtype=edge_index.dtype)
            src = jnp.concatenate([edge_index[0], loops])
            dst = jnp.concatenate([edge_index[1], loops])
            a_src = (h * att_src).sum(-1)
            a_dst = (h * att_dst).sum(-1)
            e = jax.nn.leaky_relu(a_src[src] + a_dst[dst], negative_slope=0.2)
            e_max = jax.ops.segment_max(e, dst, num_segments=M)
            ee = jnp.exp(e - e_max[dst])
            denom = jax.ops.segment_sum(ee, dst, num_segments=M)
            alpha = ee / (denom[dst] + 1e-16)
            msg = h[src] * alpha[:, :, None]
            agg = jax.ops.segment_sum(msg, dst, num_segments=M).reshape(M, HEADS * NUM_EXPERTS) + b_gat
            scores = _layernorm(agg, ln_gamma, ln_beta).reshape(M, HEADS, NUM_EXPERTS).mean(1)
            scores = scores.reshape(Bc, Nc, NUM_EXPERTS)
            topk_s, topk_i = jax.lax.top_k(scores, TOP_K)
            w = jax.nn.softmax(topk_s, axis=-1)
            out = jnp.zeros_like(x)
            for ei in range(NUM_EXPERTS):
                g = jnp.where(topk_i == ei, w, 0.0).sum(-1)
                hh = jax.nn.gelu(x @ W1[ei] + b1[ei], approximate=False)
                out = out + g[..., None] * (hh @ W2[ei] + b2[ei])
            return out
        return _forward(x, edge_index, W_gat, att_src, att_dst, b_gat, ln_gamma, ln_beta, W1, b1, W2, b2)

    def _gn(v, G=32, eps=1e-5):
        B_, H_, W_, C_ = v.shape
        g = v.reshape(B_, H_, W_, G, C_ // G)
        m = jnp.mean(g, axis=(1, 2, 4), keepdims=True)
        s = jnp.var(g, axis=(1, 2, 4), keepdims=True)
        return ((g - m) / jnp.sqrt(s + eps)).reshape(v.shape)

    def _ln_c(v, eps=1e-6):
        m = jnp.mean(v, axis=-1, keepdims=True)
        s = jnp.var(v, axis=-1, keepdims=True)
        return (v - m) / jnp.sqrt(s + eps)

    def _ln_t(v, eps=1e-5):
        m = jnp.mean(v, axis=-1, keepdims=True)
        s = jnp.var(v, axis=-1, keepdims=True)
        return (v - m) / jnp.sqrt(s + eps)

    def _to_tokens(v):
        B_, H_, W_, C_ = v.shape
        return v.reshape(B_, H_ * W_, C_)
    def _from_tokens(t, like):
        return t.reshape(like.shape)

    x = x + _L0_conv_ref(_ln_c(x), L0_conv_in_proj_w, L0_conv_conv_w, L0_conv_conv_b, L0_conv_dt_bias, L0_conv_A_log, L0_conv_D, L0_conv_norm_w, L0_conv_out_proj_w)
    t = _to_tokens(x)
    t = t + _L0_ffn_ref(_ln_t(t), L0_ffn_Wr, L0_ffn_br, L0_ffn_W1, L0_ffn_b1, L0_ffn_W2, L0_ffn_b2, L0_ffn_gamma, L0_ffn_beta)
    x = _from_tokens(t, x)
    x = x + _L1_conv_ref(_ln_c(x), L1_conv_Wq, L1_conv_bq, L1_conv_Wk, L1_conv_bk, L1_conv_Wv, L1_conv_bv, L1_conv_Wo, L1_conv_bo)
    t = _to_tokens(x)
    t = t + _L1_ffn_ref(_ln_t(t), L1_ffn_W_gat, L1_ffn_att_src, L1_ffn_att_dst, L1_ffn_b_gat, L1_ffn_ln_gamma, L1_ffn_ln_beta, L1_ffn_W1, L1_ffn_b1, L1_ffn_W2, L1_ffn_b2, L1_ffn_edge_index)
    x = _from_tokens(t, x)
    return x


_drawn_inputs = setup_inputs


def setup_inputs(seed=0):
    import zlib

    import numpy as np

    out = dict(_drawn_inputs(seed))
    spreads = {'L0_conv_norm_w': (1.0, 0.2),
     'L0_ffn_br': (0.0, 0.1),
     'L0_ffn_b1': (0.0, 0.1),
     'L0_ffn_b2': (0.0, 0.1),
     'L0_ffn_gamma': (1.0, 0.2),
     'L0_ffn_beta': (0.0, 0.1),
     'L1_conv_bq': (0.0, 0.8),
     'L1_conv_bk': (0.0, 2.0),
     'L1_conv_bv': (0.0, 0.402),
     'L1_conv_bo': (0.0, 0.1),
     'L1_ffn_b_gat': (0.0, 0.1),
     'L1_ffn_ln_gamma': (1.0, 0.2),
     'L1_ffn_ln_beta': (0.0, 0.34),
     'L1_ffn_b1': (0.0, 0.288),
     'L1_ffn_b2': (0.0, 0.1)}
    factors = {'L0_conv_dt_bias': 8.0,
     'L0_conv_A_log': 64.0,
     'L0_ffn_Wr': 8.0,
     'L1_conv_Wq': 5.33,
     'L1_conv_Wk': 7.31,
     'L1_conv_Wv': 4.02,
     'L1_ffn_att_src': 3.766,
     'L1_ffn_att_dst': 5.788}
    for name, (base, spread) in spreads.items():
        noise = np.random.default_rng([zlib.crc32(name.encode()), seed]).standard_normal(out[name].shape)
        drawn = base * np.exp(spread * noise) if base else spread * noise
        out[name] = jnp.asarray(drawn.astype(out[name].dtype))
    for name, factor in factors.items():
        out[name] = (out[name] * factor).astype(out[name].dtype)
    return out
```

```python
from contextlib import ExitStack

import concourse.bass as bass
from concourse import mybir

F32 = mybir.dt.float32
I32 = mybir.dt.int32
U32 = mybir.dt.uint32
ALU = mybir.AluOpType
ACT = mybir.ActivationFunctionType
AX = mybir.AxisListType

P = 128
C = 256
KC = C // P
BATCH = 8
SEQ = 1024
TPB = SEQ // P
TILES = BATCH * TPB

LAYERS = 2
DIN = 512
XM = DIN // P
HEADS = 8
HD = DIN // HEADS
NST = 64
TAPS = 4
OX, OB, OC, ODT = DIN, 2 * DIN, 2 * DIN + NST, 2 * DIN + 2 * NST
DPROJ = ODT + HEADS
STREAMS = 2
LN_C_EPS = 1e-6
LN_T_EPS = 1e-5
RMS_EPS = 1e-5
LN_MAX = 88.7


def row_on_all(vector, n):
    return vector.rearrange("(a n) -> a n", a=1).broadcast_to([P, n])


def counters(nc, ctx):
    taken = []
    ctx.callback(nc.all_engine_barrier)
    ctx.callback(lambda: nc.clear_and_free_semaphores(taken))

    def counter(name):
        taken.append(nc.alloc_semaphore(name))
        return taken[-1]

    return counter


def mamba_layers(nc, d, X, ident):
    with ExitStack() as ctx:
        def sb(name, shape, dt=F32):
            return ctx.enter_context(nc.sbuf_tensor(name, shape, dt))

        def per_stream(name, shape):
            return [sb(f"{name}{s}", shape) for s in range(STREAMS)]

        counter = counters(nc, ctx)

        def sems(name):
            return [counter(f"{name}{s}") for s in range(STREAMS)]

        w_in = [sb(f"w_in{l}", [P, KC, DPROJ]) for l in range(LAYERS)]
        w_out = [sb(f"w_out{l}", [P, XM, C]) for l in range(LAYERS)]
        norm_w = sb("norm_w", [P, LAYERS, XM])
        cw = sb("cw", [P, LAYERS, XM, TAPS])
        cb = sb("cb", [P, LAYERS, XM])
        cw_bc = sb("cw_bc", [NST, LAYERS, 2, TAPS])
        cb_bc = sb("cb_bc", [NST, LAYERS, 2])
        dt_bias = sb("dt_bias", [HEADS, LAYERS])
        a_log = sb("a_log", [HEADS, LAYERS])
        a_neg = sb("a_neg", [HEADS, LAYERS])
        a_exp = sb("a_exp", [HEADS, LAYERS])
        d_half = sb("d_half", [P, LAYERS, HEADS])
        d_row = sb("d_row", [P, LAYERS, HEADS])
        head_row = sb("head_row", [HEADS, HEADS, P])
        last_row = sb("last_row", [P, NST])
        diag = sb("diag", [P, 4, P])
        zero_row = sb("zero_row", [HEADS, P])
        minus_half = sb("minus_half", [P, 1])

        stats = per_stream("stats", [P, 6])
        mv = per_stream("mv", [P, 2])
        var = per_stream("var", [P, 1])
        rstd = per_stream("rstd", [P, 1])
        r0 = per_stream("r0", [P, 1])
        h_in = per_stream("h_in", [P, C])
        hT = per_stream("hT", [P, KC, P])
        x_raw = [per_stream(f"x_raw{l}_", [P, XM, TAPS - 1 + P]) for l in range(LAYERS)]
        bc_raw = [per_stream(f"bc_raw{l}_", [NST, 2, TAPS - 1 + P]) for l in range(LAYERS)]
        state = [per_stream(f"state{l}_", [NST, DIN]) for l in range(LAYERS)]
        x_conv = per_stream("x_conv", [P, XM, P])
        x_tanh = per_stream("x_tanh", [P, XM, P])
        bc_conv = per_stream("bc_conv", [NST, 2, P])
        bc_tap = [[sb(f"bc_tap{s}_{k}", [NST, 2, P]) for k in range(TAPS - 1)] for s in range(STREAMS)]
        bc_tanh = per_stream("bc_tanh", [NST, 2, P])
        dt_raw = per_stream("dt_raw", [HEADS, P])
        cb_prod = per_stream("cb_prod", [P, P])
        dt_abs = per_stream("dt_abs", [HEADS, P])
        dt_exp = per_stream("dt_exp", [HEADS, P])
        dt_pos = per_stream("dt_pos", [HEADS, P])
        dt_log = per_stream("dt_log", [HEADS, P])
        dt = per_stream("dt", [HEADS, P])
        dt_a = per_stream("dt_a", [HEADS, P])
        decay = per_stream("decay", [HEADS, P])
        decay0 = per_stream("decay0", [HEADS, P])
        decay_prod = per_stream("decay_prod", [HEADS, P])
        b_tok = per_stream("b_tok", [P, NST])
        dt_tok = per_stream("dt_tok", [P, HEADS])
        prod_tok = per_stream("prod_tok", [P, HEADS])
        x_tok = per_stream("x_tok", [P, HEADS, HD])
        x_skip = per_stream("x_skip", [P, HEADS, HD])
        x_dt = per_stream("x_dt", [P, HEADS, HD])
        x_end = per_stream("x_end", [P, HEADS, HD])
        span = per_stream("span", [P, HEADS, P])
        mix = per_stream("mix", [P, HEADS, P])
        state_dec = per_stream("state_dec", [NST, HEADS, HD])
        y = per_stream("y", [P, HEADS, HD])
        z_tanh = per_stream("z_tanh", [P, DIN])
        z_gate = per_stream("z_gate", [P, DIN])
        y_sq = z_tanh
        ssq = per_stream("ssq", [P, 1])
        r = per_stream("r", [P, 1])
        yT = x_tanh

        bankA = [ctx.enter_context(nc.psum_tensor(f"bankA{s}", [P, 512], F32)) for s in range(STREAMS)]
        bankB = [ctx.enter_context(nc.psum_tensor(f"bankB{s}", [P, 512], F32)) for s in range(STREAMS)]
        bankC = [ctx.enter_context(nc.psum_tensor(f"bankC{s}", [P, 512], F32)) for s in range(STREAMS)]
        bankD = [ctx.enter_context(nc.psum_tensor(f"bankD{s}", [P, 512], F32)) for s in range(STREAMS)]

        loaded = counter("weights_loaded")
        prepared = counter("weights_prepared")
        x_first = counter("x_first")
        x_rest = counter("x_rest")
        a_bounded = counter("a_bounded")
        a_done = counter("a_done")
        passed_dve, passed_pe, passed_pool = (counter(f"passed_{e}") for e in ("dve", "pe", "pool"))
        carry_reset = sems("carry_reset")
        names = """stats_ready mv_ready var_ready rstd_ready h_ready h_turned hT_ready bc_proj dt_raw_ready x_proj bc_copied
            x_copied conv1 conv2 conv3 conv_done bconv0 bconv1 bconv2 bconv_done x_tanh_done bc_tanh_done x_act
            bc_act dt_abs_done dt_exp_done dt_pos_done dt_log_done dt_ready dt_a_ready decay_ready decay0_ready prod_ready
            spread_lo spread_hi x_turned small_turned tok_copied x_tok_copied skip_ready xdt_ready span_ready
            mix_ready xend_ready z_proj intra_done inter_done total_done state_dec_ready state_in state_out
            z_tanh_done z_gate_ready y1_ready y2_ready y3_ready y_ready ssq_ready r0_ready r_ready y_turned yT_ready out_done
            layer_done""".split()
        S = {n: sems(n) for n in names}

        block = ctx.enter_context(nc.Block())

        def turns(t):
            return [LAYERS * t + 1 + l for l in range(LAYERS)]

        @block.sync
        def _(sp):
            xv = d["x"].rearrange("(i p) c -> p i c", p=P)

            def load_image(b, sem):
                sp.dma_start(X[:, b * TPB:(b + 1) * TPB, :], xv[:, b * TPB:(b + 1) * TPB, :]).then_inc(sem, 16)

            for s in range(STREAMS):
                load_image(s * (BATCH // STREAMS), x_first)
            for l in range(LAYERS):
                sp.dma_start(w_in[l][:, :, :], d["in_projT"][l].rearrange("(k p) n -> p k n", p=P)).then_inc(loaded, 16)
                sp.dma_start(w_out[l][:, :, :], d["out_projT"][l].rearrange("(m p) n -> p m n", p=P)).then_inc(loaded, 16)
                sp.dma_start(d_row[:, l, :], row_on_all(d["D"][l], HEADS)).then_inc(loaded, 16)
            for tile_, name in ((norm_w, "norm_w"), (cw, "conv_w"), (cb, "conv_b"), (cw_bc, "conv_w_bc"), (cb_bc, "conv_b_bc"),
                                (dt_bias, "dt_bias"), (a_log, "A_log"), (ident, "ident")):
                sp.dma_start(tile_[:], d[name]).then_inc(loaded, 16)
            for g in range(4):
                sp.dma_start(diag[:, g, :], d["ident"]).then_inc(loaded, 16)
            sp.dma_start(head_row[:, :, :], d["head_row"].rearrange("k (h p) -> k h p", h=HEADS)).then_inc(loaded, 16)
            sp.dma_start(last_row[:, :], d["last_row"]).then_inc(loaded, 16)
            for b in range(1, BATCH // STREAMS):
                for s in range(STREAMS):
                    load_image(b + s * (BATCH // STREAMS), x_rest)

        N_LOADED = 16 * (3 * LAYERS + 14)

        @block.tensor
        def _(pe):
            pe.wait_ge(prepared, 1)
            with pe.Fori(0, TILES // STREAMS) as t:
                for l, n in enumerate(turns(t)):
                    for s in range(STREAMS):
                        pe.wait_ge(S["h_ready"][s], n)
                        for k in range(KC):
                            mm = nc.tensor.transpose(bankA[s][:, k * P:(k + 1) * P], h_in[s][:, k * P:(k + 1) * P], ident[:, :])
                        mm.then_inc(S["h_turned"][s], 1)
                    for s in range(STREAMS):
                        pe.wait_ge(S["hT_ready"][s], n)
                        for out, o, m in ((bankC[s][0:HEADS, 256:384], ODT, HEADS), (bankC[s][0:NST, 0:P], OB, NST),
                                          (bankC[s][0:NST, P:2 * P], OC, NST)):
                            for k in range(KC):
                                mm = nc.tensor.matmul(out, w_in[l][:, k, o:o + m], hT[s][:, k, :], start=(k == 0), stop=(k == KC - 1))
                        mm.then_inc(S["bc_proj"][s], 1)
                        for m in range(XM):
                            for k in range(KC):
                                mm = nc.tensor.matmul(bankB[s][:, m * P:(m + 1) * P], w_in[l][:, k, OX + m * P:OX + (m + 1) * P],
                                                      hT[s][:, k, :], start=(k == 0), stop=(k == KC - 1))
                        mm.then_inc(S["x_proj"][s], 1)
                    for s in range(STREAMS):
                        pe.wait_ge(S["decay0_ready"][s], n)
                        for h in range(HEADS):
                            bank = (bankA if h < 4 else bankD)[s]
                            mm = nc.tensor.matmul(bank[:, h % 4 * P:(h % 4 + 1) * P], head_row[:, h, :], decay0[s][:, :], start=True, stop=True)
                            if h == 3:
                                mm.then_inc(S["spread_lo"][s], 1)
                        mm.then_inc(S["spread_hi"][s], 1)
                    for s in range(STREAMS):
                        pe.wait_ge(S["bc_act"][s], n)
                        nc.tensor.matmul(bankC[s][:, P:2 * P], bc_conv[s][:, 0, :], bc_conv[s][:, 1, :], start=True, stop=True)
                        nc.tensor.transpose(bankC[s][:, 0:NST], bc_conv[s][:, 0, :], ident[0:NST, 0:NST])
                        nc.tensor.transpose(bankC[s][:, 400:408], dt[s][:, :], ident[0:HEADS, 0:HEADS])
                        pe.wait_ge(S["prod_ready"][s], n)
                        pe.sem_inc(passed_pe, 1)
                        nc.tensor.transpose(bankC[s][:, 408:416], decay_prod[s][:, :], ident[0:HEADS, 0:HEADS]).then_inc(S["small_turned"][s], 1)
                        pe.wait_ge(S["x_copied"][s], n)
                        pe.wait_ge(S["x_act"][s], n)
                        for m in range(XM):
                            mm = nc.tensor.transpose(bankB[s][:, m * P:(m + 1) * P], x_conv[s][:, m, :], ident[:, :])
                        mm.then_inc(S["x_turned"][s], 1)
                    for s in range(STREAMS):
                        pe.wait_ge(S["tok_copied"][s], n)
                        nc.tensor.matmul(bankC[s][0:NST, 420:428], last_row[:, :], prod_tok[s][:, :], start=True, stop=True)\
                            .then_inc(S["total_done"][s], 1)
                        pe.wait_ge(S["span_ready"][s], n)
                        for k in range(KC):
                            mm = nc.tensor.matmul(bankD[s][:, :], hT[s][:, k, :], w_in[l][:, k, 0:DIN], start=(k == 0), stop=(k == KC - 1))
                        mm.then_inc(S["z_proj"][s], 1)
                        pe.wait_ge(S["x_tok_copied"][s], n)
                        nc.tensor.matmul(bankB[s][:, :], bc_conv[s][:, 1, :], state[l][s][:, :], start=True, stop=True)\
                            .then_inc(S["inter_done"][s], 1)
                        pe.wait_ge(S["mix_ready"][s], n)
                        pe.wait_ge(S["xdt_ready"][s], n)
                        for h in range(HEADS):
                            mm = nc.tensor.matmul(bankA[s][:, h * HD:(h + 1) * HD], mix[s][:, h, :], x_dt[s][:, h, :], start=True, stop=True)
                        mm.then_inc(S["intra_done"][s], 1)
                        pe.wait_ge(S["xend_ready"][s], n)
                        pe.wait_ge(S["state_dec_ready"][s], n)
                        nc.tensor.matmul(bankC[s][0:NST, :], b_tok[s][:, :], x_end[s][:, :, :].rearrange("p h e -> p (h e)"),
                                         start=True, stop=True).then_inc(S["state_in"][s], 1)
                    for s in range(STREAMS):
                        pe.wait_ge(S["y_ready"][s], n)
                        for m in range(XM):
                            mm = nc.tensor.transpose(bankB[s][:, m * P:(m + 1) * P],
                                                     y[s][:, 2 * m:2 * m + 2, :].rearrange("p h e -> p (h e)"), ident[:, :])
                        mm.then_inc(S["y_turned"][s], 1)
                    for s in range(STREAMS):
                        pe.wait_ge(S["yT_ready"][s], n)
                        for m in range(XM):
                            mm = nc.tensor.matmul(bankA[s][:, 0:C], yT[s][:, m, :], w_out[l][:, m, :], start=(m == 0), stop=(m == XM - 1))
                        mm.then_inc(S["out_done"][s], 1)

        @block.scalar
        def _(act):
            act.wait_ge(a_bounded, 1)
            nc.scalar.activation(a_exp[:, :], a_log[:, :], ACT.Exp).then_inc(a_done, 1)
            act.wait_ge(prepared, 1)
            with act.Fori(0, TILES // STREAMS) as t:
                for l, n in enumerate(turns(t)):
                    for s in range(STREAMS):
                        act.wait_ge(S["h_turned"][s], n)
                        nc.scalar.copy(hT[s][:, :, :].rearrange("p k t -> p (k t)"), bankA[s][:, 0:C]).then_inc(S["hT_ready"][s], 1)
                    for s in range(STREAMS):
                        act.wait_ge(S["bc_proj"][s], n)
                        nc.scalar.activation(dt_raw[s][:, :], bankC[s][0:HEADS, 256:384], ACT.Identity, bias=dt_bias[:, l:l + 1])\
                            .then_inc(S["dt_raw_ready"][s], 1)
                        nc.scalar.copy(bc_raw[l][s][:, :, TAPS - 1:], bankC[s][0:NST, 0:2 * P].rearrange("p (m t) -> p m t", m=2))\
                            .then_inc(S["bc_copied"][s], 1)
                        act.wait_ge(S["dt_raw_ready"][s], n)
                        nc.scalar.activation(dt_abs[s][:, :], dt_raw[s][:, :], ACT.Abs).then_inc(S["dt_abs_done"][s], 1)
                        act.wait_ge(S["dt_abs_done"][s], n)
                        nc.scalar.activation(dt_exp[s][:, :], dt_abs[s][:, :], ACT.Exp, scale=-1.0).then_inc(S["dt_exp_done"][s], 1)
                        act.wait_ge(S["x_proj"][s], n)
                        nc.scalar.copy(x_raw[l][s][:, :, TAPS - 1:], bankB[s][:, :].rearrange("p (m t) -> p m t", m=XM))\
                            .then_inc(S["x_copied"][s], 1)
                    for s in range(STREAMS):
                        act.wait_ge(S["dt_exp_done"][s], n)
                        nc.scalar.activation(dt_log[s][:, :], dt_exp[s][:, :], ACT.Ln, bias=1.0).then_inc(S["dt_log_done"][s], 1)
                    for s in range(STREAMS):
                        act.wait_ge(S["dt_a_ready"][s], n)
                        nc.scalar.activation(decay[s][:, :], dt_a[s][:, :], ACT.Exp).then_inc(S["decay_ready"][s], 1)
                    for s in range(STREAMS):
                        act.wait_ge(S["bconv_done"][s], n)
                        nc.scalar.activation(bc_tanh[s][:, :, :], bc_conv[s][:, :, :], ACT.Tanh, scale=0.5).then_inc(S["bc_tanh_done"][s], 1)
                        act.wait_ge(S["conv_done"][s], n)
                        nc.scalar.activation(x_tanh[s][:, :, :], x_conv[s][:, :, :], ACT.Tanh, scale=0.5).then_inc(S["x_tanh_done"][s], 1)
                    for s in range(STREAMS):
                        act.wait_ge(S["small_turned"][s], n)
                        nc.scalar.copy(cb_prod[s][:, :], bankC[s][:, P:2 * P])
                        nc.scalar.copy(b_tok[s][:, :], bankC[s][:, 0:NST])
                        nc.scalar.copy(prod_tok[s][:, :], bankC[s][:, 408:416])
                        nc.scalar.mul(dt_tok[s][:, :], bankC[s][:, 400:408], 0.125).then_inc(S["tok_copied"][s], 1)
                        act.wait_ge(S["x_turned"][s], n)
                        nc.scalar.copy(x_tok[s][:, :, :].rearrange("p h e -> p (h e)"), bankB[s][:, :]).then_inc(S["x_tok_copied"][s], 1)
                    for s in range(STREAMS):
                        act.wait_ge(S["z_proj"][s], n)
                        nc.scalar.activation(z_tanh[s][:, :], bankD[s][:, :], ACT.Tanh, scale=0.5).then_inc(S["z_tanh_done"][s], 1)
                    for s in range(STREAMS):
                        act.wait_ge(S["y_ready"][s], n)
                        nc.scalar.activation(y_sq[s][:, :], y[s][:, :, :].rearrange("p h e -> p (h e)"), ACT.Square, accum_out=ssq[s][:, :])\
                            .then_inc(S["ssq_ready"][s], 1)
                        act.wait_ge(S["y_turned"][s], n)
                        nc.scalar.copy(yT[s][:, :, :].rearrange("p m t -> p (m t)"), bankB[s][:, :]).then_inc(S["yT_ready"][s], 1)
                    if l + 1 < LAYERS:
                        for s in range(STREAMS):
                            act.wait_ge(S["out_done"][s], n)
                            act.wait_ge(S["r_ready"][s], n)
                            nc.scalar.mul(h_in[s][:, :], bankA[s][:, 0:C], r[s][:, 0:1]).then_inc(S["h_ready"][s], 1)

        @block.gpsimd
        def _(pool):
            pool.wait_ge(prepared, 1)
            with pool.Fori(0, BATCH // STREAMS) as b:
                for s in range(STREAMS):
                    pool.wait_ge(S["layer_done"][s], b * (TPB * LAYERS) + 1)
                    pool.sem_inc(passed_pool, 1)
                    for l in range(LAYERS):
                        nc.gpsimd.memset(bc_raw[l][s][:, :, 0:TAPS - 1], 0.0).then_inc(carry_reset[s], 1)
                with pool.Fori(0, TPB) as c:
                    for l, n in enumerate(turns(b * TPB + c)):
                        if l == 0:
                            for s in range(STREAMS):
                                pool.wait_ge(S["var_ready"][s], b * TPB + c + 1)
                                nc.gpsimd.tensor_tensor(rstd[s][:, :], var[s][:, :], minus_half[:, :], ALU.pow).then_inc(S["rstd_ready"][s], 1)
                        for s in range(STREAMS):
                            pool.wait_ge(carry_reset[s], LAYERS * b + LAYERS)
                            pool.wait_ge(S["bc_copied"][s], n)
                            pool.sem_inc(passed_pool, 1)
                            for k in range(TAPS):
                                for m in range(2):
                                    tap = bc_raw[l][s][:, m, k:k + P]
                                    out = bc_conv[s] if k == 0 else bc_tap[s][k - 1]
                                    ins = nc.gpsimd.tensor_scalar(out[:, m, :], tap, cw_bc[:, l, m, k:k + 1],
                                                                  cb_bc[:, l, m:m + 1] if k == 0 else 0.0, ALU.mult, ALU.add)
                            ins.then_inc(S["bconv0"][s], 1)
                            for k, (before, after) in enumerate((("bconv0", "bconv1"), ("bconv1", "bconv2"), ("bconv2", "bconv_done"))):
                                pool.wait_ge(S[before][s], n)
                                nc.gpsimd.tensor_tensor(bc_conv[s][:, :, :], bc_conv[s][:, :, :], bc_tap[s][k][:, :, :], ALU.add)\
                                    .then_inc(S[after][s], 1)
                            nc.gpsimd.tensor_copy(bc_raw[l][s][:, :, 0:TAPS - 1], bc_raw[l][s][:, :, P:])
                        for s in range(STREAMS):
                            pool.wait_ge(S["x_tok_copied"][s], n)
                            nc.gpsimd.tensor_tensor(x_skip[s][:, :, :], x_tok[s][:, :, :],
                                                    d_half[:, l, :].unsqueeze(2).broadcast_to([P, HEADS, HD]), ALU.mult)\
                                .then_inc(S["skip_ready"][s], 1)
                        for s in range(STREAMS):
                            pool.wait_ge(S["r0_ready"][s], n)
                            nc.gpsimd.tensor_tensor(r[s][:, :], r0[s][:, :], minus_half[:, :], ALU.pow).then_inc(S["r_ready"][s], 1)

        @block.vector
        def _(dve):
            dve.wait_ge(loaded, N_LOADED)
            nc.vector.tensor_scalar(a_log[:, :], a_log[:, :], LN_MAX, None, ALU.min).then_inc(a_bounded, 1)
            for l in range(LAYERS):
                for m in range(XM):
                    nc.vector.tensor_scalar(w_out[l][:, m, :], w_out[l][:, m, :], norm_w[:, l, m:m + 1], None, ALU.mult)
            nc.vector.tensor_scalar(d_half[:, :, :], d_row[:, :, :], 0.5, None, ALU.mult)
            nc.vector.memset(zero_row[:, :], 0.0)
            nc.vector.memset(minus_half[:, :], -0.5)
            for s in range(STREAMS):
                nc.vector.memset(decay0[s][:, 0:1], 0.0)
            dve.wait_ge(a_done, 1)
            nc.vector.tensor_scalar(a_neg[:, :], a_exp[:, :], -1.0, None, ALU.mult).then_inc(prepared, 1)
            for s in range(STREAMS):
                nc.vector.memset(ssq[s][:, :], 0.0).then_inc(S["layer_done"][s], 1)

            dve.wait_ge(x_first, 16 * STREAMS)
            with dve.Fori(0, BATCH // STREAMS) as b:
                for s in range(STREAMS):
                    for l in range(LAYERS):
                        nc.vector.memset(state[l][s][:, :], 0.0)
                        nc.vector.memset(x_raw[l][s][:, :, 0:TAPS - 1], 0.0)
                with dve.Fori(0, TPB) as c:
                    t = b * TPB + c
                    for l, n in enumerate(turns(t)):
                        if l == 0:
                            for s in range(STREAMS):
                                dve.wait_ge(S["layer_done"][s], n)
                                xt = X[:, bass.ds(t + s * (TILES // STREAMS), 1), :].rearrange("p a c -> p (a c)")
                                nc.vector.bn_stats(stats[s][:, :], xt).then_inc(S["stats_ready"][s], 1)
                                dve.wait_ge(S["stats_ready"][s], t + 1)
                                dve.sem_inc(passed_dve, 1)
                                nc.vector.bn_aggr(mv[s][:, :], stats[s][:, :]).then_inc(S["mv_ready"][s], 1)
                                dve.wait_ge(S["mv_ready"][s], t + 1)
                                nc.vector.tensor_scalar(var[s][:, :], mv[s][:, 1:2], LN_C_EPS, None, ALU.add)\
                                    .then_inc(S["var_ready"][s], 1)
                                dve.wait_ge(S["rstd_ready"][s], t + 1)
                                nc.vector.tensor_scalar(h_in[s][:, :], xt, mv[s][:, 0:1], rstd[s][:, 0:1], ALU.subtract, ALU.mult)\
                                    .then_inc(S["h_ready"][s], 1)
                        for s in range(STREAMS):
                            dve.wait_ge(S["dt_raw_ready"][s], n)
                            nc.vector.tensor_scalar(dt_pos[s][:, :], dt_raw[s][:, :], 0.0, None, ALU.max)\
                                .then_inc(S["dt_pos_done"][s], 1)
                        for s in range(STREAMS):
                            dve.wait_ge(S["dt_log_done"][s], n)
                            dve.wait_ge(S["dt_pos_done"][s], n)
                            nc.vector.tensor_tensor(dt[s][:, :], dt_pos[s][:, :], dt_log[s][:, :], ALU.add).then_inc(S["dt_ready"][s], 1)
                        for s in range(STREAMS):
                            dve.wait_ge(S["dt_ready"][s], n)
                            nc.vector.tensor_scalar(dt_a[s][:, :], dt[s][:, :], a_neg[:, l:l + 1], -110.0, ALU.mult, ALU.max)\
                                .then_inc(S["dt_a_ready"][s], 1)
                        for s in range(STREAMS):
                            dve.wait_ge(S["x_copied"][s], n)
                            for m in range(XM):
                                ins = nc.vector.tensor_scalar(x_conv[s][:, m, :], x_raw[l][s][:, m, 0:P], cw[:, l, m, 0:1], cb[:, l, m:m + 1],
                                                              ALU.mult, ALU.add)
                            ins.then_inc(S["conv1"][s], 1)
                        for s in range(STREAMS):
                            dve.wait_ge(S["decay_ready"][s], n)
                            nc.vector.tensor_copy(decay0[s][:, 1:P], decay[s][:, 1:P]).then_inc(S["decay0_ready"][s], 1)
                            nc.vector.tensor_tensor_scan(decay_prod[s][:, :], decay[s][:, :], zero_row[:, :], 1.0, ALU.mult, ALU.add)\
                                .then_inc(S["prod_ready"][s], 1)
                        for k, (before, after) in enumerate((("conv1", "conv2"), ("conv2", "conv3"), ("conv3", "conv_done")), 1):
                            for s in range(STREAMS):
                                dve.wait_ge(S[before][s], n)
                                for m in range(XM):
                                    ins = nc.vector.scalar_tensor_tensor(out=x_conv[s][:, m, :], in0=x_raw[l][s][:, m, k:k + P],
                                                                         scalar=cw[:, l, m, k:k + 1], in1=x_conv[s][:, m, :],
                                                                         op0=ALU.mult, op1=ALU.add)
                                ins.then_inc(S[after][s], 1)
                        for s in range(STREAMS):
                            dve.wait_ge(S["bc_tanh_done"][s], n)
                            nc.vector.scalar_tensor_tensor(out=bc_conv[s][:, :, :], in0=bc_tanh[s][:, :, :], scalar=1.0, in1=bc_conv[s][:, :, :],
                                                           op0=ALU.add, op1=ALU.mult).then_inc(S["bc_act"][s], 1)
                            nc.vector.tensor_copy(x_raw[l][s][:, :, 0:TAPS - 1], x_raw[l][s][:, :, P:])
                            flat = span[s][:, :, :].rearrange("p h t -> p (h t)")
                            d4 = diag[:, :, :].rearrange("p g t -> p (g t)")
                            dve.wait_ge(S["spread_lo"][s], n)
                            nc.vector.tensor_tensor_scan(flat[:, 0:512], bankA[s][:, :], d4, 0.0, ALU.mult, ALU.add)
                            dve.wait_ge(S["spread_hi"][s], n)
                            nc.vector.tensor_tensor_scan(flat[:, 512:1024], bankD[s][:, :], d4, 0.0, ALU.mult, ALU.add)\
                                .then_inc(S["span_ready"][s], 1)
                            dve.wait_ge(S["x_tanh_done"][s], n)
                            nc.vector.scalar_tensor_tensor(out=x_conv[s][:, :, :], in0=x_tanh[s][:, :, :], scalar=1.0, in1=x_conv[s][:, :, :],
                                                           op0=ALU.add, op1=ALU.mult).then_inc(S["x_act"][s], 1)
                        for s in range(STREAMS):
                            dve.wait_ge(S["tok_copied"][s], n)
                            dve.wait_ge(S["span_ready"][s], n)
                            nc.vector.tensor_tensor(mix[s][:, :, :], span[s][:, :, :],
                                                    cb_prod[s][:, :].unsqueeze(1).broadcast_to([P, HEADS, P]), ALU.mult)\
                                .then_inc(S["mix_ready"][s], 1)
                            dve.wait_ge(S["x_tok_copied"][s], n)
                            nc.vector.tensor_tensor(x_dt[s][:, :, :], x_tok[s][:, :, :],
                                                    dt_tok[s][:, :].unsqueeze(2).broadcast_to([P, HEADS, HD]), ALU.mult)\
                                .then_inc(S["xdt_ready"][s], 1)
                            dve.wait_ge(S["total_done"][s], n)
                            nc.vector.tensor_tensor(state_dec[s][:, :, :], state[l][s][:, :].rearrange("p (h e) -> p h e", h=HEADS),
                                                    bankC[s][0:NST, 420:428].unsqueeze(2).broadcast_to([NST, HEADS, HD]), ALU.mult)\
                                .then_inc(S["state_dec_ready"][s], 1)
                            dve.wait_ge(S["xdt_ready"][s], n)
                            nc.vector.tensor_tensor(x_end[s][:, :, :], x_dt[s][:, :, :],
                                                    span[s][:, :, P - 1:P].broadcast_to([P, HEADS, HD]), ALU.mult)\
                                .then_inc(S["xend_ready"][s], 1)
                        for s in range(STREAMS):
                            dve.wait_ge(S["inter_done"][s], n)
                            nc.vector.tensor_tensor(y[s][:, :, :], bankB[s][:, :].rearrange("p (h e) -> p h e", h=HEADS),
                                                    prod_tok[s][:, :].unsqueeze(2).broadcast_to([P, HEADS, HD]), ALU.mult)\
                                .then_inc(S["y1_ready"][s], 1)
                            dve.wait_ge(S["z_tanh_done"][s], n)
                            nc.vector.scalar_tensor_tensor(out=z_gate[s][:, :], in0=z_tanh[s][:, :], scalar=1.0, in1=bankD[s][:, :],
                                                           op0=ALU.add, op1=ALU.mult).then_inc(S["z_gate_ready"][s], 1)
                            yf = y[s][:, :, :].rearrange("p h e -> p (h e)")
                            dve.wait_ge(S["y1_ready"][s], n)
                            dve.wait_ge(S["intra_done"][s], n)
                            nc.vector.tensor_tensor(yf, bankA[s][:, :], yf, ALU.add).then_inc(S["y2_ready"][s], 1)
                            dve.wait_ge(S["state_in"][s], n)
                            dve.wait_ge(S["state_dec_ready"][s], n)
                            nc.vector.tensor_tensor(state[l][s][:, :], bankC[s][0:NST, :],
                                                    state_dec[s][:, :, :].rearrange("p h e -> p (h e)"), ALU.add).then_inc(S["state_out"][s], 1)
                            dve.wait_ge(S["y2_ready"][s], n)
                            dve.wait_ge(S["skip_ready"][s], n)
                            nc.vector.tensor_tensor(yf, yf, x_skip[s][:, :, :].rearrange("p h e -> p (h e)"), ALU.add).then_inc(S["y3_ready"][s], 1)
                            dve.wait_ge(S["y3_ready"][s], n)
                            dve.wait_ge(S["z_gate_ready"][s], n)
                            nc.vector.tensor_tensor(yf, yf, z_gate[s][:, :], ALU.mult).then_inc(S["y_ready"][s], 1)
                        for s in range(STREAMS):
                            dve.wait_ge(S["ssq_ready"][s], n)
                            nc.vector.tensor_scalar(r0[s][:, :], ssq[s][:, :], 1.0 / DIN, 4 * RMS_EPS, ALU.mult, ALU.add)\
                                .then_inc(S["r0_ready"][s], 1)
                            if l + 1 < LAYERS:
                                dve.wait_ge(S["state_out"][s], n)
                                dve.wait_ge(S["out_done"][s], n)
                                nc.vector.memset(stats[s][:, :], 0.0).then_inc(S["layer_done"][s], 1)
                            else:
                                dve.wait_ge(S["out_done"][s], n)
                                dve.wait_ge(S["r_ready"][s], n)
                                dve.wait_ge(S["state_out"][s], n)
                                xt = X[:, bass.ds(t + s * (TILES // STREAMS), 1), :].rearrange("p a c -> p (a c)")
                                nc.vector.scalar_tensor_tensor(out=xt, in0=bankA[s][:, 0:C], scalar=r[s][:, 0:1], in1=xt,
                                                               op0=ALU.mult, op1=ALU.add).then_inc(S["layer_done"][s], 1)
                dve.wait_ge(x_rest, 16 * (BATCH - STREAMS))


F = 512
FM = F // P
EXP0 = 8
TOPK = 2
CAPACITY = 1280.0
HALF = SEQ // 2
TPH = HALF // P


def norm_statistics(nc, X, mean, rstd, eps, name):
    with ExitStack() as ctx:
        counter = counters(nc, ctx)
        stats = ctx.enter_context(nc.sbuf_tensor(f"{name}_stats", [P, 2, TPB, 6], F32))
        mv = ctx.enter_context(nc.sbuf_tensor(f"{name}_mv", [P, 2, TPB, 2], F32))
        var = ctx.enter_context(nc.sbuf_tensor(f"{name}_var", [P, TILES], F32))
        minus_half = ctx.enter_context(nc.sbuf_tensor(f"{name}_mh", [P, TILES], F32))
        sem = lambda n: counter(f"{name}_{n}")
        stats_ready, mv_ready, var_ready, passed = (sem(n) for n in ("stats_ready", "mv_ready", "var_ready", "passed"))
        block = ctx.enter_context(nc.Block())

        @block.vector
        def _(dve):
            nc.vector.memset(minus_half[:, :], -0.5)
            with dve.Fori(0, BATCH // 2) as b:
                for u in range(2):
                    for i in range(TPB):
                        xt = X[:, bass.ds(b * (2 * TPB) + (u * TPB + i), 1), :].rearrange("p a c -> p (a c)")
                        ins = nc.vector.bn_stats(stats[:, u, i, :], xt)
                    ins.then_inc(stats_ready, 1)
                    dve.wait_ge(stats_ready, 2 * b + u + 1)
                    dve.sem_inc(passed, 1)
                    for i in range(TPB):
                        ins = nc.vector.bn_aggr(mv[:, u, i, :], stats[:, u, i, :])
                    ins.then_inc(mv_ready, 1)
                    dve.wait_ge(mv_ready, 2 * b + u + 1)
                    at = bass.ds(b * (2 * TPB) + u * TPB, TPB)
                    nc.vector.tensor_copy(mean[:, at], mv[:, u, :, 0])
                    nc.vector.tensor_scalar(var[:, at], mv[:, u, :, 1], eps, None, ALU.add).then_inc(var_ready, 1)

        @block.gpsimd
        def _(pool):
            pool.wait_ge(var_ready, BATCH)
            nc.gpsimd.tensor_tensor(rstd[:, :], var[:, :], minus_half[:, :], ALU.pow)


def route_images(nc, d, X, ident, mean, rstd, picked, weight):
    with ExitStack() as ctx:
        counter = counters(nc, ctx)
        sb = lambda n, s, dt=F32: ctx.enter_context(nc.sbuf_tensor(n, s, dt))
        sem = lambda n: counter(n)
        tok = [sb(f"rt_tok{u}", [P, C]) for u in range(4)]
        image_row = sb("rt_image_row", [P, BATCH, BATCH])
        w_r = sb("rt_w", [P, KC, EXP0])
        b_r = sb("rt_b", [BATCH, EXP0])
        ones = sb("rt_ones", [BATCH, BATCH])
        token_mean = sb("rt_mean", [BATCH, C])
        token_meanT = sb("rt_meanT", [P, KC, BATCH])
        logits = sb("rt_logits", [BATCH, EXP0])
        top = sb("rt_top", [BATCH, 1])
        low = sb("rt_low", [BATCH, EXP0])
        total = sb("rt_total", [BATCH, 1])
        inv = sb("rt_inv", [BATCH, 1])
        rw = sb("rt_rw", [BATCH, EXP0])
        load_ = sb("rt_load", [BATCH, EXP0])
        best = sb("rt_best", [BATCH, EXP0])
        best_at = sb("rt_best_at", [BATCH, EXP0], U32)
        pair = sb("rt_pair", [BATCH, TOPK])
        psum_mean = ctx.enter_context(nc.psum_tensor("rt_pm", [P, 512], F32))
        psum_small = ctx.enter_context(nc.psum_tensor("rt_ps", [P, 512], F32))
        at_dram = nc.dram_tensor("rt_at_dram", (BATCH * TOPK,), U32, kind="Internal").ap()
        w_dram = nc.dram_tensor("rt_w_dram", (BATCH * TOPK,), F32, kind="Internal").ap()
        loaded, tok_ready, mean_done, mean_copied, turned, turned_copied, logits_done = (
            sem(n) for n in ("rt_loaded", "rt_tok_ready", "rt_mean_done", "rt_mean_copied", "rt_turned", "rt_turned_copied", "rt_logits_done"))
        step, exp_done, load_done, routed, stored, spread, tok_free = (
            sem(n) for n in ("rt_step", "rt_exp_done", "rt_load_done", "rt_routed", "rt_stored", "rt_spread", "rt_tok_free"))
        block = ctx.enter_context(nc.Block())

        @block.sync
        def _(sp):
            sp.dma_start(image_row[:, :, :], d["image_row"].rearrange("p (b j) -> p b j", b=BATCH)).then_inc(loaded, 16)
            sp.dma_start(w_r[:, :, :], d["Wr"].rearrange("(k p) e -> p k e", p=P)).then_inc(loaded, 16)
            sp.dma_start(b_r[:, :], d["br"].rearrange("(a n) -> a n", a=1).broadcast_to([BATCH, EXP0])).then_inc(loaded, 16)
            sp.wait_ge(routed, 1)
            sp.dma_start(at_dram.rearrange("(b k) -> b k", k=TOPK), best_at[:, 0:TOPK]).then_inc(stored, 16)
            sp.dma_start(w_dram.rearrange("(b k) -> b k", k=TOPK), pair[:, :]).then_inc(stored, 16)
            sp.wait_ge(stored, 32)
            sp.dma_start(picked[:, :], at_dram.rearrange("(a n) -> a n", a=1)).then_inc(spread, 16)
            sp.dma_start(weight[:, :], row_on_all(w_dram, BATCH * TOPK)).then_inc(spread, 16)
            sp.wait_ge(spread, 32)

        @block.tensor
        def _(pe):
            pe.wait_ge(loaded, 48)
            for i in range(TILES):
                pe.wait_ge(tok_ready, i + 1)
                nc.tensor.matmul(psum_mean[0:BATCH, 0:C], image_row[:, i // TPB, :], tok[i % 4][:, :], start=(i == 0), stop=(i == TILES - 1))\
                    .then_inc(tok_free, 1)
            pe.wait_ge(mean_copied, 1)
            for k in range(KC):
                mm = nc.tensor.transpose(psum_small[:, k * BATCH:(k + 1) * BATCH], token_mean[:, k * P:(k + 1) * P], ident[0:BATCH, 0:BATCH])
            mm.then_inc(turned, 1)
            pe.wait_ge(turned_copied, 1)
            for k in range(KC):
                mm = nc.tensor.matmul(psum_small[0:BATCH, 32:32 + EXP0], token_meanT[:, k, :], w_r[:, k, :], start=(k == 0), stop=(k == KC - 1))
            mm.then_inc(logits_done, 1)
            pe.wait_ge(exp_done, 2)
            nc.tensor.matmul(psum_small[0:BATCH, 64:64 + EXP0], ones[:, :], rw[:, :], start=True, stop=True).then_inc(load_done, 1)

        @block.scalar
        def _(act):
            act.wait_ge(step, 3)
            nc.scalar.activation(rw[:, :], low[:, :], ACT.Exp, accum_out=total[:, :]).then_inc(exp_done, 1)
            act.wait_ge(step, 10)
            nc.scalar.activation(rw[:, :], low[:, :], ACT.Exp, accum_out=total[:, :]).then_inc(exp_done, 1)
            act.wait_ge(step, 14)
            nc.scalar.activation(pair[:, 1:2], low[:, 0:1], ACT.Exp).then_inc(exp_done, 1)

        @block.vector
        def _(dve):
            count = [0]

            def then(ins):
                count[0] += 1
                ins.then_inc(step, 1)
                dve.wait_ge(step, count[0])

            nc.vector.memset(ones[:, :], 1.0)
            for i in range(TILES):
                if i >= 4:
                    dve.wait_ge(tok_free, i - 3)
                nc.vector.tensor_scalar(tok[i % 4][:, :], X[:, i, :], mean[:, i:i + 1], rstd[:, i:i + 1], ALU.subtract, ALU.mult)\
                    .then_inc(tok_ready, 1)
            dve.wait_ge(tok_free, TILES)
            nc.vector.tensor_copy(token_mean[:, :], psum_mean[0:BATCH, 0:C]).then_inc(mean_copied, 1)
            dve.wait_ge(turned, 1)
            nc.vector.tensor_copy(token_meanT[:, :, :].rearrange("p k b -> p (k b)"), psum_small[:, 0:KC * BATCH]).then_inc(turned_copied, 1)
            dve.wait_ge(logits_done, 1)
            then(nc.vector.tensor_tensor(logits[:, :], psum_small[0:BATCH, 32:32 + EXP0], b_r[:, :], ALU.add))
            then(nc.vector.tensor_reduce(top[:, :], logits[:, :], AX.X, ALU.max))
            then(nc.vector.tensor_scalar(low[:, :], logits[:, :], top[:, 0:1], None, ALU.subtract))
            dve.wait_ge(exp_done, 1)
            then(nc.vector.reciprocal(inv[:, :], total[:, :]))
            nc.vector.tensor_scalar(rw[:, :], rw[:, :], inv[:, 0:1], None, ALU.mult).then_inc(exp_done, 1)
            dve.wait_ge(load_done, 1)
            then(nc.vector.tensor_scalar(load_[:, :], psum_small[0:BATCH, 64:64 + EXP0], float(SEQ), CAPACITY, ALU.mult, ALU.max))
            then(nc.vector.reciprocal(load_[:, :], load_[:, :]))
            then(nc.vector.scalar_tensor_tensor(out=logits[:, :], in0=load_[:, :], scalar=CAPACITY, in1=rw[:, :], op0=ALU.mult, op1=ALU.mult))
            then(nc.vector.tensor_reduce(top[:, :], logits[:, :], AX.X, ALU.max))
            then(nc.vector.tensor_scalar(low[:, :], logits[:, :], top[:, 0:1], None, ALU.subtract))
            nc.vector.engine_nop().then_inc(step, 1)
            dve.wait_ge(exp_done, 3)
            count[0] += 1
            then(nc.vector.reciprocal(inv[:, :], total[:, :]))
            then(nc.vector.tensor_scalar(rw[:, :], rw[:, :], inv[:, 0:1], None, ALU.mult))
            then(nc.vector.max(best[:, :], rw[:, :]))
            nc.vector.max_index(best_at[:, :], best[:, :], rw[:, :])
            then(nc.vector.tensor_tensor(low[:, 0:1], best[:, 1:2], best[:, 0:1], ALU.subtract))
            dve.wait_ge(exp_done, 4)
            then(nc.vector.tensor_scalar(total[:, :], pair[:, 1:2], 1.0, None, ALU.add))
            then(nc.vector.reciprocal(pair[:, 0:1], total[:, :]))
            nc.vector.tensor_scalar(pair[:, 1:2], pair[:, 1:2], pair[:, 0:1], None, ALU.mult).then_inc(routed, 1)


def experts_by_image(nc, d, X, ident, mean, rstd, picked, weight):
    with ExitStack() as ctx:
        counter = counters(nc, ctx)
        sb = lambda n, s, dt=F32: ctx.enter_context(nc.sbuf_tensor(n, s, dt))
        sem = lambda n: counter(n)
        w1 = [sb(f"m0_w1_{e}", [P, KC, F]) for e in range(TOPK)]
        w2 = [sb(f"m0_w2_{e}", [P, FM, C]) for e in range(TOPK)]
        b1 = [sb(f"m0_b1_{e}", [P, FM]) for e in range(TOPK)]
        b2 = [sb(f"m0_b2_{e}", [P, C]) for e in range(TOPK)]
        tok = sb("m0_tok", [P, TPB, C])
        tokT = sb("m0_tokT", [P, KC, SEQ])
        hid = [[sb(f"m0_hid{hf}_{e}", [P, FM, HALF]) for e in range(TOPK)] for hf in range(2)]
        bias = sb("m0_bias", [P, C])
        z = sb("m0_z", [P, TPH, C])
        stats = sb("m0_stats", [P, TPH, 6])
        mv = sb("m0_mv", [P, TPH, 2])
        var = sb("m0_var", [P, TPH])
        rs = sb("m0_rs", [P, TPH])
        minus_half = sb("m0_mh", [P, TPH])
        gamma = sb("m0_gamma", [P, C])
        beta = sb("m0_beta", [P, C])
        bank_t = [ctx.enter_context(nc.psum_tensor(f"m0_bt{i}", [P, 512], F32)) for i in range(2)]
        bank_h = [ctx.enter_context(nc.psum_tensor(f"m0_bh{i}", [P, 512], F32)) for i in range(2)]
        bank_y = [ctx.enter_context(nc.psum_tensor(f"m0_by{i}", [P, C], F32)) for i in range(4)]
        names = """affine_loaded w_loaded w_free tok_ready tok_free turned turned_copied h_done h_free y_done y_free w2_scaled bias1 bias2
            z_ready stats_ready mv_ready var_ready rs_ready zn_ready zg_ready zb_ready x_ready hid_free""".split()
        S = {n: sem("m0_" + n) for n in names}
        passed = {e: sem(f"m0_passed_{e}") for e in ("dve", "pool")}
        block = ctx.enter_context(nc.Block())

        @block.sync
        def _(sp):
            sp.dma_start(gamma[:, :], row_on_all(d["gamma0"], C)).then_inc(S["affine_loaded"], 16)
            sp.dma_start(beta[:, :], row_on_all(d["beta0"], C)).then_inc(S["affine_loaded"], 16)
            with sp.Fori(0, BATCH) as b:
                sp.wait_ge(S["w_free"], b + 1)
                for e in range(TOPK):
                    at = sp.value_load(picked[0:1, bass.ds(TOPK * b + e, 1)], min_val=0, max_val=EXP0 - 1)
                    sp.dma_start(w1[e][:, :, :], d["W1_0"][bass.ds(at, 1)].rearrange("a (k p) f -> p (a k) f", p=P)).then_inc(S["w_loaded"], 16)
                    sp.dma_start(w2[e][:, :, :], d["W2_0"][bass.ds(at, 1)].rearrange("a (m p) c -> p (a m) c", p=P)).then_inc(S["w_loaded"], 16)
                    sp.dma_start(b1[e][:, :], d["b1_0"][bass.ds(at, 1)].rearrange("a p m -> p (a m)")).then_inc(S["w_loaded"], 16)
                    sp.dma_start(b2[e][:, :], d["b2_0"][bass.ds(at, 1)].broadcast_to([P, C])).then_inc(S["w_loaded"], 16)

        @block.tensor
        def _(pe):
            with pe.Fori(0, BATCH) as b:
                pe.wait_ge(S["tok_ready"], b + 1)
                for q in range(4):
                    pe.wait_ge(S["turned_copied"], 4 * b + q + 1)
                    for i in range(2):
                        for k in range(KC):
                            mm = nc.tensor.transpose(bank_t[q % 2][:, (KC * i + k) * P:(KC * i + k + 1) * P], tok[:, 2 * q + i, k * P:(k + 1) * P], ident[:, :])
                    mm.then_inc(S["turned"], 1)
                pe.wait_ge(S["w_loaded"], 16 * 4 * TOPK * b + 16 * 4 * TOPK)
                pe.wait_ge(S["turned_copied"], 4 * b + 4 + 2)
                g = 0
                for hf in range(2):
                    for e in range(TOPK):
                        for m in range(FM):
                            pe.wait_ge(S["h_free"], 16 * b + g + 1)
                            for k in range(KC):
                                mm = nc.tensor.matmul(bank_h[g % 2][:, :], w1[e][:, k, m * P:(m + 1) * P], tokT[:, k, hf * HALF:(hf + 1) * HALF],
                                                      start=(k == 0), stop=(k == KC - 1))
                            mm.then_inc(S["h_done"], 1)
                            g += 1
                pe.wait_ge(S["w2_scaled"], b + 1)
                for hf in range(2):
                    pe.wait_ge(S["h_free"], 16 * b + 8 * (hf + 1) + 2)
                    for i in range(TPH):
                        j = hf * TPH + i
                        pe.wait_ge(S["y_free"], 8 * b + j + 1)
                        for e in range(TOPK):
                            for m in range(FM):
                                mm = nc.tensor.matmul(bank_y[j % 4][:, :], hid[hf][e][:, m, i * P:(i + 1) * P], w2[e][:, m, :],
                                                      start=(e == 0 and m == 0), stop=(e == TOPK - 1 and m == FM - 1))
                        mm.then_inc(S["y_done"], 1)

        @block.scalar
        def _(act):
            with act.Fori(0, BATCH) as b:
                for q in range(4):
                    act.wait_ge(S["turned"], 4 * b + q + 1)
                    nc.scalar.copy(tokT[:, :, 2 * q * P:(2 * q + 2) * P].rearrange("p k (i t) -> p i k t", i=2),
                                   bank_t[q % 2][:, :].rearrange("p (i k t) -> p i k t", i=2, k=KC)).then_inc(S["turned_copied"], 1)
                act.wait_ge(S["y_done"], 8 * b + 1)
                g = 0
                for hf in range(2):
                    for e in range(TOPK):
                        for m in range(FM):
                            act.wait_ge(S["h_done"], 16 * b + g + 1)
                            nc.scalar.activation(hid[hf][e][:, m, :], bank_h[g % 2][:, :], ACT.Gelu, bias=b1[e][:, m:m + 1]).then_inc(S["h_free"], 1)
                            g += 1

        @block.gpsimd
        def _(pool):
            with pool.Fori(0, BATCH) as b:
                for hf in range(2):
                    pool.wait_ge(S["var_ready"], 2 * b + hf + 1)
                    nc.gpsimd.tensor_tensor(rs[:, :], var[:, :], minus_half[:, :], ALU.pow).then_inc(S["rs_ready"], 1)

        @block.vector
        def _(dve):
            nc.vector.memset(minus_half[:, :], -0.5)
            for n, k in (("turned_copied", 2), ("h_free", 2), ("y_free", 4), ("y_done", 1), ("w_free", 1)):
                for _ in range(k):
                    dve.sem_inc(S[n], 1)
            dve.wait_ge(S["affine_loaded"], 32)
            with dve.Fori(0, BATCH) as b:
                for i in range(TPB):
                    t = b * TPB + i
                    ins = nc.vector.tensor_scalar(tok[:, i, :], X[:, bass.ds(t, 1), :].rearrange("p a c -> p (a c)"), mean[:, bass.ds(t, 1)],
                                                  rstd[:, bass.ds(t, 1)], ALU.subtract, ALU.mult)
                ins.then_inc(S["tok_ready"], 1)
                dve.wait_ge(S["w_loaded"], 16 * 4 * TOPK * b + 16 * 4 * TOPK)
                for e in range(TOPK):
                    we = weight[:, bass.ds(TOPK * b + e, 1)]
                    ins = nc.vector.tensor_scalar(w2[e][:, :, :].rearrange("p m c -> p (m c)"), w2[e][:, :, :].rearrange("p m c -> p (m c)"),
                                                  we, None, ALU.mult)
                ins.then_inc(S["w2_scaled"], 1)
                nc.vector.tensor_scalar(bias[:, :], b2[0][:, :], weight[:, bass.ds(TOPK * b, 1)], None, ALU.mult).then_inc(S["bias1"], 1)
                dve.wait_ge(S["bias1"], b + 1)
                nc.vector.scalar_tensor_tensor(out=bias[:, :], in0=b2[1][:, :], scalar=weight[:, bass.ds(TOPK * b + 1, 1)], in1=bias[:, :],
                                               op0=ALU.mult, op1=ALU.add).then_inc(S["bias2"], 1)
                dve.wait_ge(S["bias2"], b + 1)
                dve.wait_ge(S["turned"], 4 * b + 4)
                nc.vector.tensor_tensor(tok[:, :, :], tok[:, :, :], bias[:, :].unsqueeze(1).broadcast_to([P, TPB, C]), ALU.add)\
                    .then_inc(S["tok_free"], 1)
                dve.wait_ge(S["tok_free"], b + 1)
                for hf in range(2):
                    n = 2 * b + hf + 1
                    for i in range(TPH):
                        j = hf * TPH + i
                        dve.wait_ge(S["y_done"], 8 * b + j + 2)
                        nc.vector.tensor_tensor(z[:, i, :], bank_y[j % 4][:, :], tok[:, j, :], ALU.add).then_inc(S["y_free"], 1)
                    if hf == 1:
                        dve.sem_inc(S["w_free"], 1)
                    dve.wait_ge(S["y_free"], 8 * b + 4 * hf + 4 + 4)
                    dve.sem_inc(passed["dve"], 1)
                    for i in range(TPH):
                        ins = nc.vector.bn_stats(stats[:, i, :], z[:, i, :])
                    ins.then_inc(S["stats_ready"], 1)
                    dve.wait_ge(S["stats_ready"], n)
                    dve.sem_inc(passed["dve"], 1)
                    for i in range(TPH):
                        ins = nc.vector.bn_aggr(mv[:, i, :], stats[:, i, :])
                    ins.then_inc(S["mv_ready"], 1)
                    dve.wait_ge(S["mv_ready"], n)
                    nc.vector.tensor_scalar(var[:, :], mv[:, :, 1], LN_T_EPS, None, ALU.add).then_inc(S["var_ready"], 1)
                    dve.wait_ge(S["rs_ready"], n)
                    for i in range(TPH):
                        ins = nc.vector.tensor_scalar(z[:, i, :], z[:, i, :], mv[:, i, 0:1], rs[:, i:i + 1], ALU.subtract, ALU.mult)
                    ins.then_inc(S["zn_ready"], 1)
                    dve.wait_ge(S["zn_ready"], n)
                    nc.vector.tensor_tensor(z[:, :, :], z[:, :, :], gamma[:, :].unsqueeze(1).broadcast_to([P, TPH, C]), ALU.mult)\
                        .then_inc(S["zg_ready"], 1)
                    dve.wait_ge(S["zg_ready"], n)
                    nc.vector.tensor_tensor(z[:, :, :], z[:, :, :], beta[:, :].unsqueeze(1).broadcast_to([P, TPH, C]), ALU.add)\
                        .then_inc(S["zb_ready"], 1)
                    dve.wait_ge(S["zb_ready"], n)
                    xt = X[:, bass.ds(b * TPB + hf * TPH, TPH), :]
                    nc.vector.tensor_tensor(xt, xt, z[:, :, :], ALU.add).then_inc(S["x_ready"], 1)
                    dve.wait_ge(S["x_ready"], n)


ROW = 32
RPT = P // ROW
AH = 8
GT = 4
GROUPS = TILES // GT
RH = RPT * AH


def row_attention(nc, d, X, ident, mean, rstd):
    with ExitStack() as ctx:
        counter = counters(nc, ctx)
        def sb(name, shape, dt=F32):
            return ctx.enter_context(nc.sbuf_tensor("at_" + name, shape, dt))

        def per_stream(name, shape):
            return [sb(f"{name}{s}", shape) for s in range(STREAMS)]

        def sems(name):
            return [counter(f"at_{name}{s}") for s in range(STREAMS)]

        w_qk = sb("w_qk", [P, KC, 2 * RH])
        b_qk = sb("b_qk", [2 * RH, 1])
        scale = sb("scale", [2 * RH, 1])
        row_mask = sb("row_mask", [2 * RH, P])
        head_mask = sb("head_mask", [P, KC, GT * RH])
        w_v = sb("w_v", [P, KC, C])
        b_v = sb("b_v", [P, KC])
        w_o = sb("w_o", [P, KC, C])
        b_o = sb("b_o", [P, C])
        tok = per_stream("tok", [P, GT, C])
        tokT = per_stream("tokT", [P, KC, GT * P])
        neg = per_stream("neg", [2 * RH, GT * P])
        neg_exp = per_stream("neg_exp", [2 * RH, GT * P])
        pos = per_stream("pos", [2 * RH, GT * P])
        total = per_stream("total", [2 * RH, GT * RPT])
        inv = per_stream("inv", [2 * RH, GT * RPT])
        qk = per_stream("qk", [2 * RH, GT * P])
        qk_tok = per_stream("qk_tok", [P, GT, 2 * RH])
        kx = per_stream("kx", [P, KC, GT * RH])
        val = per_stream("val", [P, KC, GT * RH])
        val_out = per_stream("val_out", [RH, GT, C])
        z = per_stream("z", [P, GT, C])
        bank = [[ctx.enter_context(nc.psum_tensor(f"at_bank{i}_{s}", [P, 512], F32)) for s in range(STREAMS)] for i in range(4)]
        loaded = counter("at_loaded")
        names = """tok_ready turned tokT_ready qk_done neg_ready exp_done pos_ready sum_ready total_ready inv_ready invs_ready
            qkn_ready qk_ready qk_turned qk_tok_ready kx_done kx_ready val_done val_ready vo_done vo_ready out_done z_ready x_ready""".split()
        S = {n: sems(n) for n in names}
        passed = {e: counter(f"at_passed_{e}") for e in ("dve", "pe")}
        block = ctx.enter_context(nc.Block())
        N = GROUPS // STREAMS
        both = range(STREAMS)

        @block.sync
        def _(sp):
            for t, n in ((w_qk, "w_qk"), (w_v, "w_v"), (w_o, "w_o")):
                sp.dma_start(t[:, :, :], d[n].rearrange("(k p) f -> p k f", p=P)).then_inc(loaded, 16)
            for t, n in ((b_qk, "b_qk"), (scale, "qk_scale"), (row_mask, "row_mask"), (head_mask, "head_mask"), (b_v, "b_v")):
                sp.dma_start(t[:], d[n]).then_inc(loaded, 16)
            sp.dma_start(b_o[:, :], row_on_all(d["b_o"], C)).then_inc(loaded, 16)

        N_LOADED = 16 * 9

        @block.tensor
        def _(pe):
            pe.wait_ge(loaded, N_LOADED)
            with pe.Fori(0, N) as t:
                n = t + 1
                for s in both:
                    pe.wait_ge(S["tok_ready"][s], n)
                    for k in range(KC):
                        for j in range(GT):
                            mm = nc.tensor.transpose(bank[k][s][:, j * P:(j + 1) * P], tok[s][:, j, k * P:(k + 1) * P], ident[:, :])
                    mm.then_inc(S["turned"][s], 1)
                for s in both:
                    pe.wait_ge(S["tokT_ready"][s], n)
                    for k in range(KC):
                        mm = nc.tensor.matmul(bank[2][s][0:2 * RH, :], w_qk[:, k, :], tokT[s][:, k, :], start=(k == 0), stop=(k == KC - 1))
                    mm.then_inc(S["qk_done"][s], 1)
                for s in both:
                    pe.wait_ge(S["qk_ready"][s], n)
                    pe.sem_inc(passed["pe"], 1)
                    for j in range(GT):
                        mm = nc.tensor.transpose(bank[2][s][:, j * 2 * RH:(j + 1) * 2 * RH], qk[s][:, j * P:(j + 1) * P], ident[0:2 * RH, 0:2 * RH])
                    mm.then_inc(S["qk_turned"][s], 1)
                for s in both:
                    pe.wait_ge(S["qk_tok_ready"][s], n)
                    for k in range(KC):
                        for j in range(GT):
                            mm = nc.tensor.matmul(bank[0][s][:, k * GT * RH + j * RH:k * GT * RH + (j + 1) * RH],
                                                  tok[s][:, j, k * P:(k + 1) * P], qk_tok[s][:, j, RH:2 * RH], start=True, stop=True)
                    mm.then_inc(S["kx_done"][s], 1)
                for s in both:
                    pe.wait_ge(S["kx_ready"][s], n)
                    for m in range(KC):
                        for k in range(KC):
                            mm = nc.tensor.matmul(bank[1][s][:, m * GT * RH:(m + 1) * GT * RH], w_v[:, k, m * P:(m + 1) * P], kx[s][:, k, :],
                                                  start=(k == 0), stop=(k == KC - 1))
                    mm.then_inc(S["val_done"][s], 1)
                for s in both:
                    pe.wait_ge(S["val_ready"][s], n)
                    for j in range(GT):
                        for m in range(KC):
                            mm = nc.tensor.matmul(bank[j // 2][s][0:RH, j % 2 * C:(j % 2 + 1) * C], val[s][:, m, j * RH:(j + 1) * RH], w_o[:, m, :],
                                                  start=(m == 0), stop=(m == KC - 1))
                    mm.then_inc(S["vo_done"][s], 1)
                for s in both:
                    pe.wait_ge(S["vo_ready"][s], n)
                    pe.sem_inc(passed["pe"], 1)
                    for j in range(GT):
                        mm = nc.tensor.matmul(bank[2 + j // 2][s][:, j % 2 * C:(j % 2 + 1) * C], qk[s][0:RH, j * P:(j + 1) * P], val_out[s][:, j, :],
                                              start=True, stop=True)
                    mm.then_inc(S["out_done"][s], 1)

        @block.scalar
        def _(act):
            act.wait_ge(loaded, N_LOADED)
            with act.Fori(0, N) as t:
                n = t + 1
                for s in both:
                    act.wait_ge(S["turned"][s], n)
                    for k in range(KC):
                        ins = nc.scalar.copy(tokT[s][:, k, :], bank[k][s][:, :])
                    ins.then_inc(S["tokT_ready"][s], 1)
                for s in both:
                    act.wait_ge(S["neg_ready"][s], n)
                    nc.scalar.activation(neg_exp[s][:, :], neg[s][:, :], ACT.Exp).then_inc(S["exp_done"][s], 1)
                for s in both:
                    act.wait_ge(S["qk_turned"][s], n)
                    nc.scalar.copy(qk_tok[s][:, :, :].rearrange("p j c -> p (j c)"), bank[2][s][:, 0:GT * 2 * RH]).then_inc(S["qk_tok_ready"][s], 1)
                for s in both:
                    act.wait_ge(S["kx_done"][s], n)
                    nc.scalar.copy(kx[s][:, :, :].rearrange("p k c -> p (k c)"), bank[0][s][:, 0:KC * GT * RH]).then_inc(S["kx_ready"][s], 1)
                for s in both:
                    act.wait_ge(S["vo_done"][s], n)
                    for i in range(2):
                        ins = nc.scalar.copy(val_out[s][:, 2 * i:2 * i + 2, :].rearrange("p j c -> p (j c)"), bank[i][s][0:RH, :])
                    ins.then_inc(S["vo_ready"][s], 1)

        @block.vector
        def _(dve):
            dve.wait_ge(loaded, N_LOADED)
            for s in both:
                dve.sem_inc(S["x_ready"][s], 1)
            with dve.Fori(0, N) as t:
                n = t + 1
                for s in both:
                    dve.wait_ge(S["x_ready"][s], n)
                    for j in range(GT):
                        at = (t + s * N) * GT + j
                        ins = nc.vector.tensor_scalar(tok[s][:, j, :], X[:, bass.ds(at, 1), :].rearrange("p a c -> p (a c)"), mean[:, bass.ds(at, 1)],
                                                      rstd[:, bass.ds(at, 1)], ALU.subtract, ALU.mult)
                    ins.then_inc(S["tok_ready"][s], 1)
                for s in both:
                    dve.wait_ge(S["qk_done"][s], n)
                    nc.vector.tensor_scalar(neg[s][:, :], bank[2][s][0:2 * RH, :], b_qk[:, 0:1], 0.0, ALU.add, ALU.min).then_inc(S["neg_ready"][s], 1)
                    nc.vector.tensor_scalar(pos[s][:, :], bank[2][s][0:2 * RH, :], b_qk[:, 0:1], 0.0, ALU.add, ALU.max).then_inc(S["pos_ready"][s], 1)
                for s in both:
                    dve.wait_ge(S["pos_ready"][s], n)
                    dve.wait_ge(S["exp_done"][s], n)
                    nc.vector.tensor_tensor(pos[s][:, :], pos[s][:, :], neg_exp[s][:, :], ALU.add).then_inc(S["sum_ready"][s], 1)
                    dve.wait_ge(S["sum_ready"][s], n)
                    nc.vector.tensor_reduce(total[s][:, :], pos[s][:, :].rearrange("p (r c) -> p r c", c=ROW), AX.X, ALU.add)\
                        .then_inc(S["total_ready"][s], 1)
                    nc.vector.tensor_tensor(qk[s][:, :].rearrange("p (j c) -> p j c", j=GT), pos[s][:, :].rearrange("p (j c) -> p j c", j=GT),
                                            row_mask[:, :].unsqueeze(1).broadcast_to([2 * RH, GT, P]), ALU.mult).then_inc(S["qkn_ready"][s], 1)
                    dve.wait_ge(S["total_ready"][s], n)
                    nc.vector.reciprocal(inv[s][:, :], total[s][:, :]).then_inc(S["inv_ready"][s], 1)
                    dve.wait_ge(S["inv_ready"][s], n)
                    nc.vector.tensor_scalar(inv[s][:, :], inv[s][:, :], scale[:, 0:1], None, ALU.mult).then_inc(S["invs_ready"][s], 1)
                    dve.wait_ge(S["invs_ready"][s], n)
                    dve.wait_ge(S["qkn_ready"][s], n)
                    q3 = qk[s][:, :].rearrange("p (r c) -> p r c", c=ROW)
                    nc.vector.tensor_tensor(q3, q3, inv[s][:, :].unsqueeze(2).broadcast_to([2 * RH, GT * RPT, ROW]), ALU.mult)\
                        .then_inc(S["qk_ready"][s], 1)
                for s in both:
                    dve.wait_ge(S["val_done"][s], n)
                    for m in range(KC):
                        ins = nc.vector.scalar_tensor_tensor(out=val[s][:, m, :], in0=bank[1][s][:, m * GT * RH:(m + 1) * GT * RH], scalar=b_v[:, m:m + 1],
                                                             in1=head_mask[:, m, :], op0=ALU.add, op1=ALU.mult)
                    ins.then_inc(S["val_ready"][s], 1)
                for s in both:
                    dve.wait_ge(S["out_done"][s], n)
                    for i in range(2):
                        ins = nc.vector.tensor_tensor(z[s][:, 2 * i:2 * i + 2, :], bank[2 + i][s][:, :].rearrange("p (j c) -> p j c", j=2),
                                                      b_o[:, :].unsqueeze(1).broadcast_to([P, 2, C]), ALU.add)
                    ins.then_inc(S["z_ready"][s], 1)
                    dve.wait_ge(S["z_ready"][s], n)
                    xt = X[:, bass.ds((t + s * N) * GT, GT), :]
                    nc.vector.tensor_tensor(xt, xt, z[s][:, :, :], ALU.add).then_inc(S["x_ready"][s], 1)


EXP1 = 4
GH = 4
GF = GH * EXP1
GM = GF + GH
GT1 = GF + 2 * GH
NODES = TILES * P
EDGE_COLS = 8192
ECB = 8
BITS = 13
DST_TILES = NODES // P


def node_features(nc, d, X, ident, mean, rstd, h_all):
    with ExitStack() as ctx:
        counter = counters(nc, ctx)
        sb = lambda n, s, dt=F32: ctx.enter_context(nc.sbuf_tensor("nf_" + n, s, dt))
        both = range(2)
        w = sb("w", [P, KC, GF])
        tok = [sb(f"tok{s}", [P, TPH, C]) for s in both]
        tokT = [sb(f"tokT{s}", [P, KC, HALF]) for s in both]
        bank_t = [[ctx.enter_context(nc.psum_tensor(f"nf_bt{k}_{s}", [P, 512], F32)) for s in both] for k in range(KC)]
        bank_f = [ctx.enter_context(nc.psum_tensor(f"nf_bf{s}", [P, TPH * GF], F32)) for s in both]
        loaded = counter("nf_loaded")
        S = {n: [counter(f"nf_{n}{s}") for s in both] for n in ("tok_ready", "turned", "tokT_ready", "f_done", "f_copied")}
        block = ctx.enter_context(nc.Block())
        N = TILES // TPH // 2

        @block.sync
        def _(sp):
            sp.dma_start(w[:, :, :], d["w_gat"].rearrange("(k p) f -> p k f", p=P)).then_inc(loaded, 16)

        @block.vector
        def _(dve):
            for s in both:
                dve.sem_inc(S["turned"][s], 1)
            with dve.Fori(0, N) as t:
                for s in both:
                    dve.wait_ge(S["turned"][s], t + 1)
                    for i in range(TPH):
                        at = t * (2 * TPH) + (s * TPH + i)
                        ins = nc.vector.tensor_scalar(tok[s][:, i, :], X[:, bass.ds(at, 1), :].rearrange("p a c -> p (a c)"),
                                                      mean[:, bass.ds(at, 1)], rstd[:, bass.ds(at, 1)], ALU.subtract, ALU.mult)
                    ins.then_inc(S["tok_ready"][s], 1)

        @block.tensor
        def _(pe):
            pe.wait_ge(loaded, 16)
            for s in both:
                pe.sem_inc(S["tokT_ready"][s], 1)
            with pe.Fori(0, N) as t:
                for s in both:
                    pe.wait_ge(S["tokT_ready"][s], t + 1)
                    pe.wait_ge(S["tok_ready"][s], t + 1)
                    for k in range(KC):
                        for i in range(TPH):
                            mm = nc.tensor.transpose(bank_t[k][s][:, i * P:(i + 1) * P], tok[s][:, i, k * P:(k + 1) * P], ident[:, :])
                    mm.then_inc(S["turned"][s], 1)
                for s in both:
                    pe.wait_ge(S["tokT_ready"][s], t + 2)
                    for i in range(TPH):
                        for k in range(KC):
                            mm = nc.tensor.matmul(bank_f[s][:, i * GF:(i + 1) * GF], tokT[s][:, k, i * P:(i + 1) * P], w[:, k, :],
                                                  start=(k == 0), stop=(k == KC - 1))
                    mm.then_inc(S["f_done"][s], 1)

        @block.scalar
        def _(act):
            with act.Fori(0, N) as t:
                for s in both:
                    act.wait_ge(S["turned"][s], t + 2)
                    for k in range(KC):
                        ins = nc.scalar.copy(tokT[s][:, k, :], bank_t[k][s][:, :])
                    ins.then_inc(S["tokT_ready"][s], 1)
                for s in both:
                    act.wait_ge(S["f_done"][s], t + 1)
                    nc.scalar.copy(h_all[:, bass.ds(t * (2 * TPH) + s * TPH, TPH), :].rearrange("p i f -> p (i f)"), bank_f[s][:, :])\
                        .then_inc(S["f_copied"][s], 1)


def attention_tables(nc, d, h_all, own, src_rows, dst_rows):
    with ExitStack() as ctx:
        counter = counters(nc, ctx)
        sb = lambda n, s, dt=F32: ctx.enter_context(nc.sbuf_tensor("tb_" + n, s, dt))
        att = [sb(f"att{i}", [P, GF]) for i in range(2)]
        prod = [sb(f"prod{i}", [P, TILES, GF]) for i in range(2)]
        a_src, a_dst, diff, total, low, high = (sb(n, [P, TILES, GH]) for n in ("a_src", "a_dst", "diff", "total", "low", "high"))
        own_max, g = sb("own_max", [P, GH]), sb("g", [P, GH])
        src = sb("src", [P, TILES, GT1])
        dst = sb("dst", [P, TILES, 2 * GH])
        both_w = sb("both_w", [P, TILES, 2 * GH])
        sem = lambda n: counter("tb_" + n)
        names = """loaded prods a_ready max_ready g_ready diffs_ready bounds_ready factors_ready h_placed w_pairs w_ready own_ready stored""".split()
        S = {n: sem(n) for n in names}
        block = ctx.enter_context(nc.Block())
        wide = lambda a: a[:, :].unsqueeze(1).broadcast_to([P, TILES, a.shape[-1]])

        @block.sync
        def _(sp):
            for a, n in zip(att, ("att_src", "att_dst")):
                sp.dma_start(a[:, :], row_on_all(d[n], GF)).then_inc(S["loaded"], 16)
            sp.wait_ge(S["factors_ready"], 4)
            sp.wait_ge(S["h_placed"], 1)
            sp.dma_start(src_rows.rearrange("(i p) c -> p i c", p=P), src[:, :, :]).then_inc(S["stored"], 16)
            sp.dma_start(dst_rows.rearrange("(i p) c -> p i c", p=P), dst[:, :, :]).then_inc(S["stored"], 16)
            sp.wait_ge(S["stored"], 32)

        @block.gpsimd
        def _(pool):
            pool.wait_ge(S["max_ready"], 1)
            nc.gpsimd.partition_all_reduce(g[:, :], own_max[:, :], P, bass.bass_isa.ReduceOp.max).then_inc(S["g_ready"], 1)

        @block.vector
        def _(dve):
            dve.wait_ge(S["loaded"], 32)
            for i in range(2):
                ins = nc.vector.tensor_tensor(prod[i][:, :, :], h_all[:, :, :], wide(att[i]), ALU.mult)
            ins.then_inc(S["prods"], 1)
            nc.vector.tensor_copy(src[:, :, 0:GF], h_all[:, :, :]).then_inc(S["h_placed"], 1)
            dve.wait_ge(S["prods"], 1)
            for a, p_ in ((a_src, prod[0]), (a_dst, prod[1])):
                ins = nc.vector.tensor_reduce(a[:, :, :], p_[:, :, :].rearrange("p t (h e) -> p t h e", h=GH), AX.X, ALU.add)
            ins.then_inc(S["a_ready"], 1)
            dve.wait_ge(S["a_ready"], 1)
            nc.vector.tensor_reduce(own_max[:, :], a_src[:, :, :].rearrange("p t h -> p h t"), AX.X, ALU.max).then_inc(S["max_ready"], 1)
            dve.wait_ge(S["g_ready"], 1)
            nc.vector.tensor_tensor(diff[:, :, :], a_src[:, :, :], wide(g), ALU.subtract)
            nc.vector.tensor_tensor(total[:, :, :], a_dst[:, :, :], wide(g), ALU.add).then_inc(S["diffs_ready"], 1)
            dve.wait_ge(S["diffs_ready"], 1)
            nc.vector.tensor_scalar(low[:, :, :], total[:, :, :], 0.8, 0.0, ALU.mult, ALU.min)
            nc.vector.tensor_scalar(high[:, :, :], total[:, :, :], -0.8, 0.0, ALU.mult, ALU.min).then_inc(S["bounds_ready"], 1)
            dve.wait_ge(S["factors_ready"], 4)
            nc.vector.tensor_tensor(both_w[:, :, :], src[:, :, GF:GT1], dst[:, :, :], ALU.mult).then_inc(S["w_pairs"], 1)
            dve.wait_ge(S["w_pairs"], 1)
            nc.vector.tensor_tensor(own[:, :, GF:GM], both_w[:, :, 0:GH], both_w[:, :, GH:2 * GH], ALU.max).then_inc(S["w_ready"], 1)
            dve.wait_ge(S["w_ready"], 1)
            for e in range(EXP1):
                nc.vector.tensor_tensor(own[:, :, 0:GF].rearrange("p t (h e) -> p t h e", h=GH)[:, :, :, e],
                                        h_all[:, :, :].rearrange("p t (h e) -> p t h e", h=GH)[:, :, :, e], own[:, :, GF:GM], ALU.mult)

        @block.scalar
        def _(act):
            act.wait_ge(S["diffs_ready"], 1)
            nc.scalar.activation(src[:, :, GF:GF + GH], diff[:, :, :], ACT.Exp).then_inc(S["factors_ready"], 1)
            nc.scalar.activation(src[:, :, GF + GH:GT1], diff[:, :, :], ACT.Exp, scale=0.2).then_inc(S["factors_ready"], 1)
            act.wait_ge(S["bounds_ready"], 1)
            nc.scalar.activation(dst[:, :, 0:GH], low[:, :, :], ACT.Exp).then_inc(S["factors_ready"], 1)
            nc.scalar.activation(dst[:, :, GH:2 * GH], high[:, :, :], ACT.Exp).then_inc(S["factors_ready"], 1)


def compact_edges(nc, d, edge, longest):
    with ExitStack() as ctx:
        counter = counters(nc, ctx)
        sb = lambda n, s, dt: ctx.enter_context(nc.sbuf_tensor("ce_" + n, s, dt))
        I16 = mybir.dt.int16
        raw = sb("raw", [P, EDGE_COLS], I32)
        valid = sb("valid", [P, EDGE_COLS], I16)
        shift = sb("shift", [P, EDGE_COLS], I16)
        move = sb("move", [P, EDGE_COLS], I16)
        place = sb("place", [P, EDGE_COLS], I16)
        mine = sb("mine", [P, 1], F32)
        most = sb("most", [P, 1], F32)
        loaded, packed, step, counted, most_ready = (
            counter("ce_" + n) for n in ("loaded", "packed", "step", "counted", "most_ready"))
        block = ctx.enter_context(nc.Block())

        @block.sync
        def _(sp):
            sp.dma_start(edge[:, 0:EDGE_COLS], d["edges"][1]).then_inc(loaded, 16)
            sp.dma_start(raw[:, :], d["edges"][0]).then_inc(loaded, 16)
            sp.dma_start(place[:, :], row_on_all(d["place"], EDGE_COLS)).then_inc(loaded, 16)

        @block.gpsimd
        def _(pool):
            pool.wait_ge(counted, 1)
            nc.gpsimd.partition_all_reduce(most[:, :], mine[:, :], P, bass.bass_isa.ReduceOp.max).then_inc(most_ready, 1)

        @block.vector
        def _(dve):
            count = [0]

            def then(ins):
                count[0] += 1
                ins.then_inc(step, 1)
                dve.wait_ge(step, count[0])

            N = EDGE_COLS
            nc.vector.memset(edge[:, N:], 0)
            dve.wait_ge(loaded, 48)
            then(nc.vector.tensor_scalar(valid[:, :], edge[:, 0:EDGE_COLS], NODES, None, ALU.is_lt))
            then(nc.vector.tensor_tensor_scan(move[:, :], valid[:, :], valid[:, :], 0.0, ALU.add, ALU.max))
            nc.vector.tensor_copy(mine[:, :], move[:, N - 1:N]).then_inc(counted, 1)
            then(nc.vector.tensor_tensor(shift[:, :], place[:, :], move[:, :], ALU.subtract))
            then(nc.vector.tensor_tensor(shift[:, :], shift[:, :], valid[:, :], ALU.mult))
            nc.vector.tensor_scalar(raw[:, :], raw[:, :], NODES - 1, None, ALU.min)
            then(nc.vector.tensor_scalar(edge[:, 0:EDGE_COLS], edge[:, 0:EDGE_COLS], BITS, None, ALU.logical_shift_left))
            then(nc.vector.tensor_tensor(edge[:, 0:EDGE_COLS], edge[:, 0:EDGE_COLS], raw[:, :], ALU.bitwise_or))
            for b in range(BITS):
                by = 1 << b
                then(nc.vector.tensor_scalar(move[:, :], shift[:, :], by, None, ALU.bitwise_and))
                then(nc.vector.copy_predicated(edge[:, 0:N - by], move[:, by:N], edge[:, by:N]))
                then(nc.vector.scalar_tensor_tensor(out=valid[:, :], in0=move[:, :], scalar=0, in1=shift[:, :], op0=ALU.is_gt, op1=ALU.mult))
                then(nc.vector.tensor_tensor(shift[:, :], shift[:, :], valid[:, :], ALU.subtract))
                then(nc.vector.tensor_tensor(shift[:, 0:N - by], shift[:, 0:N - by], valid[:, by:N], ALU.add))
            then(nc.vector.tensor_scalar(raw[:, :], place[:, :], mine[:, 0:1], None, ALU.is_gt))
            then(nc.vector.tensor_scalar(raw[:, :], raw[:, :], 2 * BITS, None, ALU.logical_shift_left))
            then(nc.vector.tensor_tensor(edge[:, 0:EDGE_COLS], edge[:, 0:EDGE_COLS], raw[:, :], ALU.bitwise_or))
            dve.wait_ge(most_ready, 1)
            nc.vector.tensor_copy(longest[:, :], most[:, :])


def sum_edges(nc, d, edge, longest, src_rows, dst_rows, own, agg):
    with ExitStack() as ctx:
        counter = counters(nc, ctx)
        sb = lambda n, s, dt=F32: ctx.enter_context(nc.sbuf_tensor("se_" + n, s, dt))
        sem = lambda n: counter("se_" + n)
        both = range(2)
        RING = 4
        lane = sb("lane", [P, P])
        zero = sb("zero", [P, P])
        now = [sb(f"now{u}", [P, ECB], I32) for u in both]
        src_at = [sb(f"src_at{u}", [P, ECB], I32) for u in both]
        dst_full = [sb(f"dst_full{u}", [P, ECB], I32) for u in both]
        dst_at = [sb(f"dst_at{u}", [P, ECB], I32) for u in both]
        dst_lane = [sb(f"dst_lane{u}", [P, ECB], I32) for u in both]
        dst_tile = [sb(f"dst_tile{u}", [P, ECB], I32) for u in both]
        lane_f = [sb(f"lane_f{u}", [P, ECB]) for u in both]
        tile_f = [sb(f"tile_f{u}", [P, ECB]) for u in both]
        is_lane = [sb(f"is_lane{u}", [P, ECB, P]) for u in both]
        is_tile = [sb(f"is_tile{u}", [P, ECB, DST_TILES]) for u in both]
        src_row = [sb(f"src_row{u}", [P, ECB, GT1]) for u in both]
        dst_row = [sb(f"dst_row{u}", [P, ECB, 2 * GH]) for u in both]
        pair = [sb(f"pair{u}", [P, ECB, 2 * GH]) for u in both]
        msg = [sb(f"msg{u}", [P, ECB, GM]) for u in both]
        spread = [sb(f"spread{i}", [P, DST_TILES, GM]) for i in range(RING)]
        bank = [ctx.enter_context(nc.psum_tensor(f"se_b{i}", [P, 512], F32)) for i in range(3)]
        WIDTH = DST_TILES * GM
        parts = [(i, i * 512, min(512, WIDTH - i * 512)) for i in range(3)]
        names = """loaded cleared taken decoded floated hot_ready gathered0 gathered1 paired weighed msg_ready spread_ready spread_used summed""".split()
        S = {n: sem(n) for n in names}
        gathered = [S["gathered0"], S["gathered1"]]
        passed = {e: sem("passed_" + e) for e in ("dve", "pe", "pool")}
        block = ctx.enter_context(nc.Block())
        STEPS = EDGE_COLS // (2 * ECB)
        count_in = longest[0:1, 0:1]

        @block.sync
        def _(sp):
            sp.dma_start(lane[:, :], row_on_all(d["lane"], P)).then_inc(S["loaded"], 16)

        @block.gpsimd
        def _(pool):
            m = pool.value_load(count_in, min_val=0, max_val=EDGE_COLS)
            with pool.Fori(0, STEPS) as t:
                with pool.If(t * (2 * ECB) < m):
                    for u in both:
                        pool.wait_ge(S["decoded"], 2 * t + (u + 1))
                        pool.wait_ge(S["msg_ready"], 2 * t + (u + 1))
                        pool.sem_inc(passed["pool"], 1)
                        for c in range(ECB):
                            for row, rows, at in ((src_row, src_rows, src_at), (dst_row, dst_rows, dst_at)):
                                pool.indirect_dma_start(out=row[u][:, c, :], out_offset=None, in_=rows,
                                                        in_offset=bass.IndirectOffsetOnAxis(ap=at[u][:, c:c + 1], axis=0),
                                                        bounds_check=NODES - 1, oob_is_err=False).then_inc(gathered[u], 16)

        @block.vector
        def _(dve):
            m = dve.value_load(count_in, min_val=0, max_val=EDGE_COLS)
            nc.vector.memset(zero[:, :], 0.0).then_inc(S["cleared"], 1)
            for n, k in (("msg_ready", 2), ("spread_ready", 1), ("spread_used", ECB + 1)):
                for _ in range(k):
                    dve.sem_inc(S[n], 1)
            dve.wait_ge(S["loaded"], 16)

            def decode(step_, u):
                n = step_ + 1
                dve.wait_ge(S["msg_ready"], n)
                nc.vector.tensor_copy(now[u][:, :], edge[:, bass.ds(step_ * ECB, ECB)]).then_inc(S["taken"], 1)
                dve.wait_ge(S["taken"], 2 * n - 1)
                nc.vector.tensor_scalar(src_at[u][:, :], now[u][:, :], NODES - 1, None, ALU.bitwise_and)
                nc.vector.tensor_scalar(dst_tile[u][:, :], now[u][:, :], BITS + 7, None, ALU.logical_shift_right)
                nc.vector.tensor_scalar(dst_full[u][:, :], now[u][:, :], BITS, None, ALU.logical_shift_right).then_inc(S["taken"], 1)
                dve.wait_ge(S["taken"], 2 * n)
                nc.vector.tensor_scalar(dst_lane[u][:, :], dst_full[u][:, :], P - 1, None, ALU.bitwise_and)
                nc.vector.tensor_scalar(dst_at[u][:, :], dst_full[u][:, :], NODES - 1, None, ALU.bitwise_and).then_inc(S["decoded"], 1)
                dve.wait_ge(S["decoded"], n)
                nc.vector.tensor_copy(lane_f[u][:, :], dst_lane[u][:, :])
                nc.vector.tensor_copy(tile_f[u][:, :], dst_tile[u][:, :]).then_inc(S["floated"], 1)

            def mark(step_, u):
                dve.wait_ge(S["floated"], step_ + 1)
                dve.wait_ge(S["spread_used"], step_ * ECB + 1)
                dve.sem_inc(passed["dve"], 1)
                nc.vector.tensor_tensor(is_lane[u][:, :, :], lane[:, :].unsqueeze(1).broadcast_to([P, ECB, P]),
                                        lane_f[u][:, :].unsqueeze(2).broadcast_to([P, ECB, P]), ALU.is_equal)
                nc.vector.tensor_tensor(is_tile[u][:, :, :], lane[:, 0:DST_TILES].unsqueeze(1).broadcast_to([P, ECB, DST_TILES]),
                                        tile_f[u][:, :].unsqueeze(2).broadcast_to([P, ECB, DST_TILES]), ALU.is_equal).then_inc(S["hot_ready"], 1)

            def spread_out(step_, u, c):
                dve.wait_ge(S["spread_used"], step_ * ECB + c + (ECB - 2))
                nc.vector.tensor_tensor(spread[c % RING][:, :, :], msg[u][:, c, :].unsqueeze(1).broadcast_to([P, DST_TILES, GM]),
                                        is_tile[u][:, c, :].unsqueeze(2).broadcast_to([P, DST_TILES, GM]), ALU.mult).then_inc(S["spread_ready"], 1)

            decode(0, 0)
            mark(0, 0)
            with dve.Fori(0, STEPS) as t:
                with dve.If(t * (2 * ECB) < m):
                    for u in both:
                        now_, next_ = 2 * t + u, 2 * t + (u + 1)
                        decode(next_, 1 - u)
                        dve.wait_ge(S["hot_ready"], now_ + 1)
                        dve.wait_ge(gathered[u], t * (32 * ECB) + 32 * ECB)
                        nc.vector.tensor_tensor(pair[u][:, :, :], src_row[u][:, :, GF:GT1], dst_row[u][:, :, :], ALU.mult).then_inc(S["paired"], 1)
                        dve.wait_ge(S["paired"], now_ + 1)
                        dve.wait_ge(S["spread_ready"], now_ * ECB + 1)
                        nc.vector.tensor_tensor(msg[u][:, :, GF:GM], pair[u][:, :, 0:GH], pair[u][:, :, GH:2 * GH], ALU.max).then_inc(S["weighed"], 1)
                        dve.wait_ge(S["weighed"], now_ + 1)
                        nc.vector.tensor_tensor(msg[u][:, :, 0:GF].rearrange("p c (h e) -> p c h e", h=GH),
                                                src_row[u][:, :, 0:GF].rearrange("p c (h e) -> p c h e", h=GH),
                                                msg[u][:, :, GF:GM].unsqueeze(3).broadcast_to([P, ECB, GH, EXP1]), ALU.mult).then_inc(S["msg_ready"], 1)
                        dve.wait_ge(S["msg_ready"], now_ + 3)
                        for c in range(ECB):
                            if c == ECB // 2:
                                mark(next_, 1 - u)
                            spread_out(now_, u, c)
            dve.wait_ge(S["summed"], 1)
            own_row = own[:, :, :].rearrange("p t m -> p (t m)")
            agg_row = agg[:, :, :].rearrange("p t m -> p (t m)")
            for i, o, w in parts:
                nc.vector.tensor_tensor(agg_row[:, o:o + w], bank[i][:, 0:w], own_row[:, o:o + w], ALU.add)

        @block.tensor
        def _(pe):
            m = pe.value_load(count_in, min_val=0, max_val=EDGE_COLS)
            own_row = own[:, :, :].rearrange("p t m -> p (t m)")
            pe.wait_ge(S["cleared"], 1)
            for i, o, w in parts:
                nc.tensor.matmul(bank[i][:, 0:w], zero[:, :], own_row[:, o:o + w], start=True, stop=False, skip_group_check=True)
            with pe.Fori(0, STEPS) as t:
                with pe.If(t * (2 * ECB) < m):
                    for u in both:
                        for c in range(ECB):
                            k = (2 * t + u) * ECB + c
                            pe.wait_ge(S["spread_ready"], k + 2)
                            pe.sem_inc(passed["pe"], 1)
                            row = spread[c % RING][:, :, :].rearrange("p t m -> p (t m)")
                            for i, o, w in parts:
                                mm = nc.tensor.matmul(bank[i][:, 0:w], is_lane[u][:, c, :], row[:, o:o + w], start=False, stop=False,
                                                      skip_group_check=True)
                            mm.then_inc(S["spread_used"], 1)
            for i, o, w in parts:
                mm = nc.tensor.matmul(bank[i][:, 0:w], zero[:, :], own_row[:, o:o + w], start=False, stop=True, skip_group_check=True)
            mm.then_inc(S["summed"], 1)


def scores_to_gate(nc, d, agg, gate):
    with ExitStack() as ctx:
        counter = counters(nc, ctx)
        sb = lambda n, s, dt=F32: ctx.enter_context(nc.sbuf_tensor("sg_" + n, s, dt))
        rows = {n: sb(n, [P, GF]) for n in ("b_gat", "ln_gamma", "ln_beta")}
        inv = sb("inv", [P, TILES, GH])
        f = sb("f", [P, TILES, GF])
        sq = sb("sq", [P, TILES, GF])
        total, mean, var, r, mh = (sb(n, [P, TILES]) for n in ("total", "mean", "var", "r", "mh"))
        score, low, chosen, ex = (sb(n, [P, TILES, EXP1]) for n in ("score", "low", "chosen", "ex"))
        beats = sb("beats", [P, TILES, EXP1, EXP1])
        top = sb("top", [P, TILES])
        loaded, step, var_ready, r_ready, low_ready, exp_done = (
            counter("sg_" + n) for n in ("loaded", "step", "var_ready", "r_ready", "low_ready", "exp_done"))
        block = ctx.enter_context(nc.Block())

        def wide(a, n):
            return a[:, :].unsqueeze(2).broadcast_to([P, TILES, n])

        def each(a):
            return a[:, :].unsqueeze(1).broadcast_to([P, TILES, GF])

        @block.sync
        def _(sp):
            for n, row in rows.items():
                sp.dma_start(row[:, :], row_on_all(d[n], GF)).then_inc(loaded, 16)

        @block.gpsimd
        def _(pool):
            pool.wait_ge(var_ready, 1)
            nc.gpsimd.tensor_tensor(r[:, :], var[:, :], mh[:, :], ALU.pow).then_inc(r_ready, 1)

        @block.scalar
        def _(act):
            act.wait_ge(low_ready, 1)
            nc.scalar.activation(ex[:, :, :], low[:, :, :], ACT.Exp).then_inc(exp_done, 1)

        @block.vector
        def _(dve):
            count = [0]

            def then(ins):
                count[0] += 1
                ins.then_inc(step, 1)
                dve.wait_ge(step, count[0])

            nc.vector.memset(mh[:, :], -0.5)
            nc.vector.memset(beats[:, :, :, :], 0.0)
            then(nc.vector.tensor_scalar(inv[:, :, :], agg[:, :, GF:GM], 1e-37, None, ALU.max))
            then(nc.vector.reciprocal(inv[:, :, :], inv[:, :, :]))
            dve.wait_ge(loaded, 48)
            then(nc.vector.tensor_tensor(f[:, :, :].rearrange("p t (h e) -> p t h e", h=GH), agg[:, :, 0:GF].rearrange("p t (h e) -> p t h e", h=GH),
                                         inv[:, :, :].unsqueeze(3).broadcast_to([P, TILES, GH, EXP1]), ALU.mult))
            then(nc.vector.tensor_tensor(f[:, :, :], f[:, :, :], each(rows["b_gat"]), ALU.add))
            then(nc.vector.tensor_reduce(total[:, :], f[:, :, :], AX.X, ALU.add))
            then(nc.vector.tensor_scalar(mean[:, :], total[:, :], 1.0 / GF, None, ALU.mult))
            then(nc.vector.tensor_tensor(f[:, :, :], f[:, :, :], wide(mean, GF), ALU.subtract))
            then(nc.vector.tensor_tensor(sq[:, :, :], f[:, :, :], f[:, :, :], ALU.mult))
            then(nc.vector.tensor_reduce(total[:, :], sq[:, :, :], AX.X, ALU.add))
            nc.vector.tensor_scalar(var[:, :], total[:, :], 1.0 / GF, LN_T_EPS, ALU.mult, ALU.add).then_inc(var_ready, 1)
            dve.wait_ge(r_ready, 1)
            then(nc.vector.tensor_tensor(f[:, :, :], f[:, :, :], wide(r, GF), ALU.mult))
            then(nc.vector.tensor_tensor(f[:, :, :], f[:, :, :], each(rows["ln_gamma"]), ALU.mult))
            then(nc.vector.tensor_tensor(f[:, :, :], f[:, :, :], each(rows["ln_beta"]), ALU.add))
            then(nc.vector.tensor_reduce(score[:, :, :], f[:, :, :].rearrange("p t (h e) -> p t e h", h=GH), AX.X, ALU.add))
            then(nc.vector.tensor_scalar(score[:, :, :], score[:, :, :], 1.0 / GH, None, ALU.mult))
            then(nc.vector.tensor_reduce(top[:, :], score[:, :, :], AX.X, ALU.max))
            nc.vector.tensor_tensor(low[:, :, :], score[:, :, :], wide(top, EXP1), ALU.subtract).then_inc(low_ready, 1)
            for e in range(EXP1):
                for lo, hi, op in ((0, e, ALU.is_gt), (e + 1, EXP1, ALU.is_ge)):
                    if hi > lo:
                        ins = nc.vector.tensor_tensor(beats[:, :, e, lo:hi], score[:, :, e:e + 1].broadcast_to([P, TILES, hi - lo]),
                                                      score[:, :, lo:hi], op)
            then(ins)
            then(nc.vector.tensor_reduce(chosen[:, :, :], beats[:, :, :, :], AX.X, ALU.add))
            then(nc.vector.tensor_scalar(chosen[:, :, :], chosen[:, :, :], 1.5, None, ALU.is_gt))
            dve.wait_ge(exp_done, 1)
            then(nc.vector.tensor_tensor(ex[:, :, :], ex[:, :, :], chosen[:, :, :], ALU.mult))
            then(nc.vector.tensor_reduce(total[:, :], ex[:, :, :], AX.X, ALU.add))
            then(nc.vector.reciprocal(total[:, :], total[:, :]))
            nc.vector.tensor_tensor(gate[:, :, :], ex[:, :, :], wide(total, EXP1), ALU.mult)


def graph_scores(nc, d, X, ident, mean, rstd, gate):
    with ExitStack() as ctx:
        sb = lambda n, s, dt=F32: ctx.enter_context(nc.sbuf_tensor("gs_" + n, s, dt))
        own = sb("own", [P, TILES, GM])
        agg = sb("agg", [P, TILES, GM])
        longest = sb("longest", [P, 1], I32)
        src_rows = nc.dram_tensor("gs_src_rows", (NODES, GT1), F32, kind="Internal").ap()
        dst_rows = nc.dram_tensor("gs_dst_rows", (NODES, 2 * GH), F32, kind="Internal").ap()
        with ExitStack() as c1:
            h_all = c1.enter_context(nc.sbuf_tensor("gs_h_all", [P, TILES, GF], F32))
            node_features(nc, d, X, ident, mean, rstd, h_all)
            attention_tables(nc, d, h_all, own, src_rows, dst_rows)
        edge = sb("edge", [P, EDGE_COLS + ECB], I32)
        compact_edges(nc, d, edge, longest)
        sum_edges(nc, d, edge, longest, src_rows, dst_rows, own, agg)
        scores_to_gate(nc, d, agg, gate)


def experts_by_token(nc, d, X, ident, mean, rstd, gate):
    with ExitStack() as ctx:
        counter = counters(nc, ctx)
        sb = lambda n, s, dt=F32: ctx.enter_context(nc.sbuf_tensor("m1_" + n, s, dt))
        sem = lambda n: counter("m1_" + n)
        w1 = sb("w1", [P, EXP1, KC, F])
        w2 = sb("w2", [P, EXP1, FM, C])
        b1 = sb("b1", [P, EXP1, FM])
        b2 = sb("b2", [EXP1, C])
        tok = sb("tok", [P, TPH, C])
        gate_in = sb("gate_in", [P, TPH, EXP1])
        gateT = sb("gateT", [EXP1, HALF])
        tokT = sb("tokT", [P, KC, HALF])
        hid = [sb(f"hid{i}", [P, FM, HALF]) for i in range(2)]
        z = sb("z", [P, TPH, C])
        bank_t = [ctx.enter_context(nc.psum_tensor(f"m1_bt{i}", [P, 512], F32)) for i in range(2)]
        bank_h = [ctx.enter_context(nc.psum_tensor(f"m1_bh{i}", [P, 512], F32)) for i in range(2)]
        bank_y = [ctx.enter_context(nc.psum_tensor(f"m1_by{i}", [P, C], F32)) for i in range(4)]
        names = """w_loaded tok_ready turned tokT_ready gate_turned gateT_ready h_done h_free y_done y_free z_ready x_ready hid_free""".split()
        S = {n: sem(n) for n in names}
        passed = sem("passed")
        block = ctx.enter_context(nc.Block())
        BLOCKS = TILES // TPH
        HPB = EXP1 * FM
        YPB = (EXP1 + 1) * TPH

        @block.sync
        def _(sp):
            for e in range(EXP1):
                sp.dma_start(w1[:, e, :, :], d["W1_1"][e].rearrange("(k p) f -> p k f", p=P)).then_inc(S["w_loaded"], 16)
                sp.dma_start(w2[:, e, :, :], d["W2_1"][e].rearrange("(m p) c -> p m c", p=P)).then_inc(S["w_loaded"], 16)
            sp.dma_start(b1[:, :, :], d["b1_1"]).then_inc(S["w_loaded"], 16)
            sp.dma_start(b2[:, :], d["b2_1"]).then_inc(S["w_loaded"], 16)

        N_LOADED = 16 * (2 * EXP1 + 2)

        @block.tensor
        def _(pe):
            def hidden(b, e):
                for m in range(FM):
                    g = e * FM + m
                    pe.wait_ge(S["h_free"], HPB * b + g + 1)
                    for k in range(KC):
                        mm = nc.tensor.matmul(bank_h[g % 2][:, :], w1[:, e, k, m * P:(m + 1) * P], tokT[:, k, :], start=(k == 0), stop=(k == KC - 1))
                    mm.then_inc(S["h_done"], 1)

            def output(b, e):
                pe.wait_ge(S["h_free"], HPB * b + (e + 1) * FM + 2)
                for i in range(TPH):
                    y = (e + 1) * TPH + i
                    pe.wait_ge(S["y_free"], YPB * b + y + 1)
                    for m in range(FM):
                        mm = nc.tensor.matmul(bank_y[y % 4][:, :], hid[e % 2][:, m, i * P:(i + 1) * P], w2[:, e, m, :], start=(m == 0), stop=(m == FM - 1))
                    mm.then_inc(S["y_done"], 1)

            pe.wait_ge(S["w_loaded"], N_LOADED)
            with pe.Fori(0, BLOCKS) as b:
                pe.wait_ge(S["tok_ready"], b + 1)
                for k in range(KC):
                    for i in range(TPH):
                        mm = nc.tensor.transpose(bank_t[k][:, i * P:(i + 1) * P], tok[:, i, k * P:(k + 1) * P], ident[:, :])
                mm.then_inc(S["turned"], 1)
                pe.wait_ge(S["y_free"], YPB * b + 4)
                pe.wait_ge(S["tokT_ready"], b + 1)
                pe.sem_inc(passed, 1)
                for i in range(TPH):
                    mm = nc.tensor.transpose(bank_t[0][0:EXP1, i * P:(i + 1) * P], gate_in[:, i, :], ident[:, :])
                mm.then_inc(S["gate_turned"], 1)
                hidden(b, 0)
                pe.wait_ge(S["gateT_ready"], b + 1)
                for i in range(TPH):
                    pe.wait_ge(S["y_free"], YPB * b + i + 1)
                    pe.sem_inc(passed, 1)
                    nc.tensor.matmul(bank_y[i][:, :], gateT[:, i * P:(i + 1) * P], b2[:, :], start=True, stop=True).then_inc(S["y_done"], 1)
                for e in range(1, EXP1):
                    hidden(b, e)
                    output(b, e - 1)
                output(b, EXP1 - 1)

        @block.scalar
        def _(act):
            act.wait_ge(S["w_loaded"], N_LOADED)
            with act.Fori(0, BLOCKS) as b:
                act.wait_ge(S["turned"], b + 1)
                for k in range(KC):
                    ins = nc.scalar.copy(tokT[:, k, :], bank_t[k][:, :])
                ins.then_inc(S["tokT_ready"], 1)
                act.wait_ge(S["gate_turned"], b + 1)
                nc.scalar.copy(gateT[:, :], bank_t[0][0:EXP1, :]).then_inc(S["gateT_ready"], 1)
                for e in range(EXP1):
                    act.wait_ge(S["y_done"], YPB * b + TPH + (e * TPH if e > 1 else 0))
                    for m in range(FM):
                        g = e * FM + m
                        act.wait_ge(S["h_done"], HPB * b + g + 1)
                        nc.scalar.activation(hid[e % 2][:, m, :], bank_h[g % 2][:, :], ACT.Gelu, bias=b1[:, e, m:m + 1]).then_inc(S["h_free"], 1)

        @block.vector
        def _(dve):
            for n, k in (("h_free", 2), ("y_free", 4), ("x_ready", 1), ("y_done", TPH)):
                for _ in range(k):
                    dve.sem_inc(S[n], 1)
            with dve.Fori(0, BLOCKS) as b:
                dve.wait_ge(S["x_ready"], b + 1)
                nc.vector.tensor_copy(gate_in[:, :, :], gate[:, bass.ds(b * TPH, TPH), :])
                for i in range(TPH):
                    t = b * TPH + i
                    ins = nc.vector.tensor_scalar(tok[:, i, :], X[:, bass.ds(t, 1), :].rearrange("p a c -> p (a c)"), mean[:, bass.ds(t, 1)],
                                                  rstd[:, bass.ds(t, 1)], ALU.subtract, ALU.mult)
                ins.then_inc(S["tok_ready"], 1)
                for e in range(EXP1 + 1):
                    for i in range(TPH):
                        y = e * TPH + i
                        dve.wait_ge(S["y_done"], YPB * b + TPH + y + 1)
                        if e == 0:
                            nc.vector.tensor_copy(z[:, i, :], bank_y[y % 4][:, :]).then_inc(S["y_free"], 1)
                        else:
                            dve.wait_ge(S["y_free"], YPB * b + 4 + y - TPH + 1)
                            nc.vector.scalar_tensor_tensor(out=z[:, i, :], in0=bank_y[y % 4][:, :], scalar=gate_in[:, i, e - 1:e], in1=z[:, i, :],
                                                           op0=ALU.mult, op1=ALU.add).then_inc(S["y_free"], 1)
                dve.wait_ge(S["y_free"], YPB * b + 4 + YPB)
                xt = X[:, bass.ds(b * TPH, TPH), :]
                nc.vector.tensor_tensor(xt, xt, z[:, :, :], ALU.add).then_inc(S["x_ready"], 1)


def metaformer(nc, d, out):
    with ExitStack() as ctx:
        X = ctx.enter_context(nc.sbuf_tensor("X", [P, TILES, C], F32))
        ident = ctx.enter_context(nc.sbuf_tensor("ident", [P, P], F32))
        mean = ctx.enter_context(nc.sbuf_tensor("mean", [P, TILES], F32))
        rstd = ctx.enter_context(nc.sbuf_tensor("rstd", [P, TILES], F32))
        gate = ctx.enter_context(nc.sbuf_tensor("gate", [P, TILES, EXP1], F32))
        picked = ctx.enter_context(nc.sbuf_tensor("picked", [1, BATCH * TOPK], U32))
        weight = ctx.enter_context(nc.sbuf_tensor("weight", [P, BATCH * TOPK], F32))
        mamba_layers(nc, d, X, ident)
        norm_statistics(nc, X, mean, rstd, LN_T_EPS, "ln1")
        route_images(nc, d, X, ident, mean, rstd, picked, weight)
        experts_by_image(nc, d, X, ident, mean, rstd, picked, weight)
        norm_statistics(nc, X, mean, rstd, LN_C_EPS, "ln2")
        row_attention(nc, d, X, ident, mean, rstd)
        norm_statistics(nc, X, mean, rstd, LN_T_EPS, "ln3")
        graph_scores(nc, d, X, ident, mean, rstd, gate)
        experts_by_token(nc, d, X, ident, mean, rstd, gate)
        with ExitStack() as c2:
            stored = c2.enter_context(nc.semaphore("stored"))
            block = c2.enter_context(nc.Block())

            @block.sync
            def _(sp):
                sp.dma_start(out.rearrange("(i p) c -> p i c", p=P), X[:, :, :]).then_inc(stored, 16)
                sp.wait_ge(stored, 16)


def kernel(**inputs):
    import numpy as np
    import concourse.bacc as bacc
    from concourse.bass_utils import run_bass_kernel_spmd

    g = {k: np.asarray(v) for k, v in inputs.items()}
    a = {
        "x": g["x"].reshape(TILES * P, C),
        "in_projT": g["L0_conv_in_proj_w"].transpose(0, 2, 1),
        "out_projT": g["L0_conv_out_proj_w"].transpose(0, 2, 1),
        "norm_w": g["L0_conv_norm_w"].reshape(LAYERS, XM, P).transpose(2, 0, 1),
        "conv_w": g["L0_conv_conv_w"][:, :DIN].reshape(LAYERS, XM, P, TAPS).transpose(2, 0, 1, 3),
        "conv_b": g["L0_conv_conv_b"][:, :DIN].reshape(LAYERS, XM, P).transpose(2, 0, 1),
        "conv_w_bc": g["L0_conv_conv_w"][:, DIN:].reshape(LAYERS, 2, NST, TAPS).transpose(2, 0, 1, 3),
        "conv_b_bc": g["L0_conv_conv_b"][:, DIN:].reshape(LAYERS, 2, NST).transpose(2, 0, 1),
        "dt_bias": g["L0_conv_dt_bias"].T,
        "A_log": g["L0_conv_A_log"].T,
        "D": g["L0_conv_D"],
        "ident": np.eye(P, dtype=np.float32),
        "head_row": np.repeat(np.eye(HEADS, dtype=np.float32), P, axis=1),
        "last_row": np.repeat(np.eye(P, dtype=np.float32)[:, P - 1:], NST, axis=1),
    }
    a |= {
        "image_row": np.tile(np.eye(BATCH, dtype=np.float32).reshape(1, -1) / np.float32(SEQ), (P, 1)),
        "Wr": g["L0_ffn_Wr"], "br": g["L0_ffn_br"], "W1_0": g["L0_ffn_W1"], "W2_0": g["L0_ffn_W2"],
        "b1_0": g["L0_ffn_b1"].reshape(EXP0, FM, P).transpose(0, 2, 1), "b2_0": g["L0_ffn_b2"],
        "gamma0": g["L0_ffn_gamma"], "beta0": g["L0_ffn_beta"],
    }
    a |= {"W1_1": g["L1_ffn_W1"], "W2_1": g["L1_ffn_W2"], "b1_1": g["L1_ffn_b1"].reshape(EXP1, FM, P).transpose(2, 0, 1), "b2_1": g["L1_ffn_b2"]}
    a |= {
        "w_gat": g["L1_ffn_W_gat"], "att_src": g["L1_ffn_att_src"].reshape(-1), "att_dst": g["L1_ffn_att_dst"].reshape(-1),
        "b_gat": g["L1_ffn_b_gat"], "ln_gamma": g["L1_ffn_ln_gamma"], "ln_beta": g["L1_ffn_ln_beta"],
        "edges": g["L1_ffn_edge_index"].reshape(2, P, EDGE_COLS), "place": np.arange(1, EDGE_COLS + 1, dtype=np.int16),
        "lane": np.arange(P, dtype=np.float32),
    }
    rows = np.arange(2 * RH) % RH // AH
    a |= {
        "w_qk": np.concatenate([np.tile(g["L1_conv_Wq"].T, (1, RPT)), np.tile(g["L1_conv_Wk"].T, (1, RPT))], axis=1),
        "b_qk": np.concatenate([np.tile(g["L1_conv_bq"], RPT), np.tile(g["L1_conv_bk"], RPT)]).reshape(-1, 1),
        "qk_scale": np.concatenate([np.full((RH, 1), ROW, np.float32), np.ones((RH, 1), np.float32)]),
        "row_mask": (rows[:, None] == np.arange(P)[None, :] // ROW).astype(np.float32),
        "head_mask": (np.arange(C).reshape(KC, P).T[:, :, None] // (C // AH) == np.arange(GT * RH)[None, None, :] % AH).astype(np.float32),
        "w_v": g["L1_conv_Wv"].T, "b_v": g["L1_conv_bv"].reshape(KC, P).T, "w_o": g["L1_conv_Wo"].T, "b_o": g["L1_conv_bo"],
    }
    a = {k: np.ascontiguousarray(v) for k, v in a.items()}
    nc = bacc.Bacc("TRN2", target_bir_lowering=False, num_devices=1)
    d = {k: nc.dram_tensor("in_" + k, v.shape, mybir.dt.from_np(v.dtype), kind="ExternalInput").ap() for k, v in a.items()}
    out = nc.dram_tensor("out", (TILES * P, C), F32, kind="ExternalOutput").ap()
    metaformer(nc, d, out)
    r = run_bass_kernel_spmd(nc, [{"in_" + k: v for k, v in a.items()}], core_ids=[0])
    return r.results[0]["out"].reshape(BATCH, 32, 32, C)
```

```python
from contextlib import ExitStack

import concourse.bass as bass
from concourse import mybir

F32 = mybir.dt.float32
I32 = mybir.dt.int32
U32 = mybir.dt.uint32
ALU = mybir.AluOpType
ACT = mybir.ActivationFunctionType
AX = mybir.AxisListType

P = 128
C = 256
KC = C // P
BATCH = 8
SEQ = 1024
TPB = SEQ // P
TILES = BATCH * TPB

LAYERS = 2
DIN = 512
XM = DIN // P
HEADS = 8
HD = DIN // HEADS
NST = 64
TAPS = 4
OX, OB, OC, ODT = DIN, 2 * DIN, 2 * DIN + NST, 2 * DIN + 2 * NST
DPROJ = ODT + HEADS
STREAMS = 2
LN_C_EPS = 1e-6
LN_T_EPS = 1e-5
RMS_EPS = 1e-5
LN_MAX = 88.7


def row_on_all(vector, n):
    return vector.rearrange("(a n) -> a n", a=1).broadcast_to([P, n])


def counters(nc, ctx):
    taken = []
    ctx.callback(nc.all_engine_barrier)
    ctx.callback(lambda: nc.clear_and_free_semaphores(taken))

    def counter(name):
        taken.append(nc.alloc_semaphore(name))
        return taken[-1]

    return counter


def norm_as_they_come(nc, ctx, counter, name, X, mean, rstd, eps, tiles):
    stats = ctx.enter_context(nc.sbuf_tensor(f"{name}_stats", [P, tiles, 6], F32))
    mv = ctx.enter_context(nc.sbuf_tensor(f"{name}_mv", [P, tiles, 2], F32))
    var = ctx.enter_context(nc.sbuf_tensor(f"{name}_var", [P, tiles], F32))
    minus_half = ctx.enter_context(nc.sbuf_tensor(f"{name}_mh", [P, tiles], F32))
    begun, stats_ready, mv_ready, var_ready, rstd_ready, passed, passed_pool = (
        counter(f"{name}_{n}") for n in ("begun", "stats_ready", "mv_ready", "var_ready", "rstd_ready", "passed", "passed_pool"))

    def begin(dve):
        nc.vector.memset(minus_half[:, :], -0.5).then_inc(begun, 1)
        dve.sem_inc(rstd_ready, 1)

    def on_vector(dve, at, n):
        dve.sem_inc(passed, 1)
        for i in range(tiles):
            ins = nc.vector.bn_stats(stats[:, i, :], X[:, bass.ds(at + i, 1), :].rearrange("p a c -> p (a c)"))
        ins.then_inc(stats_ready, 1)
        dve.wait_ge(stats_ready, n)
        dve.sem_inc(passed, 1)
        for i in range(tiles):
            ins = nc.vector.bn_aggr(mv[:, i, :], stats[:, i, :])
        ins.then_inc(mv_ready, 1)
        dve.wait_ge(mv_ready, n)
        dve.wait_ge(rstd_ready, n)
        nc.vector.tensor_scalar(var[:, :], mv[:, :, 1], eps, None, ALU.add).then_inc(var_ready, 1)
        nc.vector.tensor_copy(mean[:, bass.ds(at, tiles)], mv[:, :, 0])

    def on_gpsimd(pool, at, n):
        pool.wait_ge(var_ready, n)
        pool.sem_inc(passed_pool, 1)
        nc.gpsimd.tensor_tensor(rstd[:, bass.ds(at, tiles)], var[:, :], minus_half[:, :], ALU.pow).then_inc(rstd_ready, 1)

    return begin, on_vector, on_gpsimd


def mamba_layers(nc, d, X, ident, mean_after, rstd_after):
    with ExitStack() as ctx:
        def sb(name, shape, dt=F32):
            return ctx.enter_context(nc.sbuf_tensor(name, shape, dt))

        def per_stream(name, shape):
            return [sb(f"{name}{s}", shape) for s in range(STREAMS)]

        counter = counters(nc, ctx)

        def sems(name):
            return [counter(f"{name}{s}") for s in range(STREAMS)]

        w_in = [sb(f"w_in{l}", [P, KC, DPROJ]) for l in range(LAYERS)]
        w_out = [sb(f"w_out{l}", [P, XM, C]) for l in range(LAYERS)]
        norm_w = sb("norm_w", [P, LAYERS, XM])
        cw = sb("cw", [P, LAYERS, XM, TAPS])
        cb = sb("cb", [P, LAYERS, XM])
        cw_bc = sb("cw_bc", [NST, LAYERS, 2, TAPS])
        cb_bc = sb("cb_bc", [NST, LAYERS, 2])
        dt_bias = sb("dt_bias", [HEADS, LAYERS])
        a_log = sb("a_log", [HEADS, LAYERS])
        a_neg = sb("a_neg", [HEADS, LAYERS])
        a_exp = sb("a_exp", [HEADS, LAYERS])
        d_half = sb("d_half", [P, LAYERS, HEADS])
        d_row = sb("d_row", [P, LAYERS, HEADS])
        head_row = sb("head_row", [HEADS, HEADS, P])
        last_row = sb("last_row", [P, NST])
        diag = sb("diag", [P, 4, P])
        zero_row = sb("zero_row", [HEADS, P])
        minus_half = sb("minus_half", [P, 1])

        stats = per_stream("stats", [P, 6])
        mv = per_stream("mv", [P, 2])
        var = per_stream("var", [P, 1])
        rstd = per_stream("rstd", [P, 1])
        r0 = per_stream("r0", [P, 1])
        h_in = per_stream("h_in", [P, C])
        hT = per_stream("hT", [P, KC, P])
        x_raw = [per_stream(f"x_raw{l}_", [P, XM, TAPS - 1 + P]) for l in range(LAYERS)]
        bc_raw = [per_stream(f"bc_raw{l}_", [NST, 2, TAPS - 1 + P]) for l in range(LAYERS)]
        state = [per_stream(f"state{l}_", [NST, DIN]) for l in range(LAYERS)]
        x_conv = per_stream("x_conv", [P, XM, P])
        x_tanh = per_stream("x_tanh", [P, XM, P])
        bc_conv = per_stream("bc_conv", [NST, 2, P])
        bc_tap = [[sb(f"bc_tap{s}_{k}", [NST, 2, P]) for k in range(TAPS - 1)] for s in range(STREAMS)]
        bc_tanh = per_stream("bc_tanh", [NST, 2, P])
        dt_raw = per_stream("dt_raw", [HEADS, P])
        cb_prod = per_stream("cb_prod", [P, P])
        dt_abs = per_stream("dt_abs", [HEADS, P])
        dt_exp = per_stream("dt_exp", [HEADS, P])
        dt_pos = per_stream("dt_pos", [HEADS, P])
        dt_log = per_stream("dt_log", [HEADS, P])
        dt = per_stream("dt", [HEADS, P])
        dt_a = per_stream("dt_a", [HEADS, P])
        decay = per_stream("decay", [HEADS, P])
        decay0 = per_stream("decay0", [HEADS, P])
        decay_prod = per_stream("decay_prod", [HEADS, P])
        b_tok = per_stream("b_tok", [P, NST])
        dt_tok = per_stream("dt_tok", [P, HEADS])
        prod_tok = per_stream("prod_tok", [P, HEADS])
        x_tok = per_stream("x_tok", [P, HEADS, HD])
        x_skip = per_stream("x_skip", [P, HEADS, HD])
        x_dt = per_stream("x_dt", [P, HEADS, HD])
        x_end = per_stream("x_end", [P, HEADS, HD])
        span = per_stream("span", [P, HEADS, P])
        mix = per_stream("mix", [P, HEADS, P])
        state_dec = per_stream("state_dec", [NST, HEADS, HD])
        y = per_stream("y", [P, HEADS, HD])
        z_tanh = per_stream("z_tanh", [P, DIN])
        z_gate = per_stream("z_gate", [P, DIN])
        y_sq = z_tanh
        ssq = per_stream("ssq", [P, 1])
        r = per_stream("r", [P, 1])
        yT = x_tanh

        bankA = [ctx.enter_context(nc.psum_tensor(f"bankA{s}", [P, 512], F32)) for s in range(STREAMS)]
        bankB = [ctx.enter_context(nc.psum_tensor(f"bankB{s}", [P, 512], F32)) for s in range(STREAMS)]
        bankC = [ctx.enter_context(nc.psum_tensor(f"bankC{s}", [P, 512], F32)) for s in range(STREAMS)]
        bankD = [ctx.enter_context(nc.psum_tensor(f"bankD{s}", [P, 512], F32)) for s in range(STREAMS)]

        loaded = counter("weights_loaded")
        prepared = counter("weights_prepared")
        x_first = counter("x_first")
        x_rest = counter("x_rest")
        a_bounded = counter("a_bounded")
        a_done = counter("a_done")
        passed_dve, passed_pe, passed_pool = (counter(f"passed_{e}") for e in ("dve", "pe", "pool"))
        carry_reset = sems("carry_reset")
        names = """stats_ready mv_ready var_ready rstd_ready h_ready h_turned hT_ready bc_proj dt_raw_ready x_proj bc_copied
            x_copied conv1 conv2 conv3 conv_done bconv0 bconv1 bconv2 bconv_done x_tanh_done bc_tanh_done x_act
            bc_act dt_abs_done dt_exp_done dt_pos_done dt_log_done dt_ready dt_a_ready decay_ready decay0_ready prod_ready
            spread_lo spread_hi x_turned small_turned tok_copied x_tok_copied skip_ready xdt_ready span_ready
            mix_ready xend_ready z_proj intra_done inter_done total_done state_dec_ready state_in state_out
            z_tanh_done z_gate_ready y1_ready y2_ready y3_ready y_ready ssq_ready r0_ready r_ready y_turned yT_ready out_done
            layer_done""".split()
        S = {n: sems(n) for n in names}

        statistics = [norm_as_they_come(nc, ctx, counter, f"ln1_{s}", X, mean_after, rstd_after, LN_T_EPS, 1) for s in range(STREAMS)]
        block = ctx.enter_context(nc.Block())

        def turns(t):
            return [LAYERS * t + 1 + l for l in range(LAYERS)]

        @block.sync
        def _(sp):
            xv = d["x"].rearrange("(i p) c -> p i c", p=P)

            def load_image(b, sem):
                sp.dma_start(X[:, b * TPB:(b + 1) * TPB, :], xv[:, b * TPB:(b + 1) * TPB, :]).then_inc(sem, 16)

            for s in range(STREAMS):
                load_image(s * (BATCH // STREAMS), x_first)
            for l in range(LAYERS):
                sp.dma_start(w_in[l][:, :, :], d["in_projT"][l].rearrange("(k p) n -> p k n", p=P)).then_inc(loaded, 16)
                sp.dma_start(w_out[l][:, :, :], d["out_projT"][l].rearrange("(m p) n -> p m n", p=P)).then_inc(loaded, 16)
                sp.dma_start(d_row[:, l, :], row_on_all(d["D"][l], HEADS)).then_inc(loaded, 16)
            for tile_, name in ((norm_w, "norm_w"), (cw, "conv_w"), (cb, "conv_b"), (cw_bc, "conv_w_bc"), (cb_bc, "conv_b_bc"),
                                (dt_bias, "dt_bias"), (a_log, "A_log"), (ident, "ident")):
                sp.dma_start(tile_[:], d[name]).then_inc(loaded, 16)
            for g in range(4):
                sp.dma_start(diag[:, g, :], d["ident"]).then_inc(loaded, 16)
            sp.dma_start(head_row[:, :, :], d["head_row"].rearrange("k (h p) -> k h p", h=HEADS)).then_inc(loaded, 16)
            sp.dma_start(last_row[:, :], d["last_row"]).then_inc(loaded, 16)
            for b in range(1, BATCH // STREAMS):
                for s in range(STREAMS):
                    load_image(b + s * (BATCH // STREAMS), x_rest)

        N_LOADED = 16 * (3 * LAYERS + 14)

        @block.tensor
        def _(pe):
            pe.wait_ge(prepared, 1)
            with pe.Fori(0, TILES // STREAMS) as t:
                for l, n in enumerate(turns(t)):
                    for s in range(STREAMS):
                        pe.wait_ge(S["h_ready"][s], n)
                        pe.wait_ge(S["layer_done"][s], n)
                        for k in range(KC):
                            mm = nc.tensor.transpose(bankA[s][:, k * P:(k + 1) * P], h_in[s][:, k * P:(k + 1) * P], ident[:, :])
                        mm.then_inc(S["h_turned"][s], 1)
                    for s in range(STREAMS):
                        pe.wait_ge(S["hT_ready"][s], n)
                        for out, o, m in ((bankC[s][0:HEADS, 256:384], ODT, HEADS), (bankC[s][0:NST, 0:P], OB, NST),
                                          (bankC[s][0:NST, P:2 * P], OC, NST)):
                            for k in range(KC):
                                mm = nc.tensor.matmul(out, w_in[l][:, k, o:o + m], hT[s][:, k, :], start=(k == 0), stop=(k == KC - 1))
                        mm.then_inc(S["bc_proj"][s], 1)
                    for s in range(STREAMS):
                        for m in range(XM):
                            for k in range(KC):
                                mm = nc.tensor.matmul(bankB[s][:, m * P:(m + 1) * P], w_in[l][:, k, OX + m * P:OX + (m + 1) * P],
                                                      hT[s][:, k, :], start=(k == 0), stop=(k == KC - 1))
                        mm.then_inc(S["x_proj"][s], 1)
                    for s in range(STREAMS):
                        for k in range(KC):
                            mm = nc.tensor.matmul(bankD[s][:, :], hT[s][:, k, :], w_in[l][:, k, 0:DIN], start=(k == 0), stop=(k == KC - 1))
                        mm.then_inc(S["z_proj"][s], 1)
                    for s in range(STREAMS):
                        pe.wait_ge(S["decay0_ready"][s], n)
                        pe.wait_ge(S["x_copied"][s], n)
                        for h in range(HEADS):
                            bank = (bankA if h < 4 else bankB)[s]
                            mm = nc.tensor.matmul(bank[:, h % 4 * P:(h % 4 + 1) * P], head_row[:, h, :], decay0[s][:, :], start=True, stop=True)
                            if h == 3:
                                mm.then_inc(S["spread_lo"][s], 1)
                        mm.then_inc(S["spread_hi"][s], 1)

                    def turn_small(s):
                        pe.wait_ge(S["bc_act"][s], n)
                        nc.tensor.matmul(bankC[s][:, P:2 * P], bc_conv[s][:, 0, :], bc_conv[s][:, 1, :], start=True, stop=True)
                        nc.tensor.transpose(bankC[s][:, 0:NST], bc_conv[s][:, 0, :], ident[0:NST, 0:NST])
                        nc.tensor.transpose(bankC[s][:, 400:408], dt[s][:, :], ident[0:HEADS, 0:HEADS])
                        pe.wait_ge(S["prod_ready"][s], n)
                        pe.sem_inc(passed_pe, 1)
                        nc.tensor.transpose(bankC[s][:, 408:416], decay_prod[s][:, :], ident[0:HEADS, 0:HEADS]).then_inc(S["small_turned"][s], 1)

                    def turn_x(s):
                        pe.wait_ge(S["x_act"][s], n)
                        for m in range(XM):
                            mm = nc.tensor.transpose(bankB[s][:, m * P:(m + 1) * P], x_conv[s][:, m, :], ident[:, :])
                        mm.then_inc(S["x_turned"][s], 1)
                        pe.wait_ge(S["tok_copied"][s], n)
                        nc.tensor.matmul(bankC[s][0:NST, 420:428], last_row[:, :], prod_tok[s][:, :], start=True, stop=True)\
                            .then_inc(S["total_done"][s], 1)

                    def from_state(s):
                        pe.wait_ge(S["x_tok_copied"][s], n)
                        nc.tensor.matmul(bankB[s][:, :], bc_conv[s][:, 1, :], state[l][s][:, :], start=True, stop=True)\
                            .then_inc(S["inter_done"][s], 1)

                    def from_chunk(s):
                        pe.wait_ge(S["span_ready"][s], n)
                        pe.wait_ge(S["mix_ready"][s], n)
                        pe.wait_ge(S["xdt_ready"][s], n)
                        for h in range(HEADS):
                            mm = nc.tensor.matmul(bankA[s][:, h * HD:(h + 1) * HD], mix[s][:, h, :], x_dt[s][:, h, :], start=True, stop=True)
                        mm.then_inc(S["intra_done"][s], 1)

                    def to_state(s):
                        pe.wait_ge(S["xend_ready"][s], n)
                        pe.wait_ge(S["state_dec_ready"][s], n)
                        nc.tensor.matmul(bankC[s][0:NST, :], b_tok[s][:, :], x_end[s][:, :, :].rearrange("p h e -> p (h e)"),
                                         start=True, stop=True).then_inc(S["state_in"][s], 1)

                    turn_small(0)
                    turn_x(0)
                    from_state(0)
                    from_chunk(0)
                    turn_small(1)
                    turn_x(1)
                    to_state(0)
                    from_state(1)
                    from_chunk(1)
                    to_state(1)
                    for s in range(STREAMS):
                        pe.wait_ge(S["y_ready"][s], n)
                        for m in range(XM):
                            mm = nc.tensor.transpose(bankB[s][:, m * P:(m + 1) * P],
                                                     y[s][:, 2 * m:2 * m + 2, :].rearrange("p h e -> p (h e)"), ident[:, :])
                        mm.then_inc(S["y_turned"][s], 1)
                    for s in range(STREAMS):
                        pe.wait_ge(S["yT_ready"][s], n)
                        for m in range(XM):
                            mm = nc.tensor.matmul(bankA[s][:, 0:C], yT[s][:, m, :], w_out[l][:, m, :], start=(m == 0), stop=(m == XM - 1))
                        mm.then_inc(S["out_done"][s], 1)

        @block.scalar
        def _(act):
            act.wait_ge(a_bounded, 1)
            nc.scalar.activation(a_exp[:, :], a_log[:, :], ACT.Exp).then_inc(a_done, 1)
            act.wait_ge(prepared, 1)
            with act.Fori(0, TILES // STREAMS) as t:
                for l, n in enumerate(turns(t)):
                    for s in range(STREAMS):
                        act.wait_ge(S["h_turned"][s], n)
                        nc.scalar.copy(hT[s][:, :, :].rearrange("p k t -> p (k t)"), bankA[s][:, 0:C]).then_inc(S["hT_ready"][s], 1)
                    for s in range(STREAMS):
                        act.wait_ge(S["bc_proj"][s], n)
                        nc.scalar.activation(dt_raw[s][:, :], bankC[s][0:HEADS, 256:384], ACT.Identity, bias=dt_bias[:, l:l + 1])\
                            .then_inc(S["dt_raw_ready"][s], 1)
                        nc.scalar.copy(bc_raw[l][s][:, :, TAPS - 1:], bankC[s][0:NST, 0:2 * P].rearrange("p (m t) -> p m t", m=2))\
                            .then_inc(S["bc_copied"][s], 1)
                        act.wait_ge(S["dt_raw_ready"][s], n)
                        nc.scalar.activation(dt_abs[s][:, :], dt_raw[s][:, :], ACT.Abs).then_inc(S["dt_abs_done"][s], 1)
                        act.wait_ge(S["dt_abs_done"][s], n)
                        nc.scalar.activation(dt_exp[s][:, :], dt_abs[s][:, :], ACT.Exp, scale=-1.0).then_inc(S["dt_exp_done"][s], 1)
                    for s in range(STREAMS):
                        act.wait_ge(S["dt_exp_done"][s], n)
                        nc.scalar.activation(dt_log[s][:, :], dt_exp[s][:, :], ACT.Ln, bias=1.0).then_inc(S["dt_log_done"][s], 1)
                    for s in range(STREAMS):
                        act.wait_ge(S["x_proj"][s], n)
                        nc.scalar.copy(x_raw[l][s][:, :, TAPS - 1:], bankB[s][:, :].rearrange("p (m t) -> p m t", m=XM))\
                            .then_inc(S["x_copied"][s], 1)
                        act.wait_ge(S["dt_a_ready"][s], n)
                        nc.scalar.activation(decay[s][:, :], dt_a[s][:, :], ACT.Exp).then_inc(S["decay_ready"][s], 1)
                    act.wait_ge(S["x_copied"][1], n)
                    for m in range(XM):
                        ins = nc.scalar.activation(x_conv[1][:, m, :], x_raw[l][1][:, m, 0:P], ACT.Identity, scale=cw[:, l, m, 0:1],
                                                   bias=cb[:, l, m:m + 1])
                    ins.then_inc(S["conv1"][1], 1)
                    for s in range(STREAMS):
                        act.wait_ge(S["z_proj"][s], n)
                        nc.scalar.activation(z_tanh[s][:, :], bankD[s][:, :], ACT.Tanh, scale=0.5).then_inc(S["z_tanh_done"][s], 1)

                    def tanh_bc(s):
                        act.wait_ge(S["bconv_done"][s], n)
                        nc.scalar.activation(bc_tanh[s][:, :, :], bc_conv[s][:, :, :], ACT.Tanh, scale=0.5).then_inc(S["bc_tanh_done"][s], 1)

                    def tanh_x(s):
                        act.wait_ge(S["conv_done"][s], n)
                        nc.scalar.activation(x_tanh[s][:, :, :], x_conv[s][:, :, :], ACT.Tanh, scale=0.5).then_inc(S["x_tanh_done"][s], 1)

                    def copy_small(s):
                        act.wait_ge(S["small_turned"][s], n)
                        nc.scalar.copy(cb_prod[s][:, :], bankC[s][:, P:2 * P])
                        nc.scalar.copy(b_tok[s][:, :], bankC[s][:, 0:NST])
                        nc.scalar.copy(prod_tok[s][:, :], bankC[s][:, 408:416])
                        nc.scalar.mul(dt_tok[s][:, :], bankC[s][:, 400:408], 0.125).then_inc(S["tok_copied"][s], 1)

                    def copy_x(s):
                        act.wait_ge(S["x_turned"][s], n)
                        nc.scalar.copy(x_tok[s][:, :, :].rearrange("p h e -> p (h e)"), bankB[s][:, :]).then_inc(S["x_tok_copied"][s], 1)

                    tanh_bc(0)
                    tanh_x(0)
                    copy_small(0)
                    tanh_bc(1)
                    copy_x(0)
                    tanh_x(1)
                    copy_small(1)
                    copy_x(1)
                    for s in range(STREAMS):
                        act.wait_ge(S["y_ready"][s], n)
                        nc.scalar.activation(y_sq[s][:, :], y[s][:, :, :].rearrange("p h e -> p (h e)"), ACT.Square, accum_out=ssq[s][:, :])\
                            .then_inc(S["ssq_ready"][s], 1)
                        act.wait_ge(S["y_turned"][s], n)
                        nc.scalar.copy(yT[s][:, :, :].rearrange("p m t -> p (m t)"), bankB[s][:, :]).then_inc(S["yT_ready"][s], 1)
                    if l + 1 < LAYERS:
                        for s in range(STREAMS):
                            act.wait_ge(S["out_done"][s], n)
                            act.wait_ge(S["r_ready"][s], n)
                            nc.scalar.mul(h_in[s][:, :], bankA[s][:, 0:C], r[s][:, 0:1]).then_inc(S["h_ready"][s], 1)

        @block.gpsimd
        def _(pool):
            def root(n):
                for s in range(STREAMS):
                    pool.wait_ge(S["var_ready"][s], n)
                    nc.gpsimd.tensor_tensor(rstd[s][:, :], var[s][:, :], minus_half[:, :], ALU.pow).then_inc(S["rstd_ready"][s], 1)

            pool.wait_ge(prepared, 1)
            root(1)
            with pool.Fori(0, BATCH // STREAMS) as b:
                for s in range(STREAMS):
                    pool.wait_ge(S["layer_done"][s], b * (TPB * LAYERS) + 1)
                    pool.sem_inc(passed_pool, 1)
                    for l in range(LAYERS):
                        nc.gpsimd.memset(bc_raw[l][s][:, :, 0:TAPS - 1], 0.0).then_inc(carry_reset[s], 1)
                with pool.Fori(0, TPB) as c:
                    for l, n in enumerate(turns(b * TPB + c)):
                        for s in range(STREAMS):
                            pool.wait_ge(carry_reset[s], LAYERS * b + LAYERS)
                            pool.wait_ge(S["bc_copied"][s], n)
                            pool.sem_inc(passed_pool, 1)
                            for k in range(TAPS):
                                for m in range(2):
                                    tap = bc_raw[l][s][:, m, k:k + P]
                                    out = bc_conv[s] if k == 0 else bc_tap[s][k - 1]
                                    ins = nc.gpsimd.tensor_scalar(out[:, m, :], tap, cw_bc[:, l, m, k:k + 1],
                                                                  cb_bc[:, l, m:m + 1] if k == 0 else 0.0, ALU.mult, ALU.add)
                            ins.then_inc(S["bconv0"][s], 1)
                            for k, (before, after) in enumerate((("bconv0", "bconv1"), ("bconv1", "bconv2"), ("bconv2", "bconv_done"))):
                                pool.wait_ge(S[before][s], n)
                                nc.gpsimd.tensor_tensor(bc_conv[s][:, :, :], bc_conv[s][:, :, :], bc_tap[s][k][:, :, :], ALU.add)\
                                    .then_inc(S[after][s], 1)
                            nc.gpsimd.tensor_copy(bc_raw[l][s][:, :, 0:TAPS - 1], bc_raw[l][s][:, :, P:])
                        for s in range(STREAMS):
                            pool.wait_ge(S["x_tok_copied"][s], n)
                            nc.gpsimd.tensor_tensor(x_skip[s][:, :, :], x_tok[s][:, :, :],
                                                    d_half[:, l, :].unsqueeze(2).broadcast_to([P, HEADS, HD]), ALU.mult)\
                                .then_inc(S["skip_ready"][s], 1)
                            pool.wait_ge(S["xdt_ready"][s], n)
                            nc.gpsimd.tensor_tensor(x_end[s][:, :, :], x_dt[s][:, :, :],
                                                    span[s][:, :, P - 1:P].broadcast_to([P, HEADS, HD]), ALU.mult)\
                                .then_inc(S["xend_ready"][s], 1)
                            pool.wait_ge(S["skip_ready"][s], n)
                            pool.wait_ge(S["y1_ready"][s], n)
                            nc.gpsimd.tensor_tensor(x_skip[s][:, :, :], x_skip[s][:, :, :], y[s][:, :, :], ALU.add)\
                                .then_inc(S["y2_ready"][s], 1)
                        for s in range(STREAMS):
                            pool.wait_ge(S["r0_ready"][s], n)
                            nc.gpsimd.tensor_tensor(r[s][:, :], r0[s][:, :], minus_half[:, :], ALU.pow).then_inc(S["r_ready"][s], 1)
                        if l + 1 == LAYERS:
                            root(b * TPB + c + 2)
                            for s in range(STREAMS):
                                statistics[s][2](pool, b * TPB + c + s * (TILES // STREAMS), b * TPB + c + 1)

        @block.vector
        def _(dve):
            dve.wait_ge(loaded, N_LOADED)
            nc.vector.tensor_scalar(a_log[:, :], a_log[:, :], LN_MAX, None, ALU.min).then_inc(a_bounded, 1)
            for l in range(LAYERS):
                for m in range(XM):
                    nc.vector.tensor_scalar(w_out[l][:, m, :], w_out[l][:, m, :], norm_w[:, l, m:m + 1], None, ALU.mult)
            nc.vector.tensor_scalar(d_half[:, :, :], d_row[:, :, :], 0.5, None, ALU.mult)
            nc.vector.memset(zero_row[:, :], 0.0)
            nc.vector.memset(minus_half[:, :], -0.5)
            for s in range(STREAMS):
                nc.vector.memset(decay0[s][:, 0:1], 0.0)
            dve.wait_ge(a_done, 1)
            nc.vector.tensor_scalar(a_neg[:, :], a_exp[:, :], -1.0, None, ALU.mult).then_inc(prepared, 1)
            for s in range(STREAMS):
                nc.vector.memset(ssq[s][:, :], 0.0).then_inc(S["layer_done"][s], 1)

            dve.wait_ge(x_first, 16 * STREAMS)

            def normalise(t, n):
                for s in range(STREAMS):
                    xt = X[:, bass.ds(t + s * (TILES // STREAMS), 1), :].rearrange("p a c -> p (a c)")
                    nc.vector.bn_stats(stats[s][:, :], xt).then_inc(S["stats_ready"][s], 1)
                    dve.wait_ge(S["stats_ready"][s], n)
                    dve.sem_inc(passed_dve, 1)
                    nc.vector.bn_aggr(mv[s][:, :], stats[s][:, :]).then_inc(S["mv_ready"][s], 1)
                    dve.wait_ge(S["mv_ready"][s], n)
                    nc.vector.tensor_scalar(var[s][:, :], mv[s][:, 1:2], LN_C_EPS, None, ALU.add).then_inc(S["var_ready"][s], 1)
                for s in range(STREAMS):
                    xt = X[:, bass.ds(t + s * (TILES // STREAMS), 1), :].rearrange("p a c -> p (a c)")
                    dve.wait_ge(S["rstd_ready"][s], n)
                    nc.vector.tensor_scalar(h_in[s][:, :], xt, mv[s][:, 0:1], rstd[s][:, 0:1], ALU.subtract, ALU.mult)\
                        .then_inc(S["h_ready"][s], 1)

            for s in range(STREAMS):
                statistics[s][0](dve)
            normalise(0, 1)
            with dve.Fori(0, BATCH // STREAMS) as b:
                for s in range(STREAMS):
                    for l in range(LAYERS):
                        nc.vector.memset(state[l][s][:, :], 0.0)
                        nc.vector.memset(x_raw[l][s][:, :, 0:TAPS - 1], 0.0)
                with dve.Fori(0, TPB) as c:
                    t = b * TPB + c
                    for l, n in enumerate(turns(t)):
                        for s in range(STREAMS):
                            dve.wait_ge(S["dt_raw_ready"][s], n)
                            nc.vector.tensor_scalar(dt_pos[s][:, :], dt_raw[s][:, :], 0.0, None, ALU.max)\
                                .then_inc(S["dt_pos_done"][s], 1)
                        for s in range(STREAMS):
                            dve.wait_ge(S["dt_log_done"][s], n)
                            dve.wait_ge(S["dt_pos_done"][s], n)
                            nc.vector.tensor_tensor(dt[s][:, :], dt_pos[s][:, :], dt_log[s][:, :], ALU.add).then_inc(S["dt_ready"][s], 1)
                        for s in range(STREAMS):
                            dve.wait_ge(S["dt_ready"][s], n)
                            nc.vector.tensor_scalar(dt_a[s][:, :], dt[s][:, :], a_neg[:, l:l + 1], -110.0, ALU.mult, ALU.max)\
                                .then_inc(S["dt_a_ready"][s], 1)

                        def conv_first(s):
                            dve.wait_ge(S["x_copied"][s], n)
                            for m in range(XM):
                                ins = nc.vector.tensor_scalar(x_conv[s][:, m, :], x_raw[l][s][:, m, 0:P], cw[:, l, m, 0:1], cb[:, l, m:m + 1],
                                                              ALU.mult, ALU.add)
                            ins.then_inc(S["conv1"][s], 1)

                        def conv_tap(s, k):
                            before, after = (("conv1", "conv2"), ("conv2", "conv3"), ("conv3", "conv_done"))[k - 1]
                            dve.wait_ge(S[before][s], n)
                            for m in range(XM):
                                ins = nc.vector.scalar_tensor_tensor(out=x_conv[s][:, m, :], in0=x_raw[l][s][:, m, k:k + P],
                                                                     scalar=cw[:, l, m, k:k + 1], in1=x_conv[s][:, m, :],
                                                                     op0=ALU.mult, op1=ALU.add)
                            ins.then_inc(S[after][s], 1)

                        def decays(s):
                            dve.wait_ge(S["decay_ready"][s], n)
                            nc.vector.tensor_copy(decay0[s][:, 1:P], decay[s][:, 1:P]).then_inc(S["decay0_ready"][s], 1)
                            nc.vector.tensor_tensor_scan(decay_prod[s][:, :], decay[s][:, :], zero_row[:, :], 1.0, ALU.mult, ALU.add)\
                                .then_inc(S["prod_ready"][s], 1)

                        def activate_bc(s):
                            dve.wait_ge(S["bc_tanh_done"][s], n)
                            nc.vector.scalar_tensor_tensor(out=bc_conv[s][:, :, :], in0=bc_tanh[s][:, :, :], scalar=1.0, in1=bc_conv[s][:, :, :],
                                                           op0=ALU.add, op1=ALU.mult).then_inc(S["bc_act"][s], 1)

                        def activate_x(s):
                            nc.vector.tensor_copy(x_raw[l][s][:, :, 0:TAPS - 1], x_raw[l][s][:, :, P:])
                            flat = span[s][:, :, :].rearrange("p h t -> p (h t)")
                            d4 = diag[:, :, :].rearrange("p g t -> p (g t)")
                            dve.wait_ge(S["spread_lo"][s], n)
                            nc.vector.tensor_tensor_scan(flat[:, 0:512], bankA[s][:, :], d4, 0.0, ALU.mult, ALU.add)
                            dve.wait_ge(S["spread_hi"][s], n)
                            nc.vector.tensor_tensor_scan(flat[:, 512:1024], bankB[s][:, :], d4, 0.0, ALU.mult, ALU.add)\
                                .then_inc(S["span_ready"][s], 1)
                            dve.wait_ge(S["x_tanh_done"][s], n)
                            nc.vector.scalar_tensor_tensor(out=x_conv[s][:, :, :], in0=x_tanh[s][:, :, :], scalar=1.0, in1=x_conv[s][:, :, :],
                                                           op0=ALU.add, op1=ALU.mult).then_inc(S["x_act"][s], 1)

                        def weigh(s):
                            dve.wait_ge(S["tok_copied"][s], n)
                            dve.wait_ge(S["span_ready"][s], n)
                            nc.vector.tensor_tensor(mix[s][:, :, :], span[s][:, :, :],
                                                    cb_prod[s][:, :].unsqueeze(1).broadcast_to([P, HEADS, P]), ALU.mult)\
                                .then_inc(S["mix_ready"][s], 1)
                            dve.wait_ge(S["x_tok_copied"][s], n)
                            nc.vector.tensor_tensor(x_dt[s][:, :, :], x_tok[s][:, :, :],
                                                    dt_tok[s][:, :].unsqueeze(2).broadcast_to([P, HEADS, HD]), ALU.mult)\
                                .then_inc(S["xdt_ready"][s], 1)
                            dve.wait_ge(S["total_done"][s], n)
                            nc.vector.tensor_tensor(state_dec[s][:, :, :], state[l][s][:, :].rearrange("p (h e) -> p h e", h=HEADS),
                                                    bankC[s][0:NST, 420:428].unsqueeze(2).broadcast_to([NST, HEADS, HD]), ALU.mult)\
                                .then_inc(S["state_dec_ready"][s], 1)

                        def gate_z(s):
                            dve.wait_ge(S["z_tanh_done"][s], n)
                            nc.vector.scalar_tensor_tensor(out=z_gate[s][:, :], in0=z_tanh[s][:, :], scalar=1.0, in1=bankD[s][:, :],
                                                           op0=ALU.add, op1=ALU.mult).then_inc(S["z_gate_ready"][s], 1)

                        def decay_inter(s):
                            dve.wait_ge(S["inter_done"][s], n)
                            nc.vector.tensor_tensor(y[s][:, :, :], bankB[s][:, :].rearrange("p (h e) -> p h e", h=HEADS),
                                                    prod_tok[s][:, :].unsqueeze(2).broadcast_to([P, HEADS, HD]), ALU.mult)\
                                .then_inc(S["y1_ready"][s], 1)

                        def finish(s):
                            yf = y[s][:, :, :].rearrange("p h e -> p (h e)")
                            dve.wait_ge(S["y2_ready"][s], n)
                            dve.wait_ge(S["intra_done"][s], n)
                            nc.vector.tensor_tensor(yf, bankA[s][:, :], x_skip[s][:, :, :].rearrange("p h e -> p (h e)"), ALU.add)\
                                .then_inc(S["y3_ready"][s], 1)
                            dve.wait_ge(S["y3_ready"][s], n)
                            dve.wait_ge(S["z_gate_ready"][s], n)
                            nc.vector.tensor_tensor(yf, yf, z_gate[s][:, :], ALU.mult).then_inc(S["y_ready"][s], 1)

                        def new_state(s):
                            dve.wait_ge(S["state_in"][s], n)
                            dve.wait_ge(S["state_dec_ready"][s], n)
                            nc.vector.tensor_tensor(state[l][s][:, :], bankC[s][0:NST, :],
                                                    state_dec[s][:, :, :].rearrange("p h e -> p (h e)"), ALU.add).then_inc(S["state_out"][s], 1)

                        conv_first(0)
                        conv_tap(0, 1)
                        decays(0)
                        decays(1)
                        conv_tap(0, 2)
                        conv_tap(0, 3)
                        activate_bc(0)
                        activate_x(0)
                        conv_tap(1, 1)
                        weigh(0)
                        conv_tap(1, 2)
                        conv_tap(1, 3)
                        activate_bc(1)
                        activate_x(1)
                        gate_z(0)
                        decay_inter(0)
                        gate_z(1)
                        weigh(1)
                        finish(0)
                        decay_inter(1)
                        new_state(0)
                        finish(1)
                        new_state(1)
                        for s in range(STREAMS):
                            dve.wait_ge(S["ssq_ready"][s], n)
                            nc.vector.tensor_scalar(r0[s][:, :], ssq[s][:, :], 1.0 / DIN, 4 * RMS_EPS, ALU.mult, ALU.add)\
                                .then_inc(S["r0_ready"][s], 1)
                        if l + 1 < LAYERS:
                            for s in range(STREAMS):
                                dve.wait_ge(S["state_out"][s], n)
                                dve.wait_ge(S["out_done"][s], n)
                                dve.sem_inc(S["layer_done"][s], 1)
                        else:
                            dve.wait_ge(x_rest, 16 * (BATCH - STREAMS))
                            normalise((t + 1) & (TILES // STREAMS - 1), t + 2)
                            for s in range(STREAMS):
                                dve.wait_ge(S["out_done"][s], n)
                                dve.wait_ge(S["r_ready"][s], n)
                                dve.wait_ge(S["state_out"][s], n)
                                xt = X[:, bass.ds(t + s * (TILES // STREAMS), 1), :].rearrange("p a c -> p (a c)")
                                nc.vector.scalar_tensor_tensor(out=xt, in0=bankA[s][:, 0:C], scalar=r[s][:, 0:1], in1=xt,
                                                               op0=ALU.mult, op1=ALU.add).then_inc(S["layer_done"][s], 1)
                            for s in range(STREAMS):
                                dve.wait_ge(S["layer_done"][s], n + 1)
                                statistics[s][1](dve, t + s * (TILES // STREAMS), t + 1)


F = 512
FM = F // P
EXP0 = 8
TOPK = 2
CAPACITY = 1280.0
HALF = SEQ // 2
TPH = HALF // P
NORM_DONE = BATCH // 2


def norm_parts(nc, ctx, counter, name, X, mean, rstd, eps):
    stats = ctx.enter_context(nc.sbuf_tensor(f"{name}_stats", [P, 2, TPB, 6], F32))
    mv = ctx.enter_context(nc.sbuf_tensor(f"{name}_mv", [P, 2, TPB, 2], F32))
    var = ctx.enter_context(nc.sbuf_tensor(f"{name}_var", [P, TILES], F32))
    minus_half = ctx.enter_context(nc.sbuf_tensor(f"{name}_mh", [P, 2 * TPB], F32))
    stats_ready, mv_ready, var_ready, rstd_ready, passed, passed_pool = (
        counter(f"{name}_{n}") for n in ("stats_ready", "mv_ready", "var_ready", "rstd_ready", "passed", "passed_pool"))

    def on_vector(dve):
        nc.vector.memset(minus_half[:, :], -0.5)
        with dve.Fori(0, NORM_DONE) as b:
            for u in range(2):
                for i in range(TPB):
                    xt = X[:, bass.ds(b * (2 * TPB) + (u * TPB + i), 1), :].rearrange("p a c -> p (a c)")
                    ins = nc.vector.bn_stats(stats[:, u, i, :], xt)
                ins.then_inc(stats_ready, 1)
                dve.wait_ge(stats_ready, 2 * b + u + 1)
                dve.sem_inc(passed, 1)
                for i in range(TPB):
                    ins = nc.vector.bn_aggr(mv[:, u, i, :], stats[:, u, i, :])
                ins.then_inc(mv_ready, 1)
                dve.wait_ge(mv_ready, 2 * b + u + 1)
                at = bass.ds(b * (2 * TPB) + u * TPB, TPB)
                nc.vector.tensor_copy(mean[:, at], mv[:, u, :, 0])
                nc.vector.tensor_scalar(var[:, at], mv[:, u, :, 1], eps, None, ALU.add).then_inc(var_ready, 1)

    def on_gpsimd(pool):
        with pool.Fori(0, NORM_DONE) as b:
            pool.wait_ge(var_ready, 2 * b + 2)
            pool.sem_inc(passed_pool, 1)
            at = bass.ds(b * (2 * TPB), 2 * TPB)
            nc.gpsimd.tensor_tensor(rstd[:, at], var[:, at], minus_half[:, :], ALU.pow).then_inc(rstd_ready, 1)

    return on_vector, on_gpsimd, rstd_ready


def route_images(nc, d, X, ident, mean, rstd, picked, weight):
    with ExitStack() as ctx:
        counter = counters(nc, ctx)
        sb = lambda n, s, dt=F32: ctx.enter_context(nc.sbuf_tensor(n, s, dt))
        sem = lambda n: counter(n)
        tok = [sb(f"rt_tok{u}", [P, C]) for u in range(4)]
        image_row = sb("rt_image_row", [P, BATCH, BATCH])
        w_r = sb("rt_w", [P, KC, EXP0])
        b_r = sb("rt_b", [BATCH, EXP0])
        ones = sb("rt_ones", [BATCH, BATCH])
        token_mean = sb("rt_mean", [BATCH, C])
        token_meanT = sb("rt_meanT", [P, KC, BATCH])
        logits = sb("rt_logits", [BATCH, EXP0])
        top = sb("rt_top", [BATCH, 1])
        low = sb("rt_low", [BATCH, EXP0])
        total = sb("rt_total", [BATCH, 1])
        inv = sb("rt_inv", [BATCH, 1])
        rw = sb("rt_rw", [BATCH, EXP0])
        load_ = sb("rt_load", [BATCH, EXP0])
        best = sb("rt_best", [BATCH, EXP0])
        best_at = sb("rt_best_at", [BATCH, EXP0], U32)
        pair = sb("rt_pair", [BATCH, TOPK])
        psum_mean = ctx.enter_context(nc.psum_tensor("rt_pm", [P, 512], F32))
        psum_small = ctx.enter_context(nc.psum_tensor("rt_ps", [P, 512], F32))
        at_dram = nc.dram_tensor("rt_at_dram", (BATCH * TOPK,), U32, kind="Internal").ap()
        w_dram = nc.dram_tensor("rt_w_dram", (BATCH * TOPK,), F32, kind="Internal").ap()
        loaded, tok_ready, mean_done, mean_copied, turned, turned_copied, logits_done = (
            sem(n) for n in ("rt_loaded", "rt_tok_ready", "rt_mean_done", "rt_mean_copied", "rt_turned", "rt_turned_copied", "rt_logits_done"))
        step, exp_done, load_done, routed, stored, spread, tok_free = (
            sem(n) for n in ("rt_step", "rt_exp_done", "rt_load_done", "rt_routed", "rt_stored", "rt_spread", "rt_tok_free"))
        block = ctx.enter_context(nc.Block())

        @block.sync
        def _(sp):
            sp.dma_start(image_row[:, :, :], d["image_row"].rearrange("p (b j) -> p b j", b=BATCH)).then_inc(loaded, 16)
            sp.dma_start(w_r[:, :, :], d["Wr"].rearrange("(k p) e -> p k e", p=P)).then_inc(loaded, 16)
            sp.dma_start(b_r[:, :], d["br"].rearrange("(a n) -> a n", a=1).broadcast_to([BATCH, EXP0])).then_inc(loaded, 16)
            sp.wait_ge(routed, 1)
            sp.dma_start(at_dram.rearrange("(b k) -> b k", k=TOPK), best_at[:, 0:TOPK]).then_inc(stored, 16)
            sp.dma_start(w_dram.rearrange("(b k) -> b k", k=TOPK), pair[:, :]).then_inc(stored, 16)
            sp.wait_ge(stored, 32)
            sp.dma_start(picked[:, :], at_dram.rearrange("(a n) -> a n", a=1)).then_inc(spread, 16)
            sp.dma_start(weight[:, :], row_on_all(w_dram, BATCH * TOPK)).then_inc(spread, 16)
            sp.wait_ge(spread, 32)

        @block.tensor
        def _(pe):
            pe.wait_ge(loaded, 48)
            for i in range(TILES):
                pe.wait_ge(tok_ready, i + 1)
                nc.tensor.matmul(psum_mean[0:BATCH, 0:C], image_row[:, i // TPB, :], tok[i % 4][:, :], start=(i == 0), stop=(i == TILES - 1))\
                    .then_inc(tok_free, 1)
            pe.wait_ge(mean_copied, 1)
            for k in range(KC):
                mm = nc.tensor.transpose(psum_small[:, k * BATCH:(k + 1) * BATCH], token_mean[:, k * P:(k + 1) * P], ident[0:BATCH, 0:BATCH])
            mm.then_inc(turned, 1)
            pe.wait_ge(turned_copied, 1)
            for k in range(KC):
                mm = nc.tensor.matmul(psum_small[0:BATCH, 32:32 + EXP0], token_meanT[:, k, :], w_r[:, k, :], start=(k == 0), stop=(k == KC - 1))
            mm.then_inc(logits_done, 1)
            pe.wait_ge(exp_done, 2)
            nc.tensor.matmul(psum_small[0:BATCH, 64:64 + EXP0], ones[:, :], rw[:, :], start=True, stop=True).then_inc(load_done, 1)

        @block.scalar
        def _(act):
            act.wait_ge(step, 3)
            nc.scalar.activation(rw[:, :], low[:, :], ACT.Exp, accum_out=total[:, :]).then_inc(exp_done, 1)
            act.wait_ge(step, 10)
            nc.scalar.activation(rw[:, :], low[:, :], ACT.Exp, accum_out=total[:, :]).then_inc(exp_done, 1)
            act.wait_ge(step, 14)
            nc.scalar.activation(pair[:, 1:2], low[:, 0:1], ACT.Exp).then_inc(exp_done, 1)

        @block.vector
        def _(dve):
            count = [0]

            def then(ins):
                count[0] += 1
                ins.then_inc(step, 1)
                dve.wait_ge(step, count[0])

            nc.vector.memset(ones[:, :], 1.0)
            for i in range(TILES):
                if i >= 4:
                    dve.wait_ge(tok_free, i - 3)
                nc.vector.tensor_scalar(tok[i % 4][:, :], X[:, i, :], mean[:, i:i + 1], rstd[:, i:i + 1], ALU.subtract, ALU.mult)\
                    .then_inc(tok_ready, 1)
            dve.wait_ge(tok_free, TILES)
            nc.vector.tensor_copy(token_mean[:, :], psum_mean[0:BATCH, 0:C]).then_inc(mean_copied, 1)
            dve.wait_ge(turned, 1)
            nc.vector.tensor_copy(token_meanT[:, :, :].rearrange("p k b -> p (k b)"), psum_small[:, 0:KC * BATCH]).then_inc(turned_copied, 1)
            dve.wait_ge(logits_done, 1)
            then(nc.vector.tensor_tensor(logits[:, :], psum_small[0:BATCH, 32:32 + EXP0], b_r[:, :], ALU.add))
            then(nc.vector.tensor_reduce(top[:, :], logits[:, :], AX.X, ALU.max))
            then(nc.vector.tensor_scalar(low[:, :], logits[:, :], top[:, 0:1], None, ALU.subtract))
            dve.wait_ge(exp_done, 1)
            then(nc.vector.reciprocal(inv[:, :], total[:, :]))
            nc.vector.tensor_scalar(rw[:, :], rw[:, :], inv[:, 0:1], None, ALU.mult).then_inc(exp_done, 1)
            dve.wait_ge(load_done, 1)
            then(nc.vector.tensor_scalar(load_[:, :], psum_small[0:BATCH, 64:64 + EXP0], float(SEQ), CAPACITY, ALU.mult, ALU.max))
            then(nc.vector.reciprocal(load_[:, :], load_[:, :]))
            then(nc.vector.scalar_tensor_tensor(out=logits[:, :], in0=load_[:, :], scalar=CAPACITY, in1=rw[:, :], op0=ALU.mult, op1=ALU.mult))
            then(nc.vector.tensor_reduce(top[:, :], logits[:, :], AX.X, ALU.max))
            then(nc.vector.tensor_scalar(low[:, :], logits[:, :], top[:, 0:1], None, ALU.subtract))
            nc.vector.engine_nop().then_inc(step, 1)
            dve.wait_ge(exp_done, 3)
            count[0] += 1
            then(nc.vector.reciprocal(inv[:, :], total[:, :]))
            then(nc.vector.tensor_scalar(rw[:, :], rw[:, :], inv[:, 0:1], None, ALU.mult))
            then(nc.vector.max(best[:, :], rw[:, :]))
            nc.vector.max_index(best_at[:, :], best[:, :], rw[:, :])
            then(nc.vector.tensor_tensor(low[:, 0:1], best[:, 1:2], best[:, 0:1], ALU.subtract))
            dve.wait_ge(exp_done, 4)
            then(nc.vector.tensor_scalar(total[:, :], pair[:, 1:2], 1.0, None, ALU.add))
            then(nc.vector.reciprocal(pair[:, 0:1], total[:, :]))
            nc.vector.tensor_scalar(pair[:, 1:2], pair[:, 1:2], pair[:, 0:1], None, ALU.mult).then_inc(routed, 1)


def experts_by_image(nc, d, X, ident, mean, rstd, picked, weight, mean_after, rstd_after):
    with ExitStack() as ctx:
        counter = counters(nc, ctx)
        sb = lambda n, s, dt=F32: ctx.enter_context(nc.sbuf_tensor(n, s, dt))
        sem = lambda n: counter(n)
        w1 = [sb(f"m0_w1_{e}", [P, KC, F]) for e in range(TOPK)]
        w2 = [sb(f"m0_w2_{e}", [P, FM, C]) for e in range(TOPK)]
        b1 = [sb(f"m0_b1_{e}", [P, FM]) for e in range(TOPK)]
        b2 = [sb(f"m0_b2_{e}", [P, C]) for e in range(TOPK)]
        tok = [sb(f"m0_tok{u}", [P, TPB, C]) for u in range(2)]
        tokT = sb("m0_tokT", [P, KC, SEQ])
        hid = [[sb(f"m0_hid{hf}_{e}", [P, FM, HALF]) for e in range(TOPK)] for hf in range(2)]
        bias = sb("m0_bias", [P, C])
        z = sb("m0_z", [P, TPH, C])
        stats = sb("m0_stats", [P, TPH, 6])
        mv = sb("m0_mv", [P, TPH, 2])
        var = sb("m0_var", [P, TPH])
        rs = sb("m0_rs", [P, TPH])
        minus_half = sb("m0_mh", [P, TPH])
        gamma = sb("m0_gamma", [P, C])
        beta = sb("m0_beta", [P, C])
        bank_t = [ctx.enter_context(nc.psum_tensor(f"m0_bt{i}", [P, 512], F32)) for i in range(2)]
        bank_h = [ctx.enter_context(nc.psum_tensor(f"m0_bh{i}", [P, 512], F32)) for i in range(2)]
        bank_y = [ctx.enter_context(nc.psum_tensor(f"m0_by{i}", [P, C], F32)) for i in range(4)]
        names = """affine_loaded w1_loaded w2_loaded w2_free tok_ready tok_free turned turned_copied h_done h_free y_done y_free w2_scaled bias1 bias2
            z_ready stats_ready mv_ready var_ready rs_ready zn_ready zg_ready zb_ready x_ready hid_free""".split()
        S = {n: sem("m0_" + n) for n in names}
        passed = {e: sem(f"m0_passed_{e}") for e in ("dve", "sp")}
        after_begin, after_on_vector, after_on_gpsimd = norm_as_they_come(nc, ctx, counter, "ln2", X, mean_after, rstd_after, LN_C_EPS, TPH)
        block = ctx.enter_context(nc.Block())

        @block.sync
        def _(sp):
            sp.dma_start(gamma[:, :], row_on_all(d["gamma0"], C)).then_inc(S["affine_loaded"], 16)
            sp.dma_start(beta[:, :], row_on_all(d["beta0"], C)).then_inc(S["affine_loaded"], 16)
            with sp.Fori(0, BATCH) as b:
                sp.wait_ge(S["h_free"], 16 * b + 2)
                sp.sem_inc(passed["sp"], 1)
                for e in range(TOPK):
                    at = sp.value_load(picked[0:1, bass.ds(TOPK * b + e, 1)], min_val=0, max_val=EXP0 - 1)
                    sp.dma_start(w1[e][:, :, :], d["W1_0"][bass.ds(at, 1)].rearrange("a (k p) f -> p (a k) f", p=P)).then_inc(S["w1_loaded"], 16)
                    sp.dma_start(b1[e][:, :], d["b1_0"][bass.ds(at, 1)].rearrange("a p m -> p (a m)")).then_inc(S["w1_loaded"], 16)
                sp.wait_ge(S["w2_free"], b + 1)
                sp.sem_inc(passed["sp"], 1)
                for e in range(TOPK):
                    at = sp.value_load(picked[0:1, bass.ds(TOPK * b + e, 1)], min_val=0, max_val=EXP0 - 1)
                    sp.dma_start(w2[e][:, :, :], d["W2_0"][bass.ds(at, 1)].rearrange("a (m p) c -> p (a m) c", p=P)).then_inc(S["w2_loaded"], 16)
                    sp.dma_start(b2[e][:, :], d["b2_0"][bass.ds(at, 1)].broadcast_to([P, C])).then_inc(S["w2_loaded"], 16)

        W_PER = 16 * 2 * TOPK

        @block.tensor
        def _(pe):
            def turn(n, u):
                pe.wait_ge(S["tok_ready"], n + 1)
                for q in range(4):
                    pe.wait_ge(S["turned_copied"], 4 * n + q + 1)
                    for i in range(2):
                        for k in range(KC):
                            mm = nc.tensor.transpose(bank_t[q % 2][:, (KC * i + k) * P:(KC * i + k + 1) * P], tok[u][:, 2 * q + i, k * P:(k + 1) * P], ident[:, :])
                    mm.then_inc(S["turned"], 1)

            turn(0, 0)
            with pe.Fori(0, BATCH // 2) as pair:
                for u in range(2):
                    b = 2 * pair + u
                    pe.wait_ge(S["w1_loaded"], W_PER * b + W_PER)
                    pe.wait_ge(S["turned_copied"], 4 * b + 4 + 2)
                    g = 0
                    for hf in range(2):
                        for e in range(TOPK):
                            for m in range(FM):
                                pe.wait_ge(S["h_free"], 16 * b + g + 1)
                                for k in range(KC):
                                    mm = nc.tensor.matmul(bank_h[g % 2][:, :], w1[e][:, k, m * P:(m + 1) * P], tokT[:, k, hf * HALF:(hf + 1) * HALF],
                                                          start=(k == 0), stop=(k == KC - 1))
                                mm.then_inc(S["h_done"], 1)
                                g += 1
                    turn(b + 1, 1 - u)
                    pe.wait_ge(S["w2_scaled"], b + 1)
                    for hf in range(2):
                        pe.wait_ge(S["h_free"], 16 * b + 8 * (hf + 1) + 2)
                        for i in range(TPH):
                            j = hf * TPH + i
                            pe.wait_ge(S["y_free"], 8 * b + j + 1)
                            for e in range(TOPK):
                                for m in range(FM):
                                    mm = nc.tensor.matmul(bank_y[j % 4][:, :], hid[hf][e][:, m, i * P:(i + 1) * P], w2[e][:, m, :],
                                                          start=(e == 0 and m == 0), stop=(e == TOPK - 1 and m == FM - 1))
                            mm.then_inc(S["y_done"], 1)

        @block.scalar
        def _(act):
            def copy_turned(n):
                for q in range(4):
                    act.wait_ge(S["turned"], 4 * n + q + 1)
                    nc.scalar.copy(tokT[:, :, 2 * q * P:(2 * q + 2) * P].rearrange("p k (i t) -> p i k t", i=2),
                                   bank_t[q % 2][:, :].rearrange("p (i k t) -> p i k t", i=2, k=KC)).then_inc(S["turned_copied"], 1)

            copy_turned(0)
            with act.Fori(0, BATCH) as b:
                act.wait_ge(S["y_done"], 8 * b + 1)
                act.wait_ge(S["w1_loaded"], W_PER * b + W_PER)
                g = 0
                for hf in range(2):
                    for e in range(TOPK):
                        for m in range(FM):
                            act.wait_ge(S["h_done"], 16 * b + g + 1)
                            nc.scalar.activation(hid[hf][e][:, m, :], bank_h[g % 2][:, :], ACT.Gelu, bias=b1[e][:, m:m + 1]).then_inc(S["h_free"], 1)
                            g += 1
                copy_turned(b + 1)

        @block.gpsimd
        def _(pool):
            with pool.Fori(0, BATCH) as b:
                for hf in range(2):
                    pool.wait_ge(S["var_ready"], 2 * b + hf + 1)
                    nc.gpsimd.tensor_tensor(rs[:, :], var[:, :], minus_half[:, :], ALU.pow).then_inc(S["rs_ready"], 1)
                    after_on_gpsimd(pool, b * TPB + hf * TPH, 2 * b + hf + 1)

        @block.vector
        def _(dve):
            nc.vector.memset(minus_half[:, :], -0.5)
            for n, k in (("turned_copied", 2), ("h_free", 2), ("y_free", 4), ("y_done", 1), ("w2_free", 1)):
                for _ in range(k):
                    dve.sem_inc(S[n], 1)

            def normalise(b, u):
                for i in range(TPB):
                    t = b * TPB + i
                    ins = nc.vector.tensor_scalar(tok[u][:, i, :], X[:, bass.ds(t, 1), :].rearrange("p a c -> p (a c)"), mean[:, bass.ds(t, 1)],
                                                  rstd[:, bass.ds(t, 1)], ALU.subtract, ALU.mult)
                ins.then_inc(S["tok_ready"], 1)

            after_begin(dve)
            normalise(0, 0)
            dve.wait_ge(S["affine_loaded"], 32)
            with dve.Fori(0, BATCH // 2) as pair:
                for u in range(2):
                    b = 2 * pair + u
                    normalise((b + 1) & (BATCH - 1), 1 - u)
                    dve.wait_ge(S["w2_loaded"], W_PER * b + W_PER)
                    for e in range(TOPK):
                        we = weight[:, bass.ds(TOPK * b + e, 1)]
                        ins = nc.vector.tensor_scalar(w2[e][:, :, :].rearrange("p m c -> p (m c)"), w2[e][:, :, :].rearrange("p m c -> p (m c)"),
                                                      we, None, ALU.mult)
                    ins.then_inc(S["w2_scaled"], 1)
                    nc.vector.tensor_scalar(bias[:, :], b2[0][:, :], weight[:, bass.ds(TOPK * b, 1)], None, ALU.mult).then_inc(S["bias1"], 1)
                    dve.wait_ge(S["bias1"], b + 1)
                    nc.vector.scalar_tensor_tensor(out=bias[:, :], in0=b2[1][:, :], scalar=weight[:, bass.ds(TOPK * b + 1, 1)], in1=bias[:, :],
                                                   op0=ALU.mult, op1=ALU.add).then_inc(S["bias2"], 1)
                    dve.wait_ge(S["bias2"], b + 1)
                    dve.wait_ge(S["turned"], 4 * b + 4)
                    nc.vector.tensor_tensor(tok[u][:, :, :], tok[u][:, :, :], bias[:, :].unsqueeze(1).broadcast_to([P, TPB, C]), ALU.add)\
                        .then_inc(S["tok_free"], 1)
                    dve.wait_ge(S["tok_free"], b + 1)
                    for hf in range(2):
                        n = 2 * b + hf + 1
                        for i in range(TPH):
                            j = hf * TPH + i
                            dve.wait_ge(S["y_done"], 8 * b + j + 2)
                            nc.vector.tensor_tensor(z[:, i, :], bank_y[j % 4][:, :], tok[u][:, j, :], ALU.add).then_inc(S["y_free"], 1)
                        if hf == 1:
                            dve.sem_inc(S["w2_free"], 1)
                        dve.wait_ge(S["y_free"], 8 * b + 4 * hf + 4 + 4)
                        dve.sem_inc(passed["dve"], 1)
                        for i in range(TPH):
                            ins = nc.vector.bn_stats(stats[:, i, :], z[:, i, :])
                        ins.then_inc(S["stats_ready"], 1)
                        dve.wait_ge(S["stats_ready"], n)
                        dve.sem_inc(passed["dve"], 1)
                        for i in range(TPH):
                            ins = nc.vector.bn_aggr(mv[:, i, :], stats[:, i, :])
                        ins.then_inc(S["mv_ready"], 1)
                        dve.wait_ge(S["mv_ready"], n)
                        nc.vector.tensor_scalar(var[:, :], mv[:, :, 1], LN_T_EPS, None, ALU.add).then_inc(S["var_ready"], 1)
                        dve.wait_ge(S["rs_ready"], n)
                        for i in range(TPH):
                            ins = nc.vector.tensor_scalar(z[:, i, :], z[:, i, :], mv[:, i, 0:1], rs[:, i:i + 1], ALU.subtract, ALU.mult)
                        ins.then_inc(S["zn_ready"], 1)
                        dve.wait_ge(S["zn_ready"], n)
                        nc.vector.tensor_tensor(z[:, :, :], z[:, :, :], gamma[:, :].unsqueeze(1).broadcast_to([P, TPH, C]), ALU.mult)\
                            .then_inc(S["zg_ready"], 1)
                        dve.wait_ge(S["zg_ready"], n)
                        nc.vector.tensor_tensor(z[:, :, :], z[:, :, :], beta[:, :].unsqueeze(1).broadcast_to([P, TPH, C]), ALU.add)\
                            .then_inc(S["zb_ready"], 1)
                        dve.wait_ge(S["zb_ready"], n)
                        xt = X[:, bass.ds(b * TPB + hf * TPH, TPH), :]
                        nc.vector.tensor_tensor(xt, xt, z[:, :, :], ALU.add).then_inc(S["x_ready"], 1)
                        dve.wait_ge(S["x_ready"], n)
                        after_on_vector(dve, b * TPB + hf * TPH, n)


ROW = 32
RPT = P // ROW
AH = 8
GT = 4
GROUPS = TILES // GT
RH = RPT * AH


def row_attention(nc, d, X, ident, mean, rstd):
    with ExitStack() as ctx:
        counter = counters(nc, ctx)
        def sb(name, shape, dt=F32):
            return ctx.enter_context(nc.sbuf_tensor("at_" + name, shape, dt))

        def per_stream(name, shape):
            return [sb(f"{name}{s}", shape) for s in range(STREAMS)]

        def sems(name):
            return [counter(f"at_{name}{s}") for s in range(STREAMS)]

        w_qk = sb("w_qk", [P, KC, 2 * RH])
        b_qk = sb("b_qk", [2 * RH, 1])
        scale = sb("scale", [2 * RH, 1])
        row_mask = sb("row_mask", [2 * RH, P])
        head_mask = sb("head_mask", [P, KC, GT * RH])
        w_v = sb("w_v", [P, KC, C])
        b_v = sb("b_v", [P, KC])
        w_o = sb("w_o", [P, KC, C])
        b_o = sb("b_o", [P, C])
        tok = per_stream("tok", [P, GT, C])
        tokT = per_stream("tokT", [P, KC, GT * P])
        neg = per_stream("neg", [2 * RH, GT * P])
        neg_exp = per_stream("neg_exp", [2 * RH, GT * P])
        pos = per_stream("pos", [2 * RH, GT * P])
        total = per_stream("total", [2 * RH, GT * RPT])
        inv = per_stream("inv", [2 * RH, GT * RPT])
        qk = per_stream("qk", [2 * RH, GT * P])
        qk_tok = per_stream("qk_tok", [P, GT, 2 * RH])
        kx = per_stream("kx", [P, KC, GT * RH])
        val = per_stream("val", [P, KC, GT * RH])
        val_out = per_stream("val_out", [RH, GT, C])
        z = per_stream("z", [P, GT, C])
        bank = [[ctx.enter_context(nc.psum_tensor(f"at_bank{i}_{s}", [P, 512], F32)) for s in range(STREAMS)] for i in range(4)]
        loaded = counter("at_loaded")
        names = """tok_ready turned tokT_ready qk_done neg_ready exp_done pos_ready sum_ready total_ready inv_ready invs_ready
            qkn_ready qk_ready qk_turned qk_tok_ready kx_done kx_ready val_done val_ready vo_done vo_ready out_done z_ready x_ready""".split()
        S = {n: sems(n) for n in names}
        passed = {e: counter(f"at_passed_{e}") for e in ("dve", "pe")}
        block = ctx.enter_context(nc.Block())
        N = GROUPS // STREAMS
        both = range(STREAMS)

        @block.sync
        def _(sp):
            for t, n in ((w_qk, "w_qk"), (w_v, "w_v"), (w_o, "w_o")):
                sp.dma_start(t[:, :, :], d[n].rearrange("(k p) f -> p k f", p=P)).then_inc(loaded, 16)
            for t, n in ((b_qk, "b_qk"), (scale, "qk_scale"), (row_mask, "row_mask"), (head_mask, "head_mask"), (b_v, "b_v")):
                sp.dma_start(t[:], d[n]).then_inc(loaded, 16)
            sp.dma_start(b_o[:, :], row_on_all(d["b_o"], C)).then_inc(loaded, 16)

        N_LOADED = 16 * 9

        @block.tensor
        def _(pe):
            pe.wait_ge(loaded, N_LOADED)
            with pe.Fori(0, N) as t:
                n = t + 1
                for s in both:
                    pe.wait_ge(S["tok_ready"][s], n)
                    for k in range(KC):
                        for j in range(GT):
                            mm = nc.tensor.transpose(bank[k][s][:, j * P:(j + 1) * P], tok[s][:, j, k * P:(k + 1) * P], ident[:, :])
                    mm.then_inc(S["turned"][s], 1)
                for s in both:
                    pe.wait_ge(S["z_ready"][s], n)
                    pe.wait_ge(S["tokT_ready"][s], n)
                    for k in range(KC):
                        mm = nc.tensor.matmul(bank[2][s][0:2 * RH, :], w_qk[:, k, :], tokT[s][:, k, :], start=(k == 0), stop=(k == KC - 1))
                    mm.then_inc(S["qk_done"][s], 1)
                for s in both:
                    pe.wait_ge(S["qk_ready"][s], n)
                    pe.sem_inc(passed["pe"], 1)
                    for j in range(GT):
                        mm = nc.tensor.transpose(bank[2][s][:, j * 2 * RH:(j + 1) * 2 * RH], qk[s][:, j * P:(j + 1) * P], ident[0:2 * RH, 0:2 * RH])
                    mm.then_inc(S["qk_turned"][s], 1)
                    pe.wait_ge(S["qk_tok_ready"][s], n)
                    for k in range(KC):
                        for j in range(GT):
                            mm = nc.tensor.matmul(bank[0][s][:, k * GT * RH + j * RH:k * GT * RH + (j + 1) * RH],
                                                  tok[s][:, j, k * P:(k + 1) * P], qk_tok[s][:, j, RH:2 * RH], start=True, stop=True)
                    mm.then_inc(S["kx_done"][s], 1)
                for s in both:
                    pe.wait_ge(S["kx_ready"][s], n)
                    for m in range(KC):
                        for k in range(KC):
                            mm = nc.tensor.matmul(bank[1][s][:, m * GT * RH:(m + 1) * GT * RH], w_v[:, k, m * P:(m + 1) * P], kx[s][:, k, :],
                                                  start=(k == 0), stop=(k == KC - 1))
                    mm.then_inc(S["val_done"][s], 1)
                for s in both:
                    pe.wait_ge(S["val_ready"][s], n)
                    for j in range(GT):
                        for m in range(KC):
                            mm = nc.tensor.matmul(bank[j // 2][s][0:RH, j % 2 * C:(j % 2 + 1) * C], val[s][:, m, j * RH:(j + 1) * RH], w_o[:, m, :],
                                                  start=(m == 0), stop=(m == KC - 1))
                    mm.then_inc(S["vo_done"][s], 1)
                for s in both:
                    pe.wait_ge(S["vo_ready"][s], n)
                    pe.sem_inc(passed["pe"], 1)
                    for j in range(GT):
                        mm = nc.tensor.matmul(bank[2 + j // 2][s][:, j % 2 * C:(j % 2 + 1) * C], qk[s][0:RH, j * P:(j + 1) * P], val_out[s][:, j, :],
                                              start=True, stop=True)
                    mm.then_inc(S["out_done"][s], 1)

        @block.scalar
        def _(act):
            act.wait_ge(loaded, N_LOADED)
            with act.Fori(0, N) as t:
                n = t + 1
                for s in both:
                    act.wait_ge(S["turned"][s], n)
                    for k in range(KC):
                        ins = nc.scalar.copy(tokT[s][:, k, :], bank[k][s][:, :])
                    ins.then_inc(S["tokT_ready"][s], 1)
                for s in both:
                    act.wait_ge(S["neg_ready"][s], n)
                    nc.scalar.activation(neg_exp[s][:, :], neg[s][:, :], ACT.Exp).then_inc(S["exp_done"][s], 1)
                for s in both:
                    act.wait_ge(S["qk_turned"][s], n)
                    nc.scalar.copy(qk_tok[s][:, :, :].rearrange("p j c -> p (j c)"), bank[2][s][:, 0:GT * 2 * RH]).then_inc(S["qk_tok_ready"][s], 1)
                for s in both:
                    act.wait_ge(S["kx_done"][s], n)
                    nc.scalar.copy(kx[s][:, :, :].rearrange("p k c -> p (k c)"), bank[0][s][:, 0:KC * GT * RH]).then_inc(S["kx_ready"][s], 1)
                for s in both:
                    act.wait_ge(S["vo_done"][s], n)
                    for i in range(2):
                        ins = nc.scalar.copy(val_out[s][:, 2 * i:2 * i + 2, :].rearrange("p j c -> p (j c)"), bank[i][s][0:RH, :])
                    ins.then_inc(S["vo_ready"][s], 1)

        @block.vector
        def _(dve):
            dve.wait_ge(loaded, N_LOADED)
            for s in both:
                dve.sem_inc(S["x_ready"][s], 1)
                dve.sem_inc(S["z_ready"][s], 1)

            def normalise(t, s):
                for j in range(GT):
                    at = (t + s * N) * GT + j
                    ins = nc.vector.tensor_scalar(tok[s][:, j, :], X[:, bass.ds(at, 1), :].rearrange("p a c -> p (a c)"), mean[:, bass.ds(at, 1)],
                                                  rstd[:, bass.ds(at, 1)], ALU.subtract, ALU.mult)
                ins.then_inc(S["tok_ready"][s], 1)

            for s in both:
                normalise(0, s)
            with dve.Fori(0, N) as t:
                n = t + 1
                for s in both:
                    dve.wait_ge(S["qk_done"][s], n)
                    nc.vector.tensor_scalar(neg[s][:, :], bank[2][s][0:2 * RH, :], b_qk[:, 0:1], 0.0, ALU.add, ALU.min).then_inc(S["neg_ready"][s], 1)
                    nc.vector.tensor_scalar(pos[s][:, :], bank[2][s][0:2 * RH, :], b_qk[:, 0:1], 0.0, ALU.add, ALU.max).then_inc(S["pos_ready"][s], 1)
                for s in both:
                    dve.wait_ge(S["pos_ready"][s], n)
                    dve.wait_ge(S["exp_done"][s], n)
                    nc.vector.tensor_tensor(pos[s][:, :], pos[s][:, :], neg_exp[s][:, :], ALU.add).then_inc(S["sum_ready"][s], 1)
                    dve.wait_ge(S["sum_ready"][s], n)
                    nc.vector.tensor_reduce(total[s][:, :], pos[s][:, :].rearrange("p (r c) -> p r c", c=ROW), AX.X, ALU.add)\
                        .then_inc(S["total_ready"][s], 1)
                    nc.vector.tensor_tensor(qk[s][:, :].rearrange("p (j c) -> p j c", j=GT), pos[s][:, :].rearrange("p (j c) -> p j c", j=GT),
                                            row_mask[:, :].unsqueeze(1).broadcast_to([2 * RH, GT, P]), ALU.mult).then_inc(S["qkn_ready"][s], 1)
                    dve.wait_ge(S["total_ready"][s], n)
                    nc.vector.reciprocal(inv[s][:, :], total[s][:, :]).then_inc(S["inv_ready"][s], 1)
                    dve.wait_ge(S["inv_ready"][s], n)
                    nc.vector.tensor_scalar(inv[s][:, :], inv[s][:, :], scale[:, 0:1], None, ALU.mult).then_inc(S["invs_ready"][s], 1)
                    dve.wait_ge(S["invs_ready"][s], n)
                    dve.wait_ge(S["qkn_ready"][s], n)
                    q3 = qk[s][:, :].rearrange("p (r c) -> p r c", c=ROW)
                    nc.vector.tensor_tensor(q3, q3, inv[s][:, :].unsqueeze(2).broadcast_to([2 * RH, GT * RPT, ROW]), ALU.mult)\
                        .then_inc(S["qk_ready"][s], 1)
                for s in both:
                    dve.wait_ge(S["x_ready"][s], n)
                    dve.wait_ge(S["kx_done"][s], n)
                    normalise((t + 1) & (N - 1), s)
                for s in both:
                    dve.wait_ge(S["val_done"][s], n)
                    for m in range(KC):
                        ins = nc.vector.scalar_tensor_tensor(out=val[s][:, m, :], in0=bank[1][s][:, m * GT * RH:(m + 1) * GT * RH], scalar=b_v[:, m:m + 1],
                                                             in1=head_mask[:, m, :], op0=ALU.add, op1=ALU.mult)
                    ins.then_inc(S["val_ready"][s], 1)
                for s in both:
                    dve.wait_ge(S["out_done"][s], n)
                    for i in range(2):
                        ins = nc.vector.tensor_tensor(z[s][:, 2 * i:2 * i + 2, :], bank[2 + i][s][:, :].rearrange("p (j c) -> p j c", j=2),
                                                      b_o[:, :].unsqueeze(1).broadcast_to([P, 2, C]), ALU.add)
                    ins.then_inc(S["z_ready"][s], 1)
                    dve.wait_ge(S["z_ready"][s], n + 1)
                    xt = X[:, bass.ds((t + s * N) * GT, GT), :]
                    nc.vector.tensor_tensor(xt, xt, z[s][:, :, :], ALU.add).then_inc(S["x_ready"][s], 1)


EXP1 = 4
GH = 4
GF = GH * EXP1
GM = GF + GH
GT1 = GF + 2 * GH
NODES = TILES * P
EDGE_COLS = 8192
ECB = 8
BITS = 13
DST_TILES = NODES // P


def tables_and_edges(nc, d, X, ident, mean, rstd, own, src_rows, dst_rows, edge, longest):
    with ExitStack() as ctx:
        counter = counters(nc, ctx)
        sb = lambda n, s, dt=F32: ctx.enter_context(nc.sbuf_tensor("te_" + n, s, dt))
        I16 = mybir.dt.int16
        N = TILES // TPH
        h_all = sb("h_all", [P, TILES, GF])
        w = sb("w", [P, KC, GF])
        tok = sb("tok", [P, TPH, C])
        tokT = sb("tokT", [P, KC, HALF])
        att = [sb(f"att{i}", [P, GF]) for i in range(2)]
        prod = tok[:, :, :].rearrange("p i c -> p (i c)").rearrange("p (t f) -> p t f", f=GF)
        src = sb("src", [P, TILES, GT1])
        dst = sb("dst", [P, TILES, 2 * GH])
        both_w = sb("both_w", [P, TILES, 2 * GH])
        own_max, g = sb("own_max", [P, GH]), sb("g", [P, GH])
        a_src, a_dst = both_w[:, :, 0:GH], both_w[:, :, GH:2 * GH]
        raw = sb("raw", [P, EDGE_COLS], I32)
        invalid, shift, move = (sb(n, [P, EDGE_COLS], I16) for n in ("invalid", "shift", "move"))
        moved = invalid
        mine = sb("mine", [P, 1])
        most = sb("most", [P, 1])
        bank_t = [ctx.enter_context(nc.psum_tensor(f"te_bt{k}", [P, 512], F32)) for k in range(KC)]
        bank_f = ctx.enter_context(nc.psum_tensor("te_bf", [P, TPH * GF], F32))
        names = """w_loaded edges_loaded centred tok_ready turned tokT_ready f_done f_copied prods a_ready max_ready g_ready prod2 a2_ready
            diff_ready total_ready factors_ready h_placed w_pairs w_ready stored packed scaled place_loaded step counted most_ready""".split()
        S = {n: counter("te_" + n) for n in names}
        passed = counter("te_passed")
        norm_on_vector, norm_on_gpsimd, rstd_ready = norm_parts(nc, ctx, counter, "ln3", X, mean, rstd, LN_T_EPS)
        block = ctx.enter_context(nc.Block())
        wide = lambda a: a[:, :].unsqueeze(1).broadcast_to([P, TILES, a.shape[-1]])
        by_head = lambda a: a.rearrange("p t (h e) -> p t h e", h=GH)

        @block.sync
        def _(sp):
            sp.dma_start(edge[:, 0:EDGE_COLS], d["edges"][1]).then_inc(S["edges_loaded"], 16)
            sp.dma_start(w[:, :, :], d["w_gat"].rearrange("(k p) f -> p k f", p=P)).then_inc(S["w_loaded"], 16)
            for a, n in zip(att, ("att_src", "att_dst")):
                sp.dma_start(a[:, :], row_on_all(d[n], GF)).then_inc(S["w_loaded"], 16)
            sp.dma_start(raw[:, :], d["edges"][0]).then_inc(S["edges_loaded"], 16)
            sp.wait_ge(S["packed"], 1)
            sp.dma_start(raw[:, :], row_on_all(d["place"], EDGE_COLS)).then_inc(S["place_loaded"], 16)
            sp.wait_ge(S["factors_ready"], 4)
            sp.wait_ge(S["h_placed"], 1)
            sp.dma_start(src_rows.rearrange("(i p) c -> p i c", p=P), src[:, :, :]).then_inc(S["stored"], 16)
            sp.dma_start(dst_rows.rearrange("(i p) c -> p i c", p=P), dst[:, :, :]).then_inc(S["stored"], 16)
            sp.wait_ge(S["stored"], 32)

        @block.gpsimd
        def _(pool):
            norm_on_gpsimd(pool)
            pool.sem_inc(S["turned"], 1)
            pool.wait_ge(rstd_ready, NORM_DONE)
            with pool.Fori(0, N) as t:
                at = bass.ds(t * TPH, TPH)
                pool.wait_ge(S["turned"], t + 1)
                nc.gpsimd.tensor_tensor(tok[:, :, :], X[:, at, :], mean[:, at].unsqueeze(2).broadcast_to([P, TPH, C]), ALU.subtract)\
                    .then_inc(S["centred"], 1)
                pool.wait_ge(S["centred"], t + 1)
                nc.gpsimd.tensor_tensor(tok[:, :, :], tok[:, :, :], rstd[:, at].unsqueeze(2).broadcast_to([P, TPH, C]), ALU.mult)\
                    .then_inc(S["tok_ready"], 1)
            pool.wait_ge(S["w_loaded"], 48)
            pool.wait_ge(S["f_copied"], N + 1)
            nc.gpsimd.tensor_copy(src[:, :, 0:GF], h_all[:, :, :]).then_inc(S["h_placed"], 1)
            for i, a in enumerate((a_src, a_dst)):
                nc.gpsimd.tensor_tensor(prod, h_all[:, :, :], wide(att[i]), ALU.mult).then_inc(S["prods"], 1)
                pool.wait_ge(S["prods"], i + 1)
                p4 = by_head(prod)
                for e in range(1, EXP1):
                    nc.gpsimd.tensor_tensor(a, p4[:, :, :, 0] if e == 1 else a, p4[:, :, :, e], ALU.add).then_inc(S["a_ready"], 1)
                    pool.wait_ge(S["a_ready"], i * (EXP1 - 1) + e)
            pool.wait_ge(S["counted"], 1)
            nc.gpsimd.partition_all_reduce(most[:, :], mine[:, :], P, bass.bass_isa.ReduceOp.max).then_inc(S["most_ready"], 1)
            pool.wait_ge(S["max_ready"], 1)
            nc.gpsimd.partition_all_reduce(g[:, :], own_max[:, :], P, bass.bass_isa.ReduceOp.max).then_inc(S["g_ready"], 1)
            pool.wait_ge(S["g_ready"], 1)
            nc.gpsimd.tensor_tensor(a_src, a_src, wide(g), ALU.subtract).then_inc(S["diff_ready"], 1)
            nc.gpsimd.tensor_tensor(a_dst, a_dst, wide(g), ALU.add).then_inc(S["total_ready"], 1)
            pool.wait_ge(S["total_ready"], 1)
            nc.gpsimd.tensor_scalar(dst[:, :, 0:GH], a_dst, 0.8, 0.0, ALU.mult, ALU.min)
            nc.gpsimd.tensor_scalar(dst[:, :, GH:2 * GH], a_dst, -0.8, 0.0, ALU.mult, ALU.min).then_inc(S["scaled"], 1)
            pool.wait_ge(S["factors_ready"], 4)
            nc.gpsimd.tensor_tensor(both_w[:, :, :], src[:, :, GF:GT1], dst[:, :, :], ALU.mult).then_inc(S["w_pairs"], 1)
            pool.wait_ge(S["w_ready"], 1)
            for e in range(EXP1):
                nc.gpsimd.tensor_tensor(by_head(own[:, :, 0:GF])[:, :, :, e], by_head(h_all[:, :, :])[:, :, :, e], own[:, :, GF:GM], ALU.mult)

        @block.tensor
        def _(pe):
            pe.wait_ge(S["w_loaded"], 48)
            pe.sem_inc(S["f_copied"], 1)
            with pe.Fori(0, N) as t:
                pe.wait_ge(S["tok_ready"], t + 1)
                for k in range(KC):
                    for i in range(TPH):
                        mm = nc.tensor.transpose(bank_t[k][:, i * P:(i + 1) * P], tok[:, i, k * P:(k + 1) * P], ident[:, :])
                mm.then_inc(S["turned"], 1)
                pe.wait_ge(S["tokT_ready"], t + 1)
                pe.wait_ge(S["f_copied"], t + 1)
                pe.sem_inc(passed, 1)
                for i in range(TPH):
                    for k in range(KC):
                        mm = nc.tensor.matmul(bank_f[:, i * GF:(i + 1) * GF], tokT[:, k, i * P:(i + 1) * P], w[:, k, :],
                                              start=(k == 0), stop=(k == KC - 1))
                mm.then_inc(S["f_done"], 1)

        @block.scalar
        def _(act):
            with act.Fori(0, N) as t:
                act.wait_ge(S["turned"], t + 2)
                for k in range(KC):
                    ins = nc.scalar.copy(tokT[:, k, :], bank_t[k][:, :])
                ins.then_inc(S["tokT_ready"], 1)
                act.wait_ge(S["f_done"], t + 1)
                nc.scalar.copy(h_all[:, bass.ds(t * TPH, TPH), :].rearrange("p i f -> p (i f)"), bank_f[:, :]).then_inc(S["f_copied"], 1)
            act.wait_ge(S["diff_ready"], 1)
            nc.scalar.activation(src[:, :, GF:GF + GH], a_src, ACT.Exp).then_inc(S["factors_ready"], 1)
            nc.scalar.activation(src[:, :, GF + GH:GT1], a_src, ACT.Exp, scale=0.2).then_inc(S["factors_ready"], 1)
            act.wait_ge(S["scaled"], 1)
            nc.scalar.activation(dst[:, :, 0:GH], dst[:, :, 0:GH], ACT.Exp).then_inc(S["factors_ready"], 1)
            nc.scalar.activation(dst[:, :, GH:2 * GH], dst[:, :, GH:2 * GH], ACT.Exp).then_inc(S["factors_ready"], 1)

        @block.vector
        def _(dve):
            count = [0]

            def then(ins):
                count[0] += 1
                ins.then_inc(S["step"], 1)
                dve.wait_ge(S["step"], count[0])

            norm_on_vector(dve)
            E = EDGE_COLS
            nc.vector.memset(edge[:, E:], 0)
            dve.wait_ge(S["edges_loaded"], 32)
            then(nc.vector.tensor_scalar(invalid[:, :], edge[:, 0:E], NODES, None, ALU.is_ge))
            then(nc.vector.tensor_tensor_scan(move[:, :], invalid[:, :], invalid[:, :], 0.0, ALU.add, ALU.max))
            nc.vector.tensor_scalar(mine[:, :], move[:, E - 1:E], -1.0, float(E), ALU.mult, ALU.add).then_inc(S["counted"], 1)
            then(nc.vector.scalar_tensor_tensor(out=shift[:, :], in0=invalid[:, :], scalar=0, in1=move[:, :], op0=ALU.is_equal, op1=ALU.mult))
            nc.vector.tensor_scalar(raw[:, :], raw[:, :], NODES - 1, None, ALU.min)
            then(nc.vector.tensor_scalar(edge[:, 0:E], edge[:, 0:E], BITS, None, ALU.logical_shift_left))
            then(nc.vector.tensor_tensor(edge[:, 0:E], edge[:, 0:E], raw[:, :], ALU.bitwise_or))
            dve.sem_inc(S["packed"], 1)
            for b in range(BITS):
                if b == 2 * BITS // 3:
                    dve.wait_ge(S["a_ready"], 2 * (EXP1 - 1))
                    nc.vector.tensor_reduce(own_max[:, :], a_src.rearrange("p t h -> p h t"), AX.X, ALU.max).then_inc(S["max_ready"], 1)
                by = 1 << b
                then(nc.vector.tensor_scalar(move[:, :], shift[:, :], b, 1, ALU.logical_shift_right, ALU.bitwise_and))
                then(nc.vector.copy_predicated(edge[:, 0:E - by], move[:, by:E], edge[:, by:E]))
                then(nc.vector.tensor_tensor(moved[:, :], move[:, :], shift[:, :], ALU.mult))
                then(nc.vector.tensor_tensor(shift[:, :], shift[:, :], moved[:, :], ALU.subtract))
                then(nc.vector.tensor_tensor(shift[:, 0:E - by], shift[:, 0:E - by], moved[:, by:E], ALU.add))
            dve.wait_ge(S["place_loaded"], 16)
            then(nc.vector.tensor_scalar(raw[:, :], raw[:, :], mine[:, 0:1], None, ALU.is_gt))
            then(nc.vector.tensor_scalar(raw[:, :], raw[:, :], 2 * BITS, None, ALU.logical_shift_left))
            then(nc.vector.tensor_tensor(edge[:, 0:E], edge[:, 0:E], raw[:, :], ALU.bitwise_or))
            dve.wait_ge(S["w_pairs"], 1)
            nc.vector.tensor_tensor(own[:, :, GF:GM], both_w[:, :, 0:GH], both_w[:, :, GH:2 * GH], ALU.max).then_inc(S["w_ready"], 1)
            dve.wait_ge(S["most_ready"], 1)
            nc.vector.tensor_copy(longest[:, :], most[:, :])


def sum_edges(nc, d, edge, longest, src_rows, dst_rows, own, w1, w2, b1, b2):
    with ExitStack() as ctx:
        counter = counters(nc, ctx)
        sb = lambda n, s, dt=F32: ctx.enter_context(nc.sbuf_tensor("se_" + n, s, dt))
        sem = lambda n: counter("se_" + n)
        both = range(2)
        RING = 4
        lane = sb("lane", [P, P])
        zero = sb("zero", [P, P])
        now = [sb(f"now{u}", [P, ECB], I32) for u in both]
        src_at = [sb(f"src_at{u}", [P, ECB], I32) for u in both]
        dst_full = [sb(f"dst_full{u}", [P, ECB], I32) for u in both]
        dst_at = [sb(f"dst_at{u}", [P, ECB], I32) for u in both]
        dst_lane = [sb(f"dst_lane{u}", [P, ECB], I32) for u in both]
        dst_tile = [sb(f"dst_tile{u}", [P, ECB], I32) for u in both]
        lane_f = [sb(f"lane_f{u}", [P, ECB]) for u in both]
        tile_f = [sb(f"tile_f{u}", [P, ECB]) for u in both]
        is_lane = [sb(f"is_lane{u}", [P, ECB, P]) for u in both]
        is_tile = [sb(f"is_tile{u}", [P, ECB, DST_TILES]) for u in both]
        src_row = [sb(f"src_row{u}", [P, ECB, GT1]) for u in both]
        dst_row = [sb(f"dst_row{u}", [P, ECB, 2 * GH]) for u in both]
        pair = [sb(f"pair{u}", [P, ECB, 2 * GH]) for u in both]
        msg = [sb(f"msg{u}", [P, ECB, GM]) for u in both]
        spread = [sb(f"spread{i}", [P, DST_TILES, GM]) for i in range(RING)]
        bank = [ctx.enter_context(nc.psum_tensor(f"se_b{i}", [P, 512], F32)) for i in range(3)]
        WIDTH = DST_TILES * GM
        parts = [(i, i * 512, min(512, WIDTH - i * 512)) for i in range(3)]
        names = """loaded w_loaded cleared taken decoded floated hot_ready gathered0 gathered1 paired weighed msg_ready spread_ready spread_used summed""".split()
        S = {n: sem(n) for n in names}
        gathered = [S["gathered0"], S["gathered1"]]
        passed = {e: sem("passed_" + e) for e in ("dve", "pe", "pool")}
        block = ctx.enter_context(nc.Block())
        STEPS = EDGE_COLS // (2 * ECB)
        SKIP = 16
        count_in = longest[0:1, 0:1]

        @block.sync
        def _(sp):
            sp.dma_start(lane[:, :], row_on_all(d["lane"], P)).then_inc(S["loaded"], 16)
            for e in range(EXP1):
                sp.dma_start(w1[:, e, :, :], d["W1_1"][e].rearrange("(k p) f -> p k f", p=P)).then_inc(S["w_loaded"], 16)
                sp.dma_start(w2[:, e, :, :], d["W2_1"][e].rearrange("(m p) c -> p m c", p=P)).then_inc(S["w_loaded"], 16)
            sp.dma_start(b1[:, :, :], d["b1_1"]).then_inc(S["w_loaded"], 16)
            sp.dma_start(b2[:, :], d["b2_1"]).then_inc(S["w_loaded"], 16)
            sp.wait_ge(S["w_loaded"], 16 * (2 * EXP1 + 2))

        @block.gpsimd
        def _(pool):
            m = pool.value_load(count_in, min_val=0, max_val=EDGE_COLS)
            with pool.Fori(0, STEPS // SKIP) as far:
                with pool.If(far * (2 * ECB * SKIP) < m):
                    with pool.Fori(0, SKIP) as near:
                        t = far * SKIP + near
                        with pool.If(t * (2 * ECB) < m):
                            for u in both:
                                pool.wait_ge(S["decoded"], 2 * t + (u + 1))
                                pool.wait_ge(S["msg_ready"], 2 * t + (u + 1))
                                pool.sem_inc(passed["pool"], 1)
                                for c in range(ECB):
                                    for row, rows, at in ((src_row, src_rows, src_at), (dst_row, dst_rows, dst_at)):
                                        pool.indirect_dma_start(out=row[u][:, c, :], out_offset=None, in_=rows,
                                                                in_offset=bass.IndirectOffsetOnAxis(ap=at[u][:, c:c + 1], axis=0),
                                                                bounds_check=NODES - 1, oob_is_err=False).then_inc(gathered[u], 16)

        @block.vector
        def _(dve):
            m = dve.value_load(count_in, min_val=0, max_val=EDGE_COLS)
            nc.vector.memset(zero[:, :], 0.0).then_inc(S["cleared"], 1)
            for n, k in (("msg_ready", 2), ("spread_ready", 1), ("spread_used", ECB + 1)):
                for _ in range(k):
                    dve.sem_inc(S[n], 1)
            dve.wait_ge(S["loaded"], 16)

            def decode(step_, u):
                n = step_ + 1
                dve.wait_ge(S["msg_ready"], n)
                nc.vector.tensor_copy(now[u][:, :], edge[:, bass.ds(step_ * ECB, ECB)]).then_inc(S["taken"], 1)
                dve.wait_ge(S["taken"], 2 * n - 1)
                nc.vector.tensor_scalar(src_at[u][:, :], now[u][:, :], NODES - 1, None, ALU.bitwise_and)
                nc.vector.tensor_scalar(dst_tile[u][:, :], now[u][:, :], BITS + 7, None, ALU.logical_shift_right)
                nc.vector.tensor_scalar(dst_full[u][:, :], now[u][:, :], BITS, None, ALU.logical_shift_right).then_inc(S["taken"], 1)
                dve.wait_ge(S["taken"], 2 * n)
                nc.vector.tensor_scalar(dst_lane[u][:, :], dst_full[u][:, :], P - 1, None, ALU.bitwise_and)
                nc.vector.tensor_scalar(dst_at[u][:, :], dst_full[u][:, :], NODES - 1, None, ALU.bitwise_and).then_inc(S["decoded"], 1)
                dve.wait_ge(S["decoded"], n)
                nc.vector.tensor_copy(lane_f[u][:, :], dst_lane[u][:, :])
                nc.vector.tensor_copy(tile_f[u][:, :], dst_tile[u][:, :]).then_inc(S["floated"], 1)

            def mark(step_, u):
                dve.wait_ge(S["floated"], step_ + 1)
                dve.wait_ge(S["spread_used"], step_ * ECB + 1)
                dve.sem_inc(passed["dve"], 1)
                nc.vector.tensor_tensor(is_lane[u][:, :, :], lane[:, :].unsqueeze(1).broadcast_to([P, ECB, P]),
                                        lane_f[u][:, :].unsqueeze(2).broadcast_to([P, ECB, P]), ALU.is_equal)
                nc.vector.tensor_tensor(is_tile[u][:, :, :], lane[:, 0:DST_TILES].unsqueeze(1).broadcast_to([P, ECB, DST_TILES]),
                                        tile_f[u][:, :].unsqueeze(2).broadcast_to([P, ECB, DST_TILES]), ALU.is_equal).then_inc(S["hot_ready"], 1)

            def spread_out(step_, u, c):
                dve.wait_ge(S["spread_used"], step_ * ECB + c + (ECB - 2))
                nc.vector.tensor_tensor(spread[c % RING][:, :, :], msg[u][:, c, :].unsqueeze(1).broadcast_to([P, DST_TILES, GM]),
                                        is_tile[u][:, c, :].unsqueeze(2).broadcast_to([P, DST_TILES, GM]), ALU.mult).then_inc(S["spread_ready"], 1)

            decode(0, 0)
            mark(0, 0)
            with dve.Fori(0, STEPS // SKIP) as far:
                with dve.If(far * (2 * ECB * SKIP) < m):
                    with dve.Fori(0, SKIP) as near:
                        t = far * SKIP + near
                        with dve.If(t * (2 * ECB) < m):
                            for u in both:
                                now_, next_ = 2 * t + u, 2 * t + (u + 1)
                                decode(next_, 1 - u)
                                dve.wait_ge(S["hot_ready"], now_ + 1)
                                dve.wait_ge(gathered[u], t * (32 * ECB) + 32 * ECB)
                                nc.vector.tensor_tensor(pair[u][:, :, :], src_row[u][:, :, GF:GT1], dst_row[u][:, :, :], ALU.mult).then_inc(S["paired"], 1)
                                dve.wait_ge(S["paired"], now_ + 1)
                                dve.wait_ge(S["spread_ready"], now_ * ECB + 1)
                                nc.vector.tensor_tensor(msg[u][:, :, GF:GM], pair[u][:, :, 0:GH], pair[u][:, :, GH:2 * GH], ALU.max).then_inc(S["weighed"], 1)
                                dve.wait_ge(S["weighed"], now_ + 1)
                                nc.vector.tensor_tensor(msg[u][:, :, 0:GF].rearrange("p c (h e) -> p c h e", h=GH),
                                                        src_row[u][:, :, 0:GF].rearrange("p c (h e) -> p c h e", h=GH),
                                                        msg[u][:, :, GF:GM].unsqueeze(3).broadcast_to([P, ECB, GH, EXP1]), ALU.mult).then_inc(S["msg_ready"], 1)
                                dve.wait_ge(S["msg_ready"], now_ + 3)
                                for c in range(ECB):
                                    if c == ECB // 2:
                                        mark(next_, 1 - u)
                                    spread_out(now_, u, c)
            dve.wait_ge(S["summed"], 1)
            own_row = own[:, :, :].rearrange("p t m -> p (t m)")
            for i, o, w in parts:
                nc.vector.tensor_tensor(own_row[:, o:o + w], bank[i][:, 0:w], own_row[:, o:o + w], ALU.add)

        @block.tensor
        def _(pe):
            m = pe.value_load(count_in, min_val=0, max_val=EDGE_COLS)
            own_row = own[:, :, :].rearrange("p t m -> p (t m)")
            pe.wait_ge(S["cleared"], 1)
            for i, o, w in parts:
                nc.tensor.matmul(bank[i][:, 0:w], zero[:, :], own_row[:, o:o + w], start=True, stop=False, skip_group_check=True)
            with pe.Fori(0, STEPS // SKIP) as far:
                with pe.If(far * (2 * ECB * SKIP) < m):
                    with pe.Fori(0, SKIP) as near:
                        t = far * SKIP + near
                        with pe.If(t * (2 * ECB) < m):
                            for u in both:
                                for c in range(ECB):
                                    k = (2 * t + u) * ECB + c
                                    pe.wait_ge(S["spread_ready"], k + 2)
                                    pe.sem_inc(passed["pe"], 1)
                                    row = spread[c % RING][:, :, :].rearrange("p t m -> p (t m)")
                                    for i, o, w in parts:
                                        mm = nc.tensor.matmul(bank[i][:, 0:w], is_lane[u][:, c, :], row[:, o:o + w], start=False, stop=False,
                                                              skip_group_check=True)
                                    mm.then_inc(S["spread_used"], 1)
            for i, o, w in parts:
                mm = nc.tensor.matmul(bank[i][:, 0:w], zero[:, :], own_row[:, o:o + w], start=False, stop=True, skip_group_check=True)
            mm.then_inc(S["summed"], 1)


def scores_to_gate(nc, d, agg, gate):
    with ExitStack() as ctx:
        counter = counters(nc, ctx)
        sb = lambda n, s, dt=F32: ctx.enter_context(nc.sbuf_tensor("sg_" + n, s, dt))
        rows = {n: sb(n, [P, GF]) for n in ("b_gat", "ln_gamma", "ln_beta")}
        inv = sb("inv", [P, TILES, GH])
        f = sb("f", [P, TILES, GF])
        sq = sb("sq", [P, TILES, GF])
        total, mean, var, r, mh = (sb(n, [P, TILES]) for n in ("total", "mean", "var", "r", "mh"))
        score, low, chosen, ex = (sb(n, [P, TILES, EXP1]) for n in ("score", "low", "chosen", "ex"))
        beats = sb("beats", [P, TILES, EXP1, EXP1])
        top = sb("top", [P, TILES])
        loaded, step, var_ready, r_ready, low_ready, exp_done = (
            counter("sg_" + n) for n in ("loaded", "step", "var_ready", "r_ready", "low_ready", "exp_done"))
        block = ctx.enter_context(nc.Block())

        def wide(a, n):
            return a[:, :].unsqueeze(2).broadcast_to([P, TILES, n])

        def each(a):
            return a[:, :].unsqueeze(1).broadcast_to([P, TILES, GF])

        @block.sync
        def _(sp):
            for n, row in rows.items():
                sp.dma_start(row[:, :], row_on_all(d[n], GF)).then_inc(loaded, 16)

        @block.gpsimd
        def _(pool):
            pool.wait_ge(var_ready, 1)
            nc.gpsimd.tensor_tensor(r[:, :], var[:, :], mh[:, :], ALU.pow).then_inc(r_ready, 1)

        @block.scalar
        def _(act):
            act.wait_ge(low_ready, 1)
            nc.scalar.activation(ex[:, :, :], low[:, :, :], ACT.Exp).then_inc(exp_done, 1)

        @block.vector
        def _(dve):
            count = [0]

            def then(ins):
                count[0] += 1
                ins.then_inc(step, 1)
                dve.wait_ge(step, count[0])

            nc.vector.memset(mh[:, :], -0.5)
            nc.vector.memset(beats[:, :, :, :], 0.0)
            then(nc.vector.tensor_scalar(inv[:, :, :], agg[:, :, GF:GM], 1e-37, None, ALU.max))
            then(nc.vector.reciprocal(inv[:, :, :], inv[:, :, :]))
            dve.wait_ge(loaded, 48)
            then(nc.vector.tensor_tensor(f[:, :, :].rearrange("p t (h e) -> p t h e", h=GH), agg[:, :, 0:GF].rearrange("p t (h e) -> p t h e", h=GH),
                                         inv[:, :, :].unsqueeze(3).broadcast_to([P, TILES, GH, EXP1]), ALU.mult))
            then(nc.vector.tensor_tensor(f[:, :, :], f[:, :, :], each(rows["b_gat"]), ALU.add))
            then(nc.vector.tensor_reduce(total[:, :], f[:, :, :], AX.X, ALU.add))
            then(nc.vector.tensor_scalar(mean[:, :], total[:, :], 1.0 / GF, None, ALU.mult))
            then(nc.vector.tensor_tensor(f[:, :, :], f[:, :, :], wide(mean, GF), ALU.subtract))
            then(nc.vector.tensor_tensor(sq[:, :, :], f[:, :, :], f[:, :, :], ALU.mult))
            then(nc.vector.tensor_reduce(total[:, :], sq[:, :, :], AX.X, ALU.add))
            nc.vector.tensor_scalar(var[:, :], total[:, :], 1.0 / GF, LN_T_EPS, ALU.mult, ALU.add).then_inc(var_ready, 1)
            dve.wait_ge(r_ready, 1)
            then(nc.vector.tensor_tensor(f[:, :, :], f[:, :, :], wide(r, GF), ALU.mult))
            then(nc.vector.tensor_tensor(f[:, :, :], f[:, :, :], each(rows["ln_gamma"]), ALU.mult))
            then(nc.vector.tensor_tensor(f[:, :, :], f[:, :, :], each(rows["ln_beta"]), ALU.add))
            then(nc.vector.tensor_reduce(score[:, :, :], f[:, :, :].rearrange("p t (h e) -> p t e h", h=GH), AX.X, ALU.add))
            then(nc.vector.tensor_scalar(score[:, :, :], score[:, :, :], 1.0 / GH, None, ALU.mult))
            then(nc.vector.tensor_reduce(top[:, :], score[:, :, :], AX.X, ALU.max))
            nc.vector.tensor_tensor(low[:, :, :], score[:, :, :], wide(top, EXP1), ALU.subtract).then_inc(low_ready, 1)
            for e in range(EXP1):
                for lo, hi, op in ((0, e, ALU.is_gt), (e + 1, EXP1, ALU.is_ge)):
                    if hi > lo:
                        ins = nc.vector.tensor_tensor(beats[:, :, e, lo:hi], score[:, :, e:e + 1].broadcast_to([P, TILES, hi - lo]),
                                                      score[:, :, lo:hi], op)
            then(ins)
            then(nc.vector.tensor_reduce(chosen[:, :, :], beats[:, :, :, :], AX.X, ALU.add))
            then(nc.vector.tensor_scalar(chosen[:, :, :], chosen[:, :, :], 1.5, None, ALU.is_gt))
            dve.wait_ge(exp_done, 1)
            then(nc.vector.tensor_tensor(ex[:, :, :], ex[:, :, :], chosen[:, :, :], ALU.mult))
            then(nc.vector.tensor_reduce(total[:, :], ex[:, :, :], AX.X, ALU.add))
            then(nc.vector.reciprocal(total[:, :], total[:, :]))
            nc.vector.tensor_tensor(gate[:, :, :], ex[:, :, :], wide(total, EXP1), ALU.mult)


def graph_experts(nc, d, out, X, ident, mean, rstd, gate):
    with ExitStack() as ctx:
        sb = lambda n, s, dt=F32: ctx.enter_context(nc.sbuf_tensor("gs_" + n, s, dt))
        own = sb("own", [P, TILES, GM])
        longest = sb("longest", [P, 1], I32)
        src_rows = nc.dram_tensor("gs_src_rows", (NODES, GT1), F32, kind="Internal").ap()
        dst_rows = nc.dram_tensor("gs_dst_rows", (NODES, 2 * GH), F32, kind="Internal").ap()
        edge = sb("edge", [P, EDGE_COLS + ECB], I32)
        tables_and_edges(nc, d, X, ident, mean, rstd, own, src_rows, dst_rows, edge, longest)
        w1 = sb("w1", [P, EXP1, KC, F])
        w2 = sb("w2", [P, EXP1, FM, C])
        b1 = sb("b1", [P, EXP1, FM])
        b2 = sb("b2", [EXP1, C])
        sum_edges(nc, d, edge, longest, src_rows, dst_rows, own, w1, w2, b1, b2)
        scores_to_gate(nc, d, own, gate)
        experts_by_token(nc, out, X, ident, mean, rstd, gate, w1, w2, b1, b2)
def experts_by_token(nc, out, X, ident, mean, rstd, gate, w1, w2, b1, b2):
    with ExitStack() as ctx:
        counter = counters(nc, ctx)
        sb = lambda n, s, dt=F32: ctx.enter_context(nc.sbuf_tensor("m1_" + n, s, dt))
        sem = lambda n: counter("m1_" + n)
        tok = [sb(f"tok{u}", [P, TPH, C]) for u in range(2)]
        gate_in = [sb(f"gate_in{u}", [P, TPH, EXP1]) for u in range(2)]
        gateT = sb("gateT", [EXP1, HALF])
        tokT = sb("tokT", [P, KC, HALF])
        hid = [sb(f"hid{i}", [P, FM, HALF]) for i in range(2)]
        z = sb("z", [P, TPH, C])
        bank_t = [ctx.enter_context(nc.psum_tensor(f"m1_bt{i}", [P, 512], F32)) for i in range(2)]
        bank_h = [ctx.enter_context(nc.psum_tensor(f"m1_bh{i}", [P, 512], F32)) for i in range(2)]
        bank_y = [ctx.enter_context(nc.psum_tensor(f"m1_by{i}", [P, C], F32)) for i in range(4)]
        names = """tok_ready turned tokT_ready gate_turned gateT_ready h_done h_free y_done y_free z_ready x_ready hid_free stored passed_sp""".split()
        S = {n: sem(n) for n in names}
        passed = sem("passed")
        block = ctx.enter_context(nc.Block())
        BLOCKS = TILES // TPH
        HPB = EXP1 * FM
        YPB = (EXP1 + 1) * TPH

        @block.sync
        def _(sp):
            out_tiles = out.rearrange("(i p) c -> p i c", p=P)
            with sp.Fori(0, BLOCKS) as b:
                sp.wait_ge(S["x_ready"], b + 2)
                sp.sem_inc(S["passed_sp"], 1)
                sp.dma_start(out_tiles[:, bass.ds(b * TPH, TPH), :], X[:, bass.ds(b * TPH, TPH), :]).then_inc(S["stored"], 16)
            sp.wait_ge(S["stored"], 16 * BLOCKS)

        @block.tensor
        def _(pe):
            def hidden(b, e):
                for m in range(FM):
                    g = e * FM + m
                    pe.wait_ge(S["h_free"], HPB * b + g + 1)
                    for k in range(KC):
                        mm = nc.tensor.matmul(bank_h[g % 2][:, :], w1[:, e, k, m * P:(m + 1) * P], tokT[:, k, :], start=(k == 0), stop=(k == KC - 1))
                    mm.then_inc(S["h_done"], 1)

            def output(b, e):
                pe.wait_ge(S["h_free"], HPB * b + (e + 1) * FM + 2)
                for i in range(TPH):
                    y = (e + 1) * TPH + i
                    pe.wait_ge(S["y_free"], YPB * b + y + 1)
                    for m in range(FM):
                        mm = nc.tensor.matmul(bank_y[y % 4][:, :], hid[e % 2][:, m, i * P:(i + 1) * P], w2[:, e, m, :], start=(m == 0), stop=(m == FM - 1))
                    mm.then_inc(S["y_done"], 1)

            def turn(b, u):
                pe.wait_ge(S["tok_ready"], b + 1)
                for k in range(KC):
                    for i in range(TPH):
                        mm = nc.tensor.transpose(bank_t[k][:, i * P:(i + 1) * P], tok[u][:, i, k * P:(k + 1) * P], ident[:, :])
                mm.then_inc(S["turned"], 1)

            def turn_gates(b, u):
                pe.wait_ge(S["tokT_ready"], b + 1)
                pe.sem_inc(passed, 1)
                for i in range(TPH):
                    mm = nc.tensor.transpose(bank_t[0][0:EXP1, i * P:(i + 1) * P], gate_in[u][:, i, :], ident[:, :])
                mm.then_inc(S["gate_turned"], 1)

            turn(0, 0)
            turn_gates(0, 0)
            with pe.Fori(0, BLOCKS // 2) as pair:
                for u in range(2):
                    b = 2 * pair + u
                    pe.wait_ge(S["tokT_ready"], b + 1)
                    hidden(b, 0)
                    pe.wait_ge(S["gateT_ready"], b + 1)
                    for i in range(TPH):
                        pe.wait_ge(S["y_free"], YPB * b + i + 1)
                        pe.sem_inc(passed, 1)
                        nc.tensor.matmul(bank_y[i][:, :], gateT[:, i * P:(i + 1) * P], b2[:, :], start=True, stop=True).then_inc(S["y_done"], 1)
                    for e in range(1, EXP1):
                        hidden(b, e)
                        if e == EXP1 - 1:
                            turn(b + 1, 1 - u)
                        output(b, e - 1)
                    turn_gates(b + 1, 1 - u)
                    output(b, EXP1 - 1)

        @block.scalar
        def _(act):
            def copy_turned(b):
                act.wait_ge(S["turned"], b + 1)
                for k in range(KC):
                    ins = nc.scalar.copy(tokT[:, k, :], bank_t[k][:, :])
                ins.then_inc(S["tokT_ready"], 1)
                act.wait_ge(S["gate_turned"], b + 1)
                nc.scalar.copy(gateT[:, :], bank_t[0][0:EXP1, :]).then_inc(S["gateT_ready"], 1)

            copy_turned(0)
            with act.Fori(0, BLOCKS) as b:
                for e in range(EXP1):
                    act.wait_ge(S["y_done"], YPB * b + TPH + (e * TPH if e > 1 else 0))
                    for m in range(FM):
                        g = e * FM + m
                        act.wait_ge(S["h_done"], HPB * b + g + 1)
                        nc.scalar.activation(hid[e % 2][:, m, :], bank_h[g % 2][:, :], ACT.Gelu, bias=b1[:, e, m:m + 1]).then_inc(S["h_free"], 1)
                copy_turned(b + 1)

        @block.vector
        def _(dve):
            for n, k in (("h_free", 2), ("y_free", 4), ("x_ready", 1), ("y_done", TPH)):
                for _ in range(k):
                    dve.sem_inc(S[n], 1)
            def normalise(b, u):
                nc.vector.tensor_copy(gate_in[u][:, :, :], gate[:, bass.ds(b * TPH, TPH), :])
                for i in range(TPH):
                    t = b * TPH + i
                    ins = nc.vector.tensor_scalar(tok[u][:, i, :], X[:, bass.ds(t, 1), :].rearrange("p a c -> p (a c)"), mean[:, bass.ds(t, 1)],
                                                  rstd[:, bass.ds(t, 1)], ALU.subtract, ALU.mult)
                ins.then_inc(S["tok_ready"], 1)

            normalise(0, 0)
            with dve.Fori(0, BLOCKS // 2) as pair:
                for u in range(2):
                    b = 2 * pair + u
                    dve.wait_ge(S["x_ready"], b + 1)
                    normalise((b + 1) & (BLOCKS - 1), 1 - u)
                    for e in range(EXP1 + 1):
                        for i in range(TPH):
                            y = e * TPH + i
                            dve.wait_ge(S["y_done"], YPB * b + TPH + y + 1)
                            if e == 0:
                                nc.vector.tensor_copy(z[:, i, :], bank_y[y % 4][:, :]).then_inc(S["y_free"], 1)
                            else:
                                dve.wait_ge(S["y_free"], YPB * b + 4 + y - TPH + 1)
                                nc.vector.scalar_tensor_tensor(out=z[:, i, :], in0=bank_y[y % 4][:, :], scalar=gate_in[u][:, i, e - 1:e], in1=z[:, i, :],
                                                               op0=ALU.mult, op1=ALU.add).then_inc(S["y_free"], 1)
                    dve.wait_ge(S["y_free"], YPB * b + 4 + YPB)
                    xt = X[:, bass.ds(b * TPH, TPH), :]
                    nc.vector.tensor_tensor(xt, xt, z[:, :, :], ALU.add).then_inc(S["x_ready"], 1)


def metaformer(nc, d, out):
    with ExitStack() as ctx:
        X = ctx.enter_context(nc.sbuf_tensor("X", [P, TILES, C], F32))
        ident = ctx.enter_context(nc.sbuf_tensor("ident", [P, P], F32))
        mean = ctx.enter_context(nc.sbuf_tensor("mean", [P, TILES], F32))
        rstd = ctx.enter_context(nc.sbuf_tensor("rstd", [P, TILES], F32))
        mean2 = ctx.enter_context(nc.sbuf_tensor("mean2", [P, TILES], F32))
        rstd2 = ctx.enter_context(nc.sbuf_tensor("rstd2", [P, TILES], F32))
        gate = ctx.enter_context(nc.sbuf_tensor("gate", [P, TILES, EXP1], F32))
        picked = ctx.enter_context(nc.sbuf_tensor("picked", [1, BATCH * TOPK], U32))
        weight = ctx.enter_context(nc.sbuf_tensor("weight", [P, BATCH * TOPK], F32))
        mamba_layers(nc, d, X, ident, mean, rstd)
        route_images(nc, d, X, ident, mean, rstd, picked, weight)
        experts_by_image(nc, d, X, ident, mean, rstd, picked, weight, mean2, rstd2)
        row_attention(nc, d, X, ident, mean2, rstd2)
        graph_experts(nc, d, out, X, ident, mean, rstd, gate)


def kernel(**inputs):
    import numpy as np
    import concourse.bacc as bacc
    from concourse.bass_utils import run_bass_kernel_spmd

    g = {k: np.asarray(v) for k, v in inputs.items()}
    a = {
        "x": g["x"].reshape(TILES * P, C),
        "in_projT": g["L0_conv_in_proj_w"].transpose(0, 2, 1),
        "out_projT": g["L0_conv_out_proj_w"].transpose(0, 2, 1),
        "norm_w": g["L0_conv_norm_w"].reshape(LAYERS, XM, P).transpose(2, 0, 1),
        "conv_w": g["L0_conv_conv_w"][:, :DIN].reshape(LAYERS, XM, P, TAPS).transpose(2, 0, 1, 3),
        "conv_b": g["L0_conv_conv_b"][:, :DIN].reshape(LAYERS, XM, P).transpose(2, 0, 1),
        "conv_w_bc": g["L0_conv_conv_w"][:, DIN:].reshape(LAYERS, 2, NST, TAPS).transpose(2, 0, 1, 3),
        "conv_b_bc": g["L0_conv_conv_b"][:, DIN:].reshape(LAYERS, 2, NST).transpose(2, 0, 1),
        "dt_bias": g["L0_conv_dt_bias"].T,
        "A_log": g["L0_conv_A_log"].T,
        "D": g["L0_conv_D"],
        "ident": np.eye(P, dtype=np.float32),
        "head_row": np.repeat(np.eye(HEADS, dtype=np.float32), P, axis=1),
        "last_row": np.repeat(np.eye(P, dtype=np.float32)[:, P - 1:], NST, axis=1),
    }
    a |= {
        "image_row": np.tile(np.eye(BATCH, dtype=np.float32).reshape(1, -1) / np.float32(SEQ), (P, 1)),
        "Wr": g["L0_ffn_Wr"], "br": g["L0_ffn_br"], "W1_0": g["L0_ffn_W1"], "W2_0": g["L0_ffn_W2"],
        "b1_0": g["L0_ffn_b1"].reshape(EXP0, FM, P).transpose(0, 2, 1), "b2_0": g["L0_ffn_b2"],
        "gamma0": g["L0_ffn_gamma"], "beta0": g["L0_ffn_beta"],
    }
    a |= {"W1_1": g["L1_ffn_W1"], "W2_1": g["L1_ffn_W2"], "b1_1": g["L1_ffn_b1"].reshape(EXP1, FM, P).transpose(2, 0, 1), "b2_1": g["L1_ffn_b2"]}
    a |= {
        "w_gat": g["L1_ffn_W_gat"], "att_src": g["L1_ffn_att_src"].reshape(-1), "att_dst": g["L1_ffn_att_dst"].reshape(-1),
        "b_gat": g["L1_ffn_b_gat"], "ln_gamma": g["L1_ffn_ln_gamma"], "ln_beta": g["L1_ffn_ln_beta"],
        "edges": g["L1_ffn_edge_index"].reshape(2, P, EDGE_COLS), "place": np.arange(1, EDGE_COLS + 1, dtype=np.int32),
        "lane": np.arange(P, dtype=np.float32),
    }
    rows = np.arange(2 * RH) % RH // AH
    a |= {
        "w_qk": np.concatenate([np.tile(g["L1_conv_Wq"].T, (1, RPT)), np.tile(g["L1_conv_Wk"].T, (1, RPT))], axis=1),
        "b_qk": np.concatenate([np.tile(g["L1_conv_bq"], RPT), np.tile(g["L1_conv_bk"], RPT)]).reshape(-1, 1),
        "qk_scale": np.concatenate([np.full((RH, 1), ROW, np.float32), np.ones((RH, 1), np.float32)]),
        "row_mask": (rows[:, None] == np.arange(P)[None, :] // ROW).astype(np.float32),
        "head_mask": (np.arange(C).reshape(KC, P).T[:, :, None] // (C // AH) == np.arange(GT * RH)[None, None, :] % AH).astype(np.float32),
        "w_v": g["L1_conv_Wv"].T, "b_v": g["L1_conv_bv"].reshape(KC, P).T, "w_o": g["L1_conv_Wo"].T, "b_o": g["L1_conv_bo"],
    }
    a = {k: np.ascontiguousarray(v) for k, v in a.items()}
    nc = bacc.Bacc("TRN2", target_bir_lowering=False, num_devices=1)
    d = {k: nc.dram_tensor("in_" + k, v.shape, mybir.dt.from_np(v.dtype), kind="ExternalInput").ap() for k, v in a.items()}
    out = nc.dram_tensor("out", (TILES * P, C), F32, kind="ExternalOutput").ap()
    metaformer(nc, d, out)
    r = run_bass_kernel_spmd(nc, [{"in_" + k: v for k, v in a.items()}], core_ids=[0])
    return r.results[0]["out"].reshape(BATCH, 32, 32, C)
```
